# Optimizing a Trainium2 kernel written in Bass

```python
import numpy as np
import jax
import jax.numpy as jnp

def _softmax(x, axis=-1):
    return jax.nn.softmax(x, axis=axis)

def _gelu(x):
    return jax.nn.gelu(x, approximate=True)

def _silu(x):
    return jax.nn.silu(x)

def _sigmoid(x):
    return jax.nn.sigmoid(x)

def _layernorm(x, axis=-1, eps=1e-05):
    m = jnp.mean(x, axis=axis, keepdims=True)
    v = jnp.var(x, axis=axis, keepdims=True)
    return (x - m) / jnp.sqrt(v + eps)

def _scatter_add(tgt, idx, src, axis=0):
    return tgt.at[idx].add(src)

def _segment_sum(src, seg, n):
    return jax.ops.segment_sum(src, seg, n)
kernel_name = 'mk_decoder_postln_d4_seqx_r4_a2e18b'

def setup_inputs(seed: int=0):
    np.random.seed(seed)
    _w = jnp.asarray

    def _rec_inputs():
        import jax
        import jax.numpy as jnp
        _rk = jax.random.key(seed)
        x = -0.0003929 + 0.9999 * jax.random.normal(jax.random.fold_in(_rk, 1), (16, 128, 256), jnp.float32)
        _lenS = 128 - jax.random.randint(jax.random.fold_in(_rk, 7), (16,), 0, max(1, 128 // 4) + 1, jnp.int32)
        _lenS2 = 128 - jax.random.randint(jax.random.fold_in(_rk, 8), (16,), 0, max(1, 128 // 4) + 1, jnp.int32)
        _ctx_2048P = jax.random.normal(jax.random.fold_in(_rk, 11), (16, 16, 512), jnp.float32)
        _ctx_2048c = jax.random.dirichlet(jax.random.fold_in(_rk, 511), 0.3 * jnp.ones((16,), jnp.float32), (16, 128))
        _ctx_2048t = jnp.einsum('bsk,bkd->bsd', _ctx_2048c, _ctx_2048P)
        _ctx_2048t = _ctx_2048t * jax.lax.rsqrt(jnp.mean(jnp.square(_ctx_2048t)) + 1e-12) * 0.953939
        ctx_2048 = 4.13588e-05 + 0.999923 * (_ctx_2048t + 0.3 * jax.random.normal(jax.random.fold_in(_rk, 611), (16, 128, 512), jnp.float32))
        _validS = jnp.arange(128)[None, :] < _lenS[:, None]
        _validS2 = jnp.arange(128)[None, :] < _lenS2[:, None]
        _causal = jnp.tril(jnp.ones((128, 128), dtype=bool))
        mask_BxS2_if0 = jnp.where(jnp.ones((16, 128), dtype=bool), 4, 0).astype(jnp.int32)
        mask_BxS2_fk1 = jnp.where(jnp.broadcast_to(_validS2[:, :], (16, 128)), 1.0, 0.0).astype(jnp.float32)
        return (x, ctx_2048, mask_BxS2_if0, mask_BxS2_fk1)
    x, ctx_2048, mask_BxS2_if0, mask_BxS2_fk1 = _rec_inputs()

    def _L0_attn_setup():
        import jax, jax.numpy as jnp
        import numpy as np
        from jax import lax
        D_MODEL = 256
        EXPAND = 2
        D_INNER = EXPAND * D_MODEL
        D_STATE = 16
        D_CONV = 4
        DT_RANK = D_MODEL // 16
        B_SZ = 4
        SEQ = 512

        def _mamba_fwd(x, W_in, conv_w, conv_b, W_x, W_dt, b_dt, A_log, D, W_out):
            B, L, _ = x.shape
            xz = jnp.einsum('bld,ed->ble', x, W_in)
            u, z = jnp.split(xz, 2, axis=-1)
            u_nc = u.transpose(0, 2, 1)
            u_c = lax.conv_general_dilated(u_nc, conv_w[:, None, :], window_strides=(1,), padding=[(D_CONV - 1, 0)], feature_group_count=D_INNER, dimension_numbers=('NCH', 'OIH', 'NCH'))
            u_c = (u_c + conv_b[None, :, None]).transpose(0, 2, 1)
            u_c = jax.nn.silu(u_c)
            x_dbl = jnp.einsum('bld,ed->ble', u_c, W_x)
            dt_r, Bm, Cm = jnp.split(x_dbl, [DT_RANK, DT_RANK + D_STATE], axis=-1)
            dt = jax.nn.softplus(jnp.einsum('blr,dr->bld', dt_r, W_dt) + b_dt)
            A = -jnp.exp(A_log)

            def step(h, inp):
                dt_t, u_t, B_t, C_t = inp
                dA = jnp.exp(dt_t[..., None] * A)
                h = dA * h + (dt_t * u_t)[..., None] * B_t[:, None, :]
                y_t = jnp.einsum('bds,bs->bd', h, C_t)
                return (h, y_t)
            xs = (dt.transpose(1, 0, 2), u_c.transpose(1, 0, 2), Bm.transpose(1, 0, 2), Cm.transpose(1, 0, 2))
            h0 = jnp.zeros((B, D_INNER, D_STATE), dtype=x.dtype)
            _, ys = lax.scan(step, h0, xs)
            y = ys.transpose(1, 0, 2)
            y = y + u_c * D
            y = y * jax.nn.silu(z)
            out = jnp.einsum('bld,ed->ble', y, W_out)
            return out

        def _reference_tuple_inner(x, W_in, conv_w, conv_b, W_x, W_dt, b_dt, A_log, D, W_out):
            out = _mamba_fwd(x, W_in, conv_w, conv_b, W_x, W_dt, b_dt, A_log, D, W_out)
            return (out, None)
        key = jax.random.key(seed)
        ks = jax.random.split(key, 10)
        s = lambda k, shape, scale: jax.random.normal(k, shape, dtype=jnp.float32) * scale
        inp = {'x': s(ks[0], (B_SZ, SEQ, D_MODEL), 1.0), 'W_in': s(ks[1], (2 * D_INNER, D_MODEL), D_MODEL ** (-0.5)), 'conv_w': s(ks[2], (D_INNER, D_CONV), D_CONV ** (-0.5)), 'conv_b': s(ks[3], (D_INNER,), 0.02), 'W_x': s(ks[4], (DT_RANK + 2 * D_STATE, D_INNER), D_INNER ** (-0.5)), 'W_dt': s(ks[5], (D_INNER, DT_RANK), DT_RANK ** (-0.5)), 'b_dt': s(ks[6], (D_INNER,), 0.5), 'A_log': jnp.log(jnp.broadcast_to(jnp.arange(1, D_STATE + 1, dtype=jnp.float32), (D_INNER, D_STATE))), 'D': jnp.ones((D_INNER,), dtype=jnp.float32), 'W_out': s(ks[7], (D_MODEL, D_INNER), D_INNER ** (-0.5))}
        return inp
    _L0_attn_all = _L0_attn_setup()
    _L0_attn_in = {k: v for k, v in _L0_attn_all.items() if k in ('W_in', 'conv_w', 'conv_b', 'W_x', 'W_dt', 'b_dt', 'A_log', 'D', 'W_out')}
    del _L0_attn_all

    def _L0_xattn_setup():
        import jax, jax.numpy as jnp
        import numpy as np
        B, L, P = (4, 1024, 256)
        D_MODEL = 256
        D_GLOBAL = 512
        HEADDIM = 32
        EPSILON = 0.001
        RMS_EPS = 1e-05

        def rmsnorm(x, g, eps=RMS_EPS):
            var = jnp.mean(jnp.square(x), axis=-1, keepdims=True)
            return x * jax.lax.rsqrt(var + eps) * g

        def _hnet_depool(h, h_patch_full, patch_lens):
            h_patch = h_patch_full[..., :D_MODEL]
            bsz, plen = (h_patch.shape[0], h_patch.shape[1])
            seqlen = h.shape[1]
            logp = jnp.full((bsz, plen), -EPSILON, dtype=jnp.float32)
            bidx = jnp.cumsum(patch_lens, axis=1) - 1
            boundary_mask = jnp.zeros((bsz, seqlen), dtype=jnp.int32)
            boundary_mask = boundary_mask.at[jnp.arange(bsz)[:, None], bidx].set(1)
            dt = (-jnp.log(-jnp.expm1(logp))).astype(h_patch.dtype)
            x = h_patch / dt[..., None]
            n_heads = D_MODEL // HEADDIM
            A = -jnp.ones((n_heads,), dtype=jnp.float32)
            bcoef = jnp.exp(logp).astype(h_patch.dtype)
            x4 = x.reshape(bsz, plen, n_heads, HEADDIM)
            a = jnp.exp(dt[:, :, None] * A[None, None, :])
            u = (dt * bcoef)[:, :, None, None] * x4
            a_b = jnp.broadcast_to(a[..., None], u.shape)

            def comb(lft, rgt):
                aL, uL = lft
                aR, uR = rgt
                return (aL * aR, uL * aR + uR)
            _, s = jax.lax.associative_scan(comb, (a_b, u), axis=1)
            depool = s.reshape(bsz, plen, D_MODEL)
            plug = jnp.clip(jnp.cumsum(boundary_mask, axis=1) - 1, 0, plen - 1)
            depool_out = depool[jnp.arange(bsz)[:, None], plug]
            return depool_out + h
        key = jax.random.key(seed)
        k1, k2, k3, k4 = jax.random.split(key, 4)
        embeds = jax.random.normal(k1, (B, L, D_MODEL), dtype=jnp.float32)
        patch_embeds = jax.random.normal(k2, (B, P, D_GLOBAL), dtype=jnp.float32)
        patch_lens = jnp.full((B, P), L // P, dtype=jnp.int64)
        W_in = jax.random.normal(k3, (D_MODEL, D_MODEL), dtype=jnp.float32) * 0.02
        b_in = jnp.zeros((D_MODEL,), dtype=jnp.float32)
        g_res = jnp.ones((D_MODEL,), dtype=jnp.float32)
        g_init = jnp.ones((D_GLOBAL,), dtype=jnp.float32)
        return {'embeds': embeds, 'patch_embeds': patch_embeds, 'patch_lens': patch_lens, 'W_in': W_in, 'b_in': b_in, 'g_res': g_res, 'g_init': g_init}
    _L0_xattn_all = _L0_xattn_setup()
    _L0_xattn_in = {k: v for k, v in _L0_xattn_all.items() if k in ('W_in', 'b_in', 'g_res', 'g_init')}
    del _L0_xattn_all

    def _L0_ffn_setup():
        import jax, jax.numpy as jnp
        import numpy as np
        LN_EPS = 0.001
        EPS = 1e-05
        QB = 128.0

        def ste_round(x):
            return x + jax.lax.stop_gradient(jnp.round(x) - x)
        key = jax.random.key(seed)
        k1, k2 = jax.random.split(key)
        x = jax.random.normal(k1, (4, 2048, 256), dtype=jnp.float32)
        weight = jax.random.normal(k2, (256, 256), dtype=jnp.float32) * 0.02
        ln_gamma = jnp.ones((256,), dtype=jnp.float32)
        ln_beta = jnp.zeros((256,), dtype=jnp.float32)
        return {'x': x, 'weight': weight, 'ln_gamma': ln_gamma, 'ln_beta': ln_beta}
    _L0_ffn_all = _L0_ffn_setup()
    _L0_ffn_in = {k: v for k, v in _L0_ffn_all.items() if k in ('weight', 'ln_gamma', 'ln_beta')}
    del _L0_ffn_all

    def _L1_attn_setup():
        import jax, jax.numpy as jnp
        import numpy as np
        B, N, QD = (4, 1024, 256)
        HEADS, DIM_HEAD = (8, 64)
        HID = HEADS * DIM_HEAD
        SCALE = DIM_HEAD ** (-0.5)
        key = jax.random.key(seed)
        ks = jax.random.split(key, 6)
        s_in = 1.0 / np.sqrt(QD)
        s_h = 1.0 / np.sqrt(HID)
        return {'x': jax.random.normal(ks[0], (B, N, QD), dtype=jnp.float32), 'Wq': jax.random.uniform(ks[1], (QD, HID), jnp.float32, -s_in, s_in), 'Wk': jax.random.uniform(ks[2], (QD, HID), jnp.float32, -s_in, s_in), 'Wv': jax.random.uniform(ks[3], (QD, HID), jnp.float32, -s_in, s_in), 'Wo': jax.random.uniform(ks[4], (HID, QD), jnp.float32, -s_h, s_h), 'bo': jax.random.uniform(ks[5], (QD,), jnp.float32, -s_h, s_h)}
    _L1_attn_all = _L1_attn_setup()
    _L1_attn_in = {k: v for k, v in _L1_attn_all.items() if k in ('Wq', 'Wk', 'Wv', 'Wo', 'bo')}
    del _L1_attn_all

    def _L1_xattn_setup():
        import jax, jax.numpy as jnp
        import numpy as np
        NUM_HEADS = 16
        key = jax.random.key(seed)
        ks = jax.random.split(key, 5)
        dim = 256
        B, N, N_c = (4, 256, 64)
        x = jax.random.normal(ks[0], (B, N, dim), dtype=jnp.float32)
        context = jax.random.normal(ks[1], (B, N_c, 2 * dim), dtype=jnp.float32)
        w_qkv = jax.random.normal(ks[2], (3 * dim, dim), dtype=jnp.float32) * 0.02
        w_proj = jax.random.normal(ks[3], (dim, dim), dtype=jnp.float32) * 0.02
        b_proj = jax.random.normal(ks[4], (dim,), dtype=jnp.float32) * 0.02
        return {'x': x, 'context': context, 'w_qkv': w_qkv, 'w_proj': w_proj, 'b_proj': b_proj}
    _L1_xattn_all = _L1_xattn_setup()
    _L1_xattn_in = {k: v for k, v in _L1_xattn_all.items() if k in ('w_qkv', 'w_proj', 'b_proj')}
    del _L1_xattn_all

    def _L1_ffn_setup():
        import jax, jax.numpy as jnp
        import numpy as np
        EMB = 256
        HID = 512
        HEADS = 16
        HEAD_DIM = EMB // HEADS
        EXPERTS = 8
        TOPK = 2
        EPS = 1e-05

        def layernorm(x, scale, shift):
            mean = jnp.mean(x, axis=-1, keepdims=True)
            var = jnp.mean((x - mean) ** 2, axis=-1, keepdims=True)
            return scale * (x - mean) / jnp.sqrt(var + EPS) + shift

        def attention(x, wq, wk, wv, wo, bo):
            b, t, _ = x.shape
            q = (x @ wq).reshape(b, t, HEADS, HEAD_DIM)
            k = (x @ wk).reshape(b, t, HEADS, HEAD_DIM)
            v = (x @ wv).reshape(b, t, HEADS, HEAD_DIM)
            scores = jnp.einsum('bqhd,bkhd->bhqk', q, k)
            mask = jnp.arange(t)[:, None] < jnp.arange(t)[None, :]
            scores = jnp.where(mask, -jnp.inf, scores)
            attn = jax.nn.softmax(scores / np.sqrt(HEAD_DIM), axis=-1)
            ctx = jnp.einsum('bhqk,bkhd->bqhd', attn, v).reshape(b, t, EMB)
            return ctx @ wo + bo

        def moe_ff(x, gate_w, w1, w2, w3):
            b, t, d = x.shape
            xf = x.reshape(b * t, d)
            scores = xf @ gate_w
            topk_scores, topk_idx = jax.lax.top_k(scores, TOPK)
            topk_probs = jax.nn.softmax(topk_scores, axis=-1)
            weight = jnp.sum(jax.nn.one_hot(topk_idx, EXPERTS, dtype=xf.dtype) * topk_probs[..., None], axis=1)
            h = jax.nn.silu(jnp.einsum('td,edh->eth', xf, w1)) * jnp.einsum('td,edh->eth', xf, w2)
            out_e = jnp.einsum('eth,ehd->etd', h, w3)
            out = jnp.einsum('etd,te->td', out_e, weight)
            return out.reshape(b, t, d)
        key = jax.random.key(seed)
        ks = jax.random.split(key, 12)
        s = lambda k, shape, fan: jax.random.normal(k, shape, jnp.float32) / np.sqrt(fan)
        return {'x': jax.random.normal(ks[0], (2, 512, EMB), jnp.float32), 'ln1_scale': jnp.ones((EMB,), jnp.float32), 'ln1_shift': jnp.zeros((EMB,), jnp.float32), 'wq': s(ks[1], (EMB, EMB), EMB), 'wk': s(ks[2], (EMB, EMB), EMB), 'wv': s(ks[3], (EMB, EMB), EMB), 'wo': s(ks[4], (EMB, EMB), EMB), 'bo': jnp.zeros((EMB,), jnp.float32), 'ln2_scale': jnp.ones((EMB,), jnp.float32), 'ln2_shift': jnp.zeros((EMB,), jnp.float32), 'gate_w': s(ks[5], (EMB, EXPERTS), EMB), 'w1': s(ks[6], (EXPERTS, EMB, HID), EMB), 'w2': s(ks[7], (EXPERTS, EMB, HID), EMB), 'w3': s(ks[8], (EXPERTS, HID, EMB), HID)}
    _L1_ffn_all = _L1_ffn_setup()
    _L1_ffn_in = {k: v for k, v in _L1_ffn_all.items() if k in ('ln1_scale', 'ln1_shift', 'wq', 'wk', 'wv', 'wo', 'bo', 'ln2_scale', 'ln2_shift', 'gate_w', 'w1', 'w2', 'w3')}
    del _L1_ffn_all

    def _L2_attn_setup():
        import jax, jax.numpy as jnp
        import numpy as np
        import math
        EMBED_DIM = 256
        NUM_HEADS = 16
        HEAD_DIM = EMBED_DIM // NUM_HEADS
        key = jax.random.key(seed)
        ks = jax.random.split(key, 5)
        B, S, D = (2, 512, EMBED_DIM)
        s = 1.0 / math.sqrt(D)
        x = jax.random.normal(ks[0], (B, S, D), dtype=jnp.float32)
        W_qkv = jax.random.normal(ks[1], (3 * D, D), dtype=jnp.float32) * s
        b_qkv = jax.random.normal(ks[2], (3 * D,), dtype=jnp.float32) * 0.01
        W_out = jax.random.normal(ks[3], (D, D), dtype=jnp.float32) * s
        b_out = jax.random.normal(ks[4], (D,), dtype=jnp.float32) * 0.01
        return {'x': x, 'W_qkv': W_qkv, 'b_qkv': b_qkv, 'W_out': W_out, 'b_out': b_out}
    _L2_attn_all = _L2_attn_setup()
    _L2_attn_in = {k: v for k, v in _L2_attn_all.items() if k in ('W_qkv', 'b_qkv', 'W_out', 'b_out')}
    del _L2_attn_all

    def _L2_xattn_setup():
        import jax, jax.numpy as jnp
        import numpy as np
        B, N, DIM = (8, 1024, 256)
        M, CTX = (64, 512)
        HEADS, DH = (16, 64)
        INNER = HEADS * DH
        EPS = 1e-06

        def _split_heads(t):
            b, n, _ = t.shape
            return t.reshape(b, n, HEADS, DH).transpose(0, 2, 1, 3)
        key = jax.random.key(seed)
        ks = jax.random.split(key, 6)
        x = jax.random.normal(ks[0], (B, N, DIM), dtype=jnp.float32)
        context = jax.random.normal(ks[1], (B, M, CTX), dtype=jnp.float32)
        Wq = jax.random.normal(ks[2], (DIM, INNER), dtype=jnp.float32) / np.sqrt(DIM)
        Wkv = jax.random.normal(ks[3], (CTX, 2 * INNER), dtype=jnp.float32) / np.sqrt(CTX)
        null_kv = jax.random.normal(ks[4], (2, DH), dtype=jnp.float32) / np.sqrt(2.0)
        Wout = jax.random.normal(ks[5], (INNER, DIM), dtype=jnp.float32) / np.sqrt(INNER)
        ln_scale = jnp.ones((DIM,), dtype=jnp.float32)
        ln_bias = jnp.zeros((DIM,), dtype=jnp.float32)
        return {'x': x, 'context': context, 'Wq': Wq, 'Wkv': Wkv, 'null_kv': null_kv, 'Wout': Wout, 'ln_scale': ln_scale, 'ln_bias': ln_bias}
    _L2_xattn_all = _L2_xattn_setup()
    _L2_xattn_in = {k: v for k, v in _L2_xattn_all.items() if k in ('Wq', 'Wkv', 'null_kv', 'Wout', 'ln_scale', 'ln_bias')}
    del _L2_xattn_all

    def _L2_ffn_setup():
        import jax, jax.numpy as jnp
        import numpy as np
        B, S, H, E, DFF = (4, 1024, 256, 8, 1024)
        key = jax.random.key(seed)
        k0, k1, k2, k3 = jax.random.split(key, 4)
        hidden_states = jax.random.normal(k0, (B, S, H), dtype=jnp.float32)
        gate_w = jax.random.normal(k1, (E, H), dtype=jnp.float32) * 0.02
        w1 = jax.random.normal(k2, (E, H, DFF), dtype=jnp.float32) * 0.02
        b1 = jnp.zeros((E, DFF), dtype=jnp.float32)
        w2 = jax.random.normal(k3, (E, DFF, H), dtype=jnp.float32) * 0.02
        b2 = jnp.zeros((E, H), dtype=jnp.float32)
        return {'hidden_states': hidden_states, 'gate_w': gate_w, 'w1': w1, 'b1': b1, 'w2': w2, 'b2': b2}
    _L2_ffn_all = _L2_ffn_setup()
    _L2_ffn_in = {k: v for k, v in _L2_ffn_all.items() if k in ('gate_w', 'w1', 'b1', 'w2', 'b2')}
    del _L2_ffn_all

    def _L3_attn_setup():
        import jax, jax.numpy as jnp
        import numpy as np
        B, S, D, H = (2, 512, 256, 16)
        DK = D // H
        key = jax.random.key(seed)
        ks = jax.random.split(key, 9)
        s = 0.02
        return {'embeddings': jax.random.normal(ks[0], (B, S, D), jnp.float32), 'Wq': jax.random.normal(ks[1], (H, D, DK), jnp.float32) * s, 'bq': jax.random.normal(ks[2], (H, DK), jnp.float32) * s, 'Wk': jax.random.normal(ks[3], (H, D, DK), jnp.float32) * s, 'bk': jax.random.normal(ks[4], (H, DK), jnp.float32) * s, 'Wv': jax.random.normal(ks[5], (H, D, DK), jnp.float32) * s, 'bv': jax.random.normal(ks[6], (H, DK), jnp.float32) * s, 'Wo': jax.random.normal(ks[7], (D, D), jnp.float32) * s, 'bo': jax.random.normal(ks[8], (D,), jnp.float32) * s}
    _L3_attn_all = _L3_attn_setup()
    _L3_attn_in = {k: v for k, v in _L3_attn_all.items() if k in ('Wq', 'bq', 'Wk', 'bk', 'Wv', 'bv', 'Wo', 'bo')}
    del _L3_attn_all

    def _L3_xattn_setup():
        import jax, jax.numpy as jnp
        import numpy as np
        B, S, T = (32, 128, 128)
        SRC_SIZE, TGT_SIZE, OUT_SIZE, NUM_HEAD = (512, 256, 256, 8)
        HEAD_DIM = OUT_SIZE // NUM_HEAD
        key = jax.random.key(seed)
        ks = jax.random.split(key, 12)
        src = jax.random.normal(ks[0], (B, S, SRC_SIZE), dtype=jnp.float32)
        tgt = jax.random.normal(ks[1], (B, T, TGT_SIZE), dtype=jnp.float32)
        src_mask = (jax.random.uniform(ks[2], (B, S)) > 0.3).astype(jnp.float32)
        src_mask = src_mask.at[:, 0].set(1.0)
        tgt_mask = (jax.random.uniform(ks[3], (B, T)) > 0.3).astype(jnp.float32)
        tgt_mask = tgt_mask.at[:, 0].set(1.0)

        def lin(k, out_f, in_f):
            return jax.random.normal(k, (out_f, in_f), dtype=jnp.float32) / np.sqrt(in_f)
        W_src = lin(ks[4], 2 * OUT_SIZE, SRC_SIZE)
        b_src = jnp.zeros((2 * OUT_SIZE,), jnp.float32)
        W_tgt = lin(ks[5], OUT_SIZE, TGT_SIZE)
        b_tgt = jnp.zeros((OUT_SIZE,), jnp.float32)
        W_out = lin(ks[6], OUT_SIZE, OUT_SIZE + TGT_SIZE)
        b_out = jnp.zeros((OUT_SIZE,), jnp.float32)
        return {'src': src, 'tgt': tgt, 'src_mask': src_mask, 'tgt_mask': tgt_mask, 'W_src': W_src, 'b_src': b_src, 'W_tgt': W_tgt, 'b_tgt': b_tgt, 'W_out': W_out, 'b_out': b_out}
    _L3_xattn_all = _L3_xattn_setup()
    _L3_xattn_in = {k: v for k, v in _L3_xattn_all.items() if k in ('W_src', 'b_src', 'W_tgt', 'b_tgt', 'W_out', 'b_out')}
    del _L3_xattn_all

    def _L3_ffn_setup():
        import jax, jax.numpy as jnp
        import numpy as np
        DIM = 256
        HIDDEN = 768
        SCALE = 1.0 / 127.0

        def _dequant(w_int, dtype):
            return w_int.astype(dtype) * jnp.asarray(SCALE, dtype)
        key = jax.random.key(seed)
        k_x, k_g, k_u, k_d = jax.random.split(key, 4)
        x = jax.random.normal(k_x, (4, 512, DIM), dtype=jnp.float32)
        w_gate = jax.random.randint(k_g, (HIDDEN, DIM), -127, 128, dtype=jnp.int32)
        w_up = jax.random.randint(k_u, (HIDDEN, DIM), -127, 128, dtype=jnp.int32)
        w_down = jax.random.randint(k_d, (DIM, HIDDEN), -127, 128, dtype=jnp.int32)
        return {'x': x, 'w_gate': w_gate, 'w_up': w_up, 'w_down': w_down}
    _L3_ffn_all = _L3_ffn_setup()
    _L3_ffn_in = {k: v for k, v in _L3_ffn_all.items() if k in ('w_gate', 'w_up', 'w_down')}
    del _L3_ffn_all
    return {'x': x, 'ctx_2048': ctx_2048, 'mask_BxS2_if0': mask_BxS2_if0, 'mask_BxS2_fk1': mask_BxS2_fk1, 'L0_attn_W_in': _L0_attn_in['W_in'], 'L0_attn_conv_w': _L0_attn_in['conv_w'], 'L0_attn_conv_b': _L0_attn_in['conv_b'], 'L0_attn_W_x': _L0_attn_in['W_x'], 'L0_attn_W_dt': _L0_attn_in['W_dt'], 'L0_attn_b_dt': _L0_attn_in['b_dt'], 'L0_attn_A_log': _L0_attn_in['A_log'], 'L0_attn_D': _L0_attn_in['D'], 'L0_attn_W_out': _L0_attn_in['W_out'], 'L0_xattn_W_in': _L0_xattn_in['W_in'], 'L0_xattn_b_in': _L0_xattn_in['b_in'], 'L0_xattn_g_res': _L0_xattn_in['g_res'], 'L0_xattn_g_init': _L0_xattn_in['g_init'], 'L0_ffn_weight': _L0_ffn_in['weight'], 'L0_ffn_ln_gamma': _L0_ffn_in['ln_gamma'], 'L0_ffn_ln_beta': _L0_ffn_in['ln_beta'], 'L1_attn_Wq': _L1_attn_in['Wq'], 'L1_attn_Wk': _L1_attn_in['Wk'], 'L1_attn_Wv': _L1_attn_in['Wv'], 'L1_attn_Wo': _L1_attn_in['Wo'], 'L1_attn_bo': _L1_attn_in['bo'], 'L1_xattn_w_qkv': _L1_xattn_in['w_qkv'], 'L1_xattn_w_proj': _L1_xattn_in['w_proj'], 'L1_xattn_b_proj': _L1_xattn_in['b_proj'], 'L1_ffn_ln1_scale': _L1_ffn_in['ln1_scale'], 'L1_ffn_ln1_shift': _L1_ffn_in['ln1_shift'], 'L1_ffn_wq': _L1_ffn_in['wq'], 'L1_ffn_wk': _L1_ffn_in['wk'], 'L1_ffn_wv': _L1_ffn_in['wv'], 'L1_ffn_wo': _L1_ffn_in['wo'], 'L1_ffn_bo': _L1_ffn_in['bo'], 'L1_ffn_ln2_scale': _L1_ffn_in['ln2_scale'], 'L1_ffn_ln2_shift': _L1_ffn_in['ln2_shift'], 'L1_ffn_gate_w': _L1_ffn_in['gate_w'], 'L1_ffn_w1': _L1_ffn_in['w1'], 'L1_ffn_w2': _L1_ffn_in['w2'], 'L1_ffn_w3': _L1_ffn_in['w3'], 'L2_attn_W_qkv': _L2_attn_in['W_qkv'], 'L2_attn_b_qkv': _L2_attn_in['b_qkv'], 'L2_attn_W_out': _L2_attn_in['W_out'], 'L2_attn_b_out': _L2_attn_in['b_out'], 'L2_xattn_Wq': _L2_xattn_in['Wq'], 'L2_xattn_Wkv': _L2_xattn_in['Wkv'], 'L2_xattn_null_kv': _L2_xattn_in['null_kv'], 'L2_xattn_Wout': _L2_xattn_in['Wout'], 'L2_xattn_ln_scale': _L2_xattn_in['ln_scale'], 'L2_xattn_ln_bias': _L2_xattn_in['ln_bias'], 'L2_ffn_gate_w': _L2_ffn_in['gate_w'], 'L2_ffn_w1': _L2_ffn_in['w1'], 'L2_ffn_b1': _L2_ffn_in['b1'], 'L2_ffn_w2': _L2_ffn_in['w2'], 'L2_ffn_b2': _L2_ffn_in['b2'], 'L3_attn_Wq': _L3_attn_in['Wq'], 'L3_attn_bq': _L3_attn_in['bq'], 'L3_attn_Wk': _L3_attn_in['Wk'], 'L3_attn_bk': _L3_attn_in['bk'], 'L3_attn_Wv': _L3_attn_in['Wv'], 'L3_attn_bv': _L3_attn_in['bv'], 'L3_attn_Wo': _L3_attn_in['Wo'], 'L3_attn_bo': _L3_attn_in['bo'], 'L3_xattn_W_src': _L3_xattn_in['W_src'], 'L3_xattn_b_src': _L3_xattn_in['b_src'], 'L3_xattn_W_tgt': _L3_xattn_in['W_tgt'], 'L3_xattn_b_tgt': _L3_xattn_in['b_tgt'], 'L3_xattn_W_out': _L3_xattn_in['W_out'], 'L3_xattn_b_out': _L3_xattn_in['b_out'], 'L3_ffn_w_gate': _L3_ffn_in['w_gate'], 'L3_ffn_w_up': _L3_ffn_in['w_up'], 'L3_ffn_w_down': _L3_ffn_in['w_down']}

def reference(x, ctx_2048, mask_BxS2_if0, mask_BxS2_fk1, L0_attn_W_in, L0_attn_conv_w, L0_attn_conv_b, L0_attn_W_x, L0_attn_W_dt, L0_attn_b_dt, L0_attn_A_log, L0_attn_D, L0_attn_W_out, L0_xattn_W_in, L0_xattn_b_in, L0_xattn_g_res, L0_xattn_g_init, L0_ffn_weight, L0_ffn_ln_gamma, L0_ffn_ln_beta, L1_attn_Wq, L1_attn_Wk, L1_attn_Wv, L1_attn_Wo, L1_attn_bo, L1_xattn_w_qkv, L1_xattn_w_proj, L1_xattn_b_proj, L1_ffn_ln1_scale, L1_ffn_ln1_shift, L1_ffn_wq, L1_ffn_wk, L1_ffn_wv, L1_ffn_wo, L1_ffn_bo, L1_ffn_ln2_scale, L1_ffn_ln2_shift, L1_ffn_gate_w, L1_ffn_w1, L1_ffn_w2, L1_ffn_w3, L2_attn_W_qkv, L2_attn_b_qkv, L2_attn_W_out, L2_attn_b_out, L2_xattn_Wq, L2_xattn_Wkv, L2_xattn_null_kv, L2_xattn_Wout, L2_xattn_ln_scale, L2_xattn_ln_bias, L2_ffn_gate_w, L2_ffn_w1, L2_ffn_b1, L2_ffn_w2, L2_ffn_b2, L3_attn_Wq, L3_attn_bq, L3_attn_Wk, L3_attn_bk, L3_attn_Wv, L3_attn_bv, L3_attn_Wo, L3_attn_bo, L3_xattn_W_src, L3_xattn_b_src, L3_xattn_W_tgt, L3_xattn_b_tgt, L3_xattn_W_out, L3_xattn_b_out, L3_ffn_w_gate, L3_ffn_w_up, L3_ffn_w_down):
    import jax
    import jax.numpy as jnp

    def _L0_attn_ref(x, W_in, conv_w, conv_b, W_x, W_dt, b_dt, A_log, D, W_out):
        import jax, jax.numpy as jnp
        import numpy as np
        from jax import lax
        D_MODEL = 256
        EXPAND = 2
        D_INNER = EXPAND * D_MODEL
        D_STATE = 16
        D_CONV = 4
        DT_RANK = D_MODEL // 16
        B_SZ = 4
        SEQ = 512

        def _mamba_fwd(x, W_in, conv_w, conv_b, W_x, W_dt, b_dt, A_log, D, W_out):
            B, L, _ = x.shape
            xz = jnp.einsum('bld,ed->ble', x, W_in)
            u, z = jnp.split(xz, 2, axis=-1)
            u_nc = u.transpose(0, 2, 1)
            u_c = lax.conv_general_dilated(u_nc, conv_w[:, None, :], window_strides=(1,), padding=[(D_CONV - 1, 0)], feature_group_count=D_INNER, dimension_numbers=('NCH', 'OIH', 'NCH'))
            u_c = (u_c + conv_b[None, :, None]).transpose(0, 2, 1)
            u_c = jax.nn.silu(u_c)
            x_dbl = jnp.einsum('bld,ed->ble', u_c, W_x)
            dt_r, Bm, Cm = jnp.split(x_dbl, [DT_RANK, DT_RANK + D_STATE], axis=-1)
            dt = jax.nn.softplus(jnp.einsum('blr,dr->bld', dt_r, W_dt) + b_dt)
            A = -jnp.exp(A_log)

            def step(h, inp):
                dt_t, u_t, B_t, C_t = inp
                dA = jnp.exp(dt_t[..., None] * A)
                h = dA * h + (dt_t * u_t)[..., None] * B_t[:, None, :]
                y_t = jnp.einsum('bds,bs->bd', h, C_t)
                return (h, y_t)
            xs = (dt.transpose(1, 0, 2), u_c.transpose(1, 0, 2), Bm.transpose(1, 0, 2), Cm.transpose(1, 0, 2))
            h0 = jnp.zeros((B, D_INNER, D_STATE), dtype=x.dtype)
            _, ys = lax.scan(step, h0, xs)
            y = ys.transpose(1, 0, 2)
            y = y + u_c * D
            y = y * jax.nn.silu(z)
            out = jnp.einsum('bld,ed->ble', y, W_out)
            return out

        def _reference_tuple_inner(x, W_in, conv_w, conv_b, W_x, W_dt, b_dt, A_log, D, W_out):
            out = _mamba_fwd(x, W_in, conv_w, conv_b, W_x, W_dt, b_dt, A_log, D, W_out)
            return (out, None)
        return _reference_tuple_inner(x, W_in, conv_w, conv_b, W_x, W_dt, b_dt, A_log, D, W_out)[0]

    def _L0_xattn_ref(embeds, patch_embeds, patch_lens, W_in, b_in, g_res, g_init):
        import jax, jax.numpy as jnp
        import numpy as np
        B, L, P = (4, 1024, 256)
        D_MODEL = 256
        D_GLOBAL = 512
        HEADDIM = 32
        EPSILON = 0.001
        RMS_EPS = 1e-05

        def rmsnorm(x, g, eps=RMS_EPS):
            var = jnp.mean(jnp.square(x), axis=-1, keepdims=True)
            return x * jax.lax.rsqrt(var + eps) * g

        def _hnet_depool(h, h_patch_full, patch_lens):
            h_patch = h_patch_full[..., :D_MODEL]
            bsz, plen = (h_patch.shape[0], h_patch.shape[1])
            seqlen = h.shape[1]
            logp = jnp.full((bsz, plen), -EPSILON, dtype=jnp.float32)
            bidx = jnp.cumsum(patch_lens, axis=1) - 1
            boundary_mask = jnp.zeros((bsz, seqlen), dtype=jnp.int32)
            boundary_mask = boundary_mask.at[jnp.arange(bsz)[:, None], bidx].set(1)
            dt = (-jnp.log(-jnp.expm1(logp))).astype(h_patch.dtype)
            x = h_patch / dt[..., None]
            n_heads = D_MODEL // HEADDIM
            A = -jnp.ones((n_heads,), dtype=jnp.float32)
            bcoef = jnp.exp(logp).astype(h_patch.dtype)
            x4 = x.reshape(bsz, plen, n_heads, HEADDIM)
            a = jnp.exp(dt[:, :, None] * A[None, None, :])
            u = (dt * bcoef)[:, :, None, None] * x4
            a_b = jnp.broadcast_to(a[..., None], u.shape)

            def comb(lft, rgt):
                aL, uL = lft
                aR, uR = rgt
                return (aL * aR, uL * aR + uR)
            _, s = jax.lax.associative_scan(comb, (a_b, u), axis=1)
            depool = s.reshape(bsz, plen, D_MODEL)
            plug = jnp.clip(jnp.cumsum(boundary_mask, axis=1) - 1, 0, plen - 1)
            depool_out = depool[jnp.arange(bsz)[:, None], plug]
            return depool_out + h
        h = rmsnorm(embeds, g_res)
        h = jnp.einsum('bld,ed->ble', h, W_in) + b_in
        h_patch = rmsnorm(patch_embeds, g_init)
        return _hnet_depool(h, h_patch, patch_lens)

    def _L0_ffn_ref(x, weight, ln_gamma, ln_beta):
        import jax, jax.numpy as jnp
        import numpy as np
        LN_EPS = 0.001
        EPS = 1e-05
        QB = 128.0

        def ste_round(x):
            return x + jax.lax.stop_gradient(jnp.round(x) - x)
        mu = jnp.mean(x, axis=-1, keepdims=True)
        var = jnp.var(x, axis=-1, keepdims=True)
        xn = (x - mu) * jax.lax.rsqrt(var + LN_EPS) * ln_gamma + ln_beta
        beta = jnp.mean(jnp.abs(weight))
        w_q = jnp.clip(ste_round(weight / (beta + EPS)), -1.0, 1.0)
        gamma = jnp.max(jnp.abs(xn))
        xq = jnp.clip(xn * QB / gamma, -QB + EPS, QB - EPS)
        y = jnp.einsum('bsd,du->bsu', xq, w_q)
        return y * (gamma * beta / QB)

    def _L1_attn_ref(x, Wq, Wk, Wv, Wo, bo):
        import jax, jax.numpy as jnp
        import numpy as np
        B, N, QD = (4, 1024, 256)
        HEADS, DIM_HEAD = (8, 64)
        HID = HEADS * DIM_HEAD
        SCALE = DIM_HEAD ** (-0.5)
        b, n, _ = x.shape
        q = x @ Wq
        k = x @ Wk
        v = x @ Wv

        def split_heads(t):
            return t.reshape(b, n, HEADS, DIM_HEAD).transpose(0, 2, 3, 1)
        q = split_heads(q)
        k = split_heads(k)
        v = split_heads(v)
        q = jax.nn.softmax(q, axis=-2) * SCALE
        k = jax.nn.softmax(k, axis=-1)
        context = jnp.einsum('bhdn,bhen->bhde', k, v)
        out = jnp.einsum('bhde,bhdn->bhen', context, q)
        out = out.transpose(0, 3, 1, 2).reshape(b, n, HID)
        return out @ Wo + bo

    def _L1_xattn_ref(x, context, w_qkv, w_proj, b_proj):
        import jax, jax.numpy as jnp
        import numpy as np
        NUM_HEADS = 16
        B, N, C = x.shape
        H = NUM_HEADS
        D = C // H
        scale = D ** (-0.5)
        qkv = (x @ w_qkv.T).reshape(B, N, 3, H, D).transpose(2, 0, 3, 1, 4)
        q, k, v = (qkv[0], qkv[1], qkv[2])
        N_c = context.shape[1]
        kv = context.reshape(B, N_c, 2, H, D).transpose(2, 0, 3, 1, 4)
        extra_k, extra_v = (kv[0], kv[1])
        k = jnp.concatenate([extra_k, k], axis=2)
        v = jnp.concatenate([extra_v, v], axis=2)
        dtype = q.dtype
        attn = jnp.einsum('bhnd,bhmd->bhnm', q * scale, k).astype(jnp.float32)
        attn = jax.nn.softmax(attn, axis=-1).astype(dtype)
        out = jnp.einsum('bhnm,bhmd->bhnd', attn, v)
        out = out.transpose(0, 2, 1, 3).reshape(B, N, C)
        return out @ w_proj.T + b_proj

    def _L1_ffn_ref(x, ln1_scale, ln1_shift, wq, wk, wv, wo, bo, ln2_scale, ln2_shift, gate_w, w1, w2, w3):
        import jax, jax.numpy as jnp
        import numpy as np
        EMB = 256
        HID = 512
        HEADS = 16
        HEAD_DIM = EMB // HEADS
        EXPERTS = 8
        TOPK = 2
        EPS = 1e-05

        def layernorm(x, scale, shift):
            mean = jnp.mean(x, axis=-1, keepdims=True)
            var = jnp.mean((x - mean) ** 2, axis=-1, keepdims=True)
            return scale * (x - mean) / jnp.sqrt(var + EPS) + shift

        def attention(x, wq, wk, wv, wo, bo):
            b, t, _ = x.shape
            q = (x @ wq).reshape(b, t, HEADS, HEAD_DIM)
            k = (x @ wk).reshape(b, t, HEADS, HEAD_DIM)
            v = (x @ wv).reshape(b, t, HEADS, HEAD_DIM)
            scores = jnp.einsum('bqhd,bkhd->bhqk', q, k)
            mask = jnp.arange(t)[:, None] < jnp.arange(t)[None, :]
            scores = jnp.where(mask, -jnp.inf, scores)
            attn = jax.nn.softmax(scores / np.sqrt(HEAD_DIM), axis=-1)
            ctx = jnp.einsum('bhqk,bkhd->bqhd', attn, v).reshape(b, t, EMB)
            return ctx @ wo + bo

        def moe_ff(x, gate_w, w1, w2, w3):
            b, t, d = x.shape
            xf = x.reshape(b * t, d)
            scores = xf @ gate_w
            topk_scores, topk_idx = jax.lax.top_k(scores, TOPK)
            topk_probs = jax.nn.softmax(topk_scores, axis=-1)
            weight = jnp.sum(jax.nn.one_hot(topk_idx, EXPERTS, dtype=xf.dtype) * topk_probs[..., None], axis=1)
            h = jax.nn.silu(jnp.einsum('td,edh->eth', xf, w1)) * jnp.einsum('td,edh->eth', xf, w2)
            out_e = jnp.einsum('eth,ehd->etd', h, w3)
            out = jnp.einsum('etd,te->td', out_e, weight)
            return out.reshape(b, t, d)
        h = layernorm(x, ln1_scale, ln1_shift)
        x = x + attention(h, wq, wk, wv, wo, bo)
        h = layernorm(x, ln2_scale, ln2_shift)
        x = x + moe_ff(h, gate_w, w1, w2, w3)
        return x

    def _L2_attn_ref(x, W_qkv, b_qkv, W_out, b_out):
        import jax, jax.numpy as jnp
        import numpy as np
        import math
        EMBED_DIM = 256
        NUM_HEADS = 16
        HEAD_DIM = EMBED_DIM // NUM_HEADS
        B, S, D = x.shape
        H, Hd = (NUM_HEADS, HEAD_DIM)
        slopes = jnp.power(2.0, 8.0 * jnp.arange(0, -H, -1, dtype=jnp.float32) / H)
        qkv = x @ W_qkv.T + b_qkv
        qkv = qkv.reshape(B, S, 3, H, Hd).transpose(2, 0, 3, 1, 4)
        q, k, v = (qkv[0], qkv[1], qkv[2])
        scores = jnp.einsum('bhqd,bhkd->bhqk', q, k) / math.sqrt(Hd)
        pos = jnp.arange(S)
        rel = jnp.abs(pos[None, :] - pos[:, None]).astype(jnp.float32)
        bias = -slopes[:, None, None] * rel
        probs = jax.nn.softmax(scores + bias[None], axis=-1)
        out = jnp.einsum('bhqk,bhkd->bhqd', probs, v)
        out = out.transpose(0, 2, 1, 3).reshape(B, S, D)
        return out @ W_out.T + b_out

    def _L2_xattn_ref(x, context, Wq, Wkv, null_kv, Wout, ln_scale, ln_bias):
        import jax, jax.numpy as jnp
        import numpy as np
        B, N, DIM = (8, 1024, 256)
        M, CTX = (64, 512)
        HEADS, DH = (16, 64)
        INNER = HEADS * DH
        EPS = 1e-06

        def _split_heads(t):
            b, n, _ = t.shape
            return t.reshape(b, n, HEADS, DH).transpose(0, 2, 1, 3)
        scale = DH ** (-0.5)
        b = x.shape[0]
        q = _split_heads(jnp.einsum('bnd,df->bnf', x, Wq))
        kv = jnp.einsum('bmc,cf->bmf', context, Wkv)
        k, v = jnp.split(kv, 2, axis=-1)
        k, v = (_split_heads(k), _split_heads(v))
        nk = jnp.broadcast_to(null_kv[0], (b, HEADS, 1, DH))
        nv = jnp.broadcast_to(null_kv[1], (b, HEADS, 1, DH))
        k = jnp.concatenate((nk, k), axis=-2)
        v = jnp.concatenate((nv, v), axis=-2)
        q = q * scale
        sim = jnp.einsum('bhid,bhjd->bhij', q, k)
        attn = jax.nn.softmax(sim, axis=-1)
        out = jnp.einsum('bhij,bhjd->bhid', attn, v)
        out = out.transpose(0, 2, 1, 3).reshape(b, -1, INNER)
        out = jnp.einsum('bnf,fd->bnd', out, Wout)
        mu = jnp.mean(out, axis=-1, keepdims=True)
        var = jnp.var(out, axis=-1, keepdims=True)
        out = (out - mu) * jax.lax.rsqrt(var + EPS) * ln_scale + ln_bias
        return out

    def _L2_ffn_ref(hidden_states, gate_w, w1, b1, w2, b2):
        import jax, jax.numpy as jnp
        import numpy as np
        B, S, H, E, DFF = (4, 1024, 256, 8, 1024)
        b, s, h = hidden_states.shape
        x = hidden_states.reshape(-1, h)
        gate_logits = x @ gate_w.T
        gate_probs = jax.nn.softmax(gate_logits, axis=-1)
        expert_idx = jnp.argmax(gate_probs, axis=-1)
        expert_w = jnp.take_along_axis(gate_probs, expert_idx[:, None], axis=1)[:, 0]
        out = jnp.zeros_like(x)
        n_experts = w1.shape[0]
        for e in range(n_experts):
            ye = jax.nn.relu(x @ w1[e] + b1[e]) @ w2[e] + b2[e]
            sel = (expert_idx == e)[:, None]
            out = out + jnp.where(sel, ye * expert_w[:, None], 0.0)
        return out.reshape(b, s, h)

    def _L3_attn_ref(embeddings, Wq, bq, Wk, bk, Wv, bv, Wo, bo):
        import jax, jax.numpy as jnp
        import numpy as np
        B, S, D, H = (2, 512, 256, 16)
        DK = D // H
        b, s, d = embeddings.shape
        dk = Wq.shape[-1]
        q = jnp.einsum('bsd,hdk->bhsk', embeddings, Wq) + bq[None, :, None, :]
        k = jnp.einsum('bsd,hdk->bhsk', embeddings, Wk) + bk[None, :, None, :]
        v = jnp.einsum('bsd,hdk->bhsk', embeddings, Wv) + bv[None, :, None, :]
        scores = jnp.einsum('bhqk,bhsk->bhqs', q, k) / jnp.sqrt(jnp.float32(dk))
        causal_mask = jnp.triu(jnp.ones((s, s), dtype=bool), k=1)
        scores = jnp.where(causal_mask, jnp.float32(-1000000000.0), scores)
        weights = jax.nn.softmax(scores, axis=-1)
        ctx = jnp.einsum('bhqs,bhsk->bhqk', weights, v)
        concat = ctx.transpose(0, 2, 1, 3).reshape(b, s, d)
        return concat @ Wo + bo

    def _L3_xattn_ref(src, tgt, src_mask, tgt_mask, W_src, b_src, W_tgt, b_tgt, W_out, b_out):
        import jax, jax.numpy as jnp
        import numpy as np
        B, S, T = (32, 128, 128)
        SRC_SIZE, TGT_SIZE, OUT_SIZE, NUM_HEAD = (512, 256, 256, 8)
        HEAD_DIM = OUT_SIZE // NUM_HEAD
        b, s, _ = src.shape
        t = tgt.shape[1]
        src_trans = jnp.einsum('bsf,of->bso', src, W_src) + b_src
        tgt_trans = jnp.einsum('btf,of->bto', tgt, W_tgt) + b_tgt
        src_trans = src_trans * src_mask[:, :, None]
        tgt_trans = tgt_trans * tgt_mask[:, :, None]
        src_key, src_val = jnp.split(src_trans, 2, axis=2)
        k = src_key.reshape(b, s, NUM_HEAD, HEAD_DIM)
        v = src_val.reshape(b, s, NUM_HEAD, HEAD_DIM)
        q = tgt_trans.reshape(b, t, NUM_HEAD, HEAD_DIM)
        scores = jnp.einsum('bthd,bshd->bhts', q, k) / np.sqrt(HEAD_DIM)
        scores = jnp.where(src_mask[:, None, None, :] == 0, -jnp.inf, scores)
        attn = jax.nn.softmax(scores, axis=-1)
        tgt_update = jnp.einsum('bhts,bshd->bthd', attn, v).reshape(b, t, OUT_SIZE)
        cat_tgt = jnp.concatenate([tgt, tgt_update], axis=2)
        return jnp.einsum('btf,of->bto', cat_tgt, W_out) + b_out

    def _L3_ffn_ref(x, w_gate, w_up, w_down):
        import jax, jax.numpy as jnp
        import numpy as np
        DIM = 256
        HIDDEN = 768
        SCALE = 1.0 / 127.0

        def _dequant(w_int, dtype):
            return w_int.astype(dtype) * jnp.asarray(SCALE, dtype)
        wg = _dequant(w_gate, x.dtype)
        wu = _dequant(w_up, x.dtype)
        wd = _dequant(w_down, x.dtype)
        gate = jnp.einsum('bsd,hd->bsh', x, wg)
        up = jnp.einsum('bsd,hd->bsh', x, wu)
        h = jax.nn.silu(gate) * up
        return jnp.einsum('bsh,dh->bsd', h, wd)
    x = _layernorm(x + _L0_attn_ref(x, L0_attn_W_in, L0_attn_conv_w, L0_attn_conv_b, L0_attn_W_x, L0_attn_W_dt, L0_attn_b_dt, L0_attn_A_log, L0_attn_D, L0_attn_W_out), axis=-1)
    x = _layernorm(x + _L0_xattn_ref(x, ctx_2048, mask_BxS2_if0, L0_xattn_W_in, L0_xattn_b_in, L0_xattn_g_res, L0_xattn_g_init), axis=-1)
    x = _layernorm(x + _L0_ffn_ref(x, L0_ffn_weight, L0_ffn_ln_gamma, L0_ffn_ln_beta), axis=-1)
    x = _layernorm(x + _L1_attn_ref(x, L1_attn_Wq, L1_attn_Wk, L1_attn_Wv, L1_attn_Wo, L1_attn_bo), axis=-1)
    x = _layernorm(x + _L1_xattn_ref(x, ctx_2048, L1_xattn_w_qkv, L1_xattn_w_proj, L1_xattn_b_proj), axis=-1)
    x = _layernorm(x + _L1_ffn_ref(x, L1_ffn_ln1_scale, L1_ffn_ln1_shift, L1_ffn_wq, L1_ffn_wk, L1_ffn_wv, L1_ffn_wo, L1_ffn_bo, L1_ffn_ln2_scale, L1_ffn_ln2_shift, L1_ffn_gate_w, L1_ffn_w1, L1_ffn_w2, L1_ffn_w3), axis=-1)
    x = _layernorm(x + _L2_attn_ref(x, L2_attn_W_qkv, L2_attn_b_qkv, L2_attn_W_out, L2_attn_b_out), axis=-1)
    x = _layernorm(x + _L2_xattn_ref(x, ctx_2048, L2_xattn_Wq, L2_xattn_Wkv, L2_xattn_null_kv, L2_xattn_Wout, L2_xattn_ln_scale, L2_xattn_ln_bias), axis=-1)
    x = _layernorm(x + _L2_ffn_ref(x, L2_ffn_gate_w, L2_ffn_w1, L2_ffn_b1, L2_ffn_w2, L2_ffn_b2), axis=-1)
    x = _layernorm(x + _L3_attn_ref(x, L3_attn_Wq, L3_attn_bq, L3_attn_Wk, L3_attn_bk, L3_attn_Wv, L3_attn_bv, L3_attn_Wo, L3_attn_bo), axis=-1)
    x = _layernorm(x + _L3_xattn_ref(ctx_2048, x, mask_BxS2_fk1, mask_BxS2_fk1, L3_xattn_W_src, L3_xattn_b_src, L3_xattn_W_tgt, L3_xattn_b_tgt, L3_xattn_W_out, L3_xattn_b_out), axis=-1)
    x = _layernorm(x + _L3_ffn_ref(x, L3_ffn_w_gate, L3_ffn_w_up, L3_ffn_w_down), axis=-1)
    return x

_drawn_inputs = setup_inputs


def setup_inputs(seed=0):
    import zlib

    import numpy as np

    out = dict(_drawn_inputs(seed))
    spreads = {'L0_attn_D': (1.0, 0.2),
     'L0_xattn_b_in': (0.0, 0.1),
     'L0_xattn_g_res': (1.0, 0.2),
     'L0_xattn_g_init': (1.0, 0.2),
     'L0_ffn_ln_gamma': (1.0, 0.2),
     'L0_ffn_ln_beta': (0.0, 0.1),
     'L1_ffn_ln1_scale': (1.0, 0.2),
     'L1_ffn_ln1_shift': (0.0, 0.1),
     'L1_ffn_bo': (0.0, 0.1),
     'L1_ffn_ln2_scale': (1.0, 0.2),
     'L1_ffn_ln2_shift': (0.0, 0.1),
     'L2_xattn_ln_scale': (1.0, 0.2),
     'L2_xattn_ln_bias': (0.0, 0.1),
     'L2_ffn_b1': (0.0, 0.702),
     'L2_ffn_b2': (0.0, 0.295),
     'L3_xattn_b_src': (0.0, 0.1),
     'L3_xattn_b_tgt': (0.0, 0.488),
     'L3_xattn_b_out': (0.0, 0.1)}
    factors = {'L0_attn_conv_b': 3.218,
     'L1_attn_Wq': 8.0,
     'L1_attn_Wk': 8.0,
     'L2_attn_b_qkv': 4.995,
     'L2_attn_b_out': 5.877,
     'L2_xattn_null_kv': 3.205,
     'L3_attn_Wq': 8.0,
     'L3_attn_bq': 64.0,
     'L3_attn_Wk': 8.0,
     'L3_attn_bk': 64.0,
     'L3_attn_bv': 6.172}
    for name, (base, spread) in spreads.items():
        noise = np.random.default_rng([zlib.crc32(name.encode()), seed]).standard_normal(out[name].shape)
        drawn = base * np.exp(spread * noise) if base else spread * noise
        out[name] = jnp.asarray(drawn.astype(out[name].dtype))
    for name, factor in factors.items():
        out[name] = (out[name] * factor).astype(out[name].dtype)
    return out
```

```python
from contextlib import ExitStack

import numpy as np

import concourse.bass as bass
from concourse import mybir

ALU = mybir.AluOpType
ACT = mybir.ActivationFunctionType
AX = mybir.AxisListType
F32 = mybir.dt.float32
BF16 = mybir.dt.bfloat16
I32 = mybir.dt.int32
U32 = mybir.dt.uint32

P = 128
B = 16
D = 256
DC = D // P
CTX = 512
CC = CTX // P
LN_EPS = 1e-5
MASKED = -1e30


class Count:

    START = 24

    def __init__(self, sem):
        self.sem, self.base = sem, self.START

    def done(self, item):
        return self.base + item + 1

    def freed(self, item, deep=2):
        return self.base + item + 1 - deep

    def advance(self, items):
        self.base += items


class Core:

    def __init__(self, nc, ctx):
        self.nc, self.ctx = nc, ctx
        self.x = ctx.enter_context(nc.sbuf_tensor("x", [P, B, D], F32))
        self.ident = ctx.enter_context(nc.sbuf_tensor("ident", [P, P], F32))
        self.ident_bf = ctx.enter_context(nc.sbuf_tensor("ident_bf", [P, P], BF16))
        self.ones = ctx.enter_context(nc.sbuf_tensor("ones", [P, P], F32))
        self.ln_eps = ctx.enter_context(nc.sbuf_tensor("ln_eps", [P, 1], F32))
        self.minus_half = ctx.enter_context(nc.sbuf_tensor("minus_half", [P, 1], F32))
        self.counts, self.names = {}, {}
        self.loads = Count(ctx.enter_context(nc.semaphore("loads_landed")))
        self.loads.base = 0
        self.setup = Count(ctx.enter_context(nc.semaphore("setup_done")))
        self.setup.base = 0

    def named(self, name):
        self.names[name] = self.names.get(name, 0) + 1
        return f"{name}_{self.names[name]}"

    def count(self, name):
        if name not in self.counts:
            self.counts[name] = Count(self.ctx.enter_context(self.nc.semaphore(name)))
        return self.counts[name]


def chunked(w, rows=P):
    return w.rearrange("(c p) n -> p c n", p=rows)


def row_everywhere(v, parts=P):
    return v.rearrange("(o n) -> o n", o=1).broadcast_to([parts, v.shape[0]])



class Frame:

    def __init__(self, core, ctx, pre_norm=False, out_bias=None, target=None, norm=True,
                 inner_norm=None, own_input=False, feeds_only=False, out_scale=None,
                 ahead=False):
        nc = core.nc
        self.core, self.nc = core, nc
        self.target = target if target is not None else core.x
        self.pre_norm, self.out_bias, self.norm = pre_norm, out_bias, norm
        self.ahead = ahead
        self.own_input, self.feeds_only, self.out_scale = own_input, feeds_only, out_scale
        self.inner_norm = inner_norm
        sb = lambda n, s, t=F32: ctx.enter_context(nc.sbuf_tensor(core.named(n), s, t))
        self.x_in = sb("x_in", [P, 2, D])
        self.xT = sb("xT", [P, 2, DC, P])
        self.y = sb("y", [P, 2, D])
        self.stats = sb("stats", [P, 2, 6])
        self.mv = sb("mv", [P, 2, 2])
        self.var_eps = sb("var_eps", [P, 2, 1])
        self.rstd = sb("rstd", [P, 2, 1])
        self.xres = sb("xres", [P, 2, D]) if out_bias is not None else self.x_in
        if own_input:
            self.h_in = sb("h_in", [P, 2, D])
        if pre_norm:
            self.pre_stats = sb("pre_stats", [P, 2, 6])
            self.pre_mv = sb("pre_mv", [P, 2, 2])
            self.pre_var = sb("pre_var", [P, 2, 1])
            self.pre_rstd = sb("pre_rstd", [P, 2, 1])
            self.h_in = sb("h_in", [P, 2, D])
        self.bank = ctx.enter_context(nc.psum_tensor(core.named("frame_bank"), [P, 2, D], F32))
        if inner_norm is not None:
            self.in_stats, self.in_mv = sb("in_stats", [P, 2, 6]), sb("in_mv", [P, 2, 2])
            self.in_var, self.in_rstd = sb("in_var", [P, 2, 1]), sb("in_rstd", [P, 2, 1])
            self.inner_eps = sb("inner_eps", [P, 1])
            self.z, self.z_scaled = sb("z", [P, 2, D]), sb("z_scaled", [P, 2, D])
        self.xT_ps = self.bank[:, 0, :].rearrange("p (c t) -> p c t", c=DC)
        self.out_ps = self.bank[:, 1, :]
        c = core.count
        self.x_in_ready, self.xT_turned, self.xT_ready = c("x_in_ready"), c("xT_turned"), c("xT_ready")
        self.xres_ready = c("xres_ready")
        self.out_ready, self.out_used = c("out_ready"), c("out_used")
        self.y_stats, self.y_mv, self.y_var, self.y_rstd, self.x_saved = (
            c("y_stats"), c("y_mv"), c("y_var"), c("y_rstd"), c("x_saved"))
        self.passed = c("waits_passed")
        self.inner = [c("in_stats_done"), c("in_mv_done"), c("in_var_done"), c("in_rstd_done"), c("z_scaled_done"),
                      c("y_ready")]
        self.pre = [c("pre_stats_done"), c("pre_mv_done"), c("pre_var_done"), c("pre_rstd_done"), c("h_ready")]

    def end(self):
        if self.feeds_only:
            for c in [self.x_in_ready, self.xT_turned, self.xT_ready] + (self.pre if self.pre_norm else []):
                c.advance(B)
            return
        if self.own_input:
            self.pre[4].advance(B)
        for c in (self.x_in_ready, self.xT_turned, self.xT_ready, self.out_ready, self.out_used, self.x_saved):
            c.advance(B)
        if self.norm:
            for c in (self.y_stats, self.y_mv, self.y_var, self.y_rstd):
                c.advance(B)
        if self.out_bias is not None:
            self.xres_ready.advance(B)
        if self.inner_norm is not None:
            for c in self.inner:
                c.advance(B)
        if self.pre_norm:
            for c in self.pre:
                c.advance(B)

    def fetch(self, pool, b, j, source=None):
        through = self.xT_turned if self.feeds_only or self.ahead else self.x_saved
        pool.wait_ge(through.sem, through.freed(b))
        source = self.core.x if source is None else source
        pool.tensor_copy(self.x_in[:, j, :], source[:, b, :]).then_inc(self.x_in_ready.sem, 1)
        if self.out_bias is not None:
            pool.wait_ge(self.x_in_ready.sem, self.x_in_ready.done(b))
            bias = self.out_bias(b) if callable(self.out_bias) else self.out_bias
            pool.tensor_tensor(self.xres[:, j, :], self.x_in[:, j, :], bias, ALU.add
                               ).then_inc(self.xres_ready.sem, 1)
        if self.pre_norm:
            _, mv, var, rstd, _ = self.pre
            pool.wait_ge(mv.sem, mv.done(b))
            pool.tensor_tensor(self.pre_var[:, j, :], self.pre_mv[:, j, 1:2], self.core.ln_eps[:, :], ALU.add
                               ).then_inc(var.sem, 1)
            pool.wait_ge(var.sem, var.done(b))
            pool.tensor_tensor(self.pre_rstd[:, j, :], self.pre_var[:, j, :], self.core.minus_half[:, :], ALU.pow
                               ).then_inc(rstd.sem, 1)

    def normalise_in(self, dve, b, j):
        if not self.pre_norm:
            return
        stats, mv, _, rstd, h = self.pre
        dve.wait_ge(self.x_in_ready.sem, self.x_in_ready.done(b))
        dve.bn_stats(self.pre_stats[:, j, :], self.x_in[:, j, :]).then_inc(stats.sem, 1)
        dve.wait_ge(stats.sem, stats.done(b))
        dve.sem_inc(self.passed.sem, 1)
        dve.bn_aggr(self.pre_mv[:, j, :], self.pre_stats[:, j, :]).then_inc(mv.sem, 1)
        dve.wait_ge(rstd.sem, rstd.done(b))
        dve.wait_ge(mv.sem, mv.done(b))
        dve.wait_ge(self.xT_turned.sem, self.xT_turned.freed(b))
        dve.tensor_scalar(self.h_in[:, j, :], self.x_in[:, j, :], self.pre_mv[:, j, 0:1], self.pre_rstd[:, j, :],
                          ALU.subtract, ALU.mult).then_inc(h.sem, 1)

    def turn(self, pe, b, j):
        own = self.pre_norm or self.own_input
        src = self.h_in if own else self.x_in
        ready = self.pre[4] if own else self.x_in_ready
        pe.wait_ge(ready.sem, ready.done(b))
        if self.feeds_only:
            pe.wait_ge(self.xT_ready.sem, self.xT_ready.freed(b, 1))
        elif j == 0:
            pe.wait_ge(self.out_used.sem, self.out_used.freed(b, 1))
        else:
            pe.wait_ge(self.xT_ready.sem, self.xT_ready.done(b - 1))
        for c in range(DC):
            last = pe.transpose(self.xT_ps[:, c, :], src[:, j, c * P:(c + 1) * P], self.core.ident[:, :])
        last.then_inc(self.xT_turned.sem, 1)

    def claim_bank(self, pe, b, j):
        if j == 0:
            pe.wait_ge(self.xT_ready.sem, self.xT_ready.done(b + 1))
        else:
            pe.wait_ge(self.out_used.sem, self.out_used.done(b - 1))

    def copy_turned(self, act, b, j, scale=None, shift=None):
        act.wait_ge(self.xT_turned.sem, self.xT_turned.done(b))
        if not self.feeds_only:
            act.wait_ge(self.out_ready.sem, self.out_ready.freed(b))
        out = self.xT[:, j]
        if scale is None:
            last = act.activation(out, self.xT_ps, ACT.Copy)
        else:
            for c in range(DC):
                last = act.activation(out[:, c, :], self.xT_ps[:, c, :], ACT.Identity,
                                      bias=0.0 if shift is None else shift[:, c:c + 1],
                                      scale=scale[:, c:c + 1])
        last.then_inc(self.xT_ready.sem, 1)

    def finish(self, dve, b, j, result=None):
        dve.wait_ge(self.out_ready.sem, self.out_ready.done(b))
        if self.out_bias is not None:
            dve.wait_ge(self.xres_ready.sem, self.xres_ready.done(b))
        else:
            dve.wait_ge(self.x_in_ready.sem, self.x_in_ready.done(b))
        src = self.out_ps if result is None else result
        if self.inner_norm is not None:
            stats, mv, _, rstd, scaled, y_ready = self.inner
            dve.bn_stats(self.in_stats[:, j, :], src).then_inc(stats.sem, 1)
            dve.wait_ge(stats.sem, stats.done(b))
            dve.sem_inc(self.passed.sem, 1)
            dve.bn_aggr(self.in_mv[:, j, :], self.in_stats[:, j, :]).then_inc(mv.sem, 1)
            dve.wait_ge(mv.sem, mv.done(b))
            dve.wait_ge(rstd.sem, rstd.done(b))
            dve.tensor_scalar(self.z[:, j, :], src, self.in_mv[:, j, 0:1], self.in_rstd[:, j, :],
                              ALU.subtract, ALU.mult).then_inc(self.out_used.sem, 1)
            dve.wait_ge(self.out_used.sem, self.out_used.done(b))
            dve.tensor_tensor(self.z_scaled[:, j, :], self.z[:, j, :], self.inner_norm, ALU.mult
                              ).then_inc(scaled.sem, 1)
            dve.wait_ge(scaled.sem, scaled.done(b))
            dve.tensor_tensor(self.y[:, j, :], self.z_scaled[:, j, :], self.xres[:, j, :], ALU.add
                              ).then_inc(y_ready.sem, 1)
            dve.wait_ge(y_ready.sem, y_ready.done(b))
            self.layernorm(dve, b, j)
            return
        if not self.norm:
            dve.tensor_tensor(self.target[:, b, :], src, self.xres[:, j, :], ALU.add
                              ).then_inc(self.out_used.sem, 1)
            dve.wait_ge(self.out_used.sem, self.out_used.done(b))
            dve.sem_inc(self.x_saved.sem, 1)
            return
        if self.out_scale is not None:
            dve.scalar_tensor_tensor(out=self.y[:, j, :], in0=src, scalar=self.out_scale, in1=self.xres[:, j, :],
                                     op0=ALU.mult, op1=ALU.add).then_inc(self.out_used.sem, 1)
        else:
            residual = self.core.x[:, b, :] if self.ahead else self.xres[:, j, :]
            dve.tensor_tensor(self.y[:, j, :], src, residual, ALU.add).then_inc(self.out_used.sem, 1)
        dve.wait_ge(self.out_used.sem, self.out_used.done(b))
        self.layernorm(dve, b, j)

    def layernorm(self, dve, b, j):
        dve.bn_stats(self.stats[:, j, :], self.y[:, j, :]).then_inc(self.y_stats.sem, 1)
        dve.wait_ge(self.y_stats.sem, self.y_stats.done(b))
        dve.sem_inc(self.passed.sem, 1)
        dve.bn_aggr(self.mv[:, j, :], self.stats[:, j, :]).then_inc(self.y_mv.sem, 1)

    def rstd_out(self, pool, b, j):
        if self.inner_norm is not None:
            _, mv, var, rstd, _, _ = self.inner
            pool.wait_ge(mv.sem, mv.done(b))
            pool.tensor_tensor(self.in_var[:, j, :], self.in_mv[:, j, 1:2], self.inner_eps[:, :], ALU.add
                               ).then_inc(var.sem, 1)
            pool.wait_ge(var.sem, var.done(b))
            pool.tensor_tensor(self.in_rstd[:, j, :], self.in_var[:, j, :], self.core.minus_half[:, :], ALU.pow
                               ).then_inc(rstd.sem, 1)
        pool.wait_ge(self.y_mv.sem, self.y_mv.done(b))
        pool.tensor_tensor(self.var_eps[:, j, :], self.mv[:, j, 1:2], self.core.ln_eps[:, :], ALU.add
                           ).then_inc(self.y_var.sem, 1)
        pool.wait_ge(self.y_var.sem, self.y_var.done(b))
        pool.tensor_tensor(self.rstd[:, j, :], self.var_eps[:, j, :], self.core.minus_half[:, :], ALU.pow
                           ).then_inc(self.y_rstd.sem, 1)

    def save_normed(self, dve, b, j):
        dve.wait_ge(self.y_rstd.sem, self.y_rstd.done(b))
        dve.wait_ge(self.y_mv.sem, self.y_mv.done(b))
        dve.tensor_scalar(self.target[:, b, :], self.y[:, j, :], self.mv[:, j, 0:1], self.rstd[:, j, :],
                          ALU.subtract, ALU.mult).then_inc(self.x_saved.sem, 1)


def setup_stage(core):
    nc = core.nc
    n = core.setup
    with nc.Block() as block:
        @block.gpsimd
        def _(pool):
            for c in core.counts.values():
                pool.sem_inc(c.sem, Count.START)
            pool.memset(core.ident[:, :], 0.0).then_inc(n.sem, 1)
            pool.memset(core.ones[:, :], 1.0).then_inc(n.sem, 1)
            pool.memset(core.minus_half[:, :], -0.5).then_inc(n.sem, 1)
            pool.memset(core.ln_eps[:, :], LN_EPS).then_inc(n.sem, 1)
            pool.wait_ge(n.sem, 4)
            pool.affine_select(out=core.ident[:, :], in_=core.ident[:, :], compare_op=ALU.not_equal, fill=1.0,
                               base=0, pattern=[[-1, P]], channel_multiplier=1).then_inc(n.sem, 1)
            pool.wait_ge(n.sem, 5)
            pool.tensor_copy(core.ident_bf[:, :], core.ident[:, :]).then_inc(n.sem, 1)
            pool.wait_ge(n.sem, 6)
    n.advance(6)


def load_stage(core, x):
    nc, loads = core.nc, core.loads
    with nc.Block() as block:
        @block.sync
        def _(sp):
            sp.dma_start(core.x[:, :, :], x.rearrange("b t d -> t b d")).then_inc(loads.sem, 16)
            sp.wait_ge(loads.sem, loads.base + 16)
    loads.advance(16)


def store_stage(core, out):
    nc, loads = core.nc, core.loads
    with nc.Block() as block:
        @block.sync
        def _(sp):
            sp.dma_start(out.rearrange("b t d -> t b d"), core.x[:, :, :]).then_inc(loads.sem, 16)
            sp.wait_ge(loads.sem, loads.base + 16)
    loads.advance(16)



def int_mlp_stage(core, w_gate_t, w_up_t, w_down_t):
    nc, loads, setup = core.nc, core.loads, core.setup
    H = w_gate_t.shape[1]
    HC = H // P
    with ExitStack() as ctx:
        f = Frame(core, ctx)
        sb = lambda n, s, t=F32: ctx.enter_context(nc.sbuf_tensor(core.named(n), s, t))
        w_int = [sb("wg_int", [P, DC, H], I32), sb("wu_int", [P, DC, H], I32), sb("wd_int", [P, HC, D], I32)]
        wg, wu, wd = sb("wg", [P, DC, H]), sb("wu", [P, DC, H]), sb("wd", [P, HC, D])
        silu = sb("silu", [P, 2, HC, P])
        hT = sb("hT", [P, 2, HC, P])
        gate_ps = ctx.enter_context(nc.psum_tensor(core.named("gate_ps"), [P, 8, P], F32))
        up_ps = ctx.enter_context(nc.psum_tensor(core.named("up_ps"), [P, 8, P], F32))
        weights = setup.base + 3
        gate_ready, up_ready = core.count("gate_ready"), core.count("up_ready")
        silu_done, hT_ready = core.count("silu_done"), core.count("hT_ready")
        with nc.Block() as block:
            @block.sync
            def _(sp):
                for dst, src in zip(w_int, (w_gate_t, w_up_t, w_down_t)):
                    sp.dma_start(dst[:, :, :], chunked(src)).then_inc(loads.sem, 16)

            @block.gpsimd
            def _(pool):
                with pool.Fori(0, B // 2) as i:
                    for j in range(2):
                        f.fetch(pool, 2 * i + j, j)
                    for j in range(2):
                        f.rstd_out(pool, 2 * i + j, j)

            @block.tensor
            def _(pe):
                pe.wait_ge(setup.sem, weights)
                with pe.Fori(0, B // 2) as i:
                    for j in range(2):
                        f.turn(pe, 2 * i + j, j)
                    for j in range(2):
                        b = 2 * i + j
                        pe.wait_ge(f.xT_ready.sem, f.xT_ready.done(b))
                        for ps, w, used, ready in ((gate_ps, wg, silu_done, gate_ready), (up_ps, wu, hT_ready, up_ready)):
                            pe.wait_ge(used.sem, used.freed(b, 1))
                            for m in range(HC):
                                for c in range(DC):
                                    last = pe.matmul(ps[:, m, :], w[:, c, m * P:(m + 1) * P], f.xT[:, j, c, :],
                                                     start=(c == 0), stop=(c == DC - 1))
                            last.then_inc(ready.sem, 1)
                    for j in range(2):
                        b = 2 * i + j
                        pe.wait_ge(hT_ready.sem, hT_ready.done(b))
                        f.claim_bank(pe, b, j)
                        for m in range(HC):
                            last = pe.matmul(f.out_ps, hT[:, j, m, :], wd[:, m, :],
                                             start=(m == 0), stop=(m == HC - 1))
                        last.then_inc(f.out_ready.sem, 1)

            @block.scalar
            def _(act):
                with act.Fori(0, B // 2) as i:
                    for j in range(2):
                        f.copy_turned(act, 2 * i + j, j)
                    for j in range(2):
                        b = 2 * i + j
                        act.wait_ge(gate_ready.sem, gate_ready.done(b))
                        act.wait_ge(hT_ready.sem, hT_ready.freed(b))
                        act.activation(silu[:, j], gate_ps[:, 0:HC, :], ACT.Silu).then_inc(silu_done.sem, 1)

            @block.vector
            def _(dve):
                dve.wait_ge(loads.sem, loads.base + 48)
                for dst, src in zip((wg, wu, wd), w_int):
                    dve.tensor_scalar(dst[:, :, :], src[:, :, :], float(np.float32(1.0 / 127.0)), None, ALU.mult
                                      ).then_inc(setup.sem, 1)
                with dve.Fori(0, B // 2) as i:
                    for j in range(2):
                        b = 2 * i + j
                        dve.wait_ge(silu_done.sem, silu_done.done(b))
                        dve.wait_ge(up_ready.sem, up_ready.done(b))
                        dve.wait_ge(f.out_ready.sem, f.out_ready.freed(b))
                        dve.tensor_tensor(hT[:, j], up_ps[:, 0:HC, :], silu[:, j], ALU.mult
                                          ).then_inc(hT_ready.sem, 1)
                    for j in range(2):
                        f.finish(dve, 2 * i + j, j)
                    for j in range(2):
                        f.save_normed(dve, 2 * i + j, j)
        for c in (gate_ready, up_ready, silu_done, hT_ready):
            c.advance(B)
        f.end()
        setup.advance(3)
        loads.advance(48)



class Attention:

    def __init__(self, core, ctx, frame, heads, head_dim, chunks, scale, key_tiles=1, a_items=1, b_items=2,
                 mask=None, bias=None, null=None, q_chunks=4, parts=1):
        nc = core.nc
        self.core, self.nc, self.f = core, nc, frame
        self.H, self.hd, self.chunks, self.scale, self.kt = heads, head_dim, chunks, scale, key_tiles
        self.NA, self.NB = a_items, b_items
        self.mask, self.bias, self.null = mask, bias, null
        self.n = len(chunks)
        self.parts, self.per_part = parts, len(chunks) // parts
        self.PH = heads // parts
        self.hc = len(chunks[0][1])
        self.W = key_tiles * P
        self.vw = head_dim + (0 if null is not None else 1)
        sb = lambda n, s, t=F32: ctx.enter_context(nc.sbuf_tensor(core.named(n), s, t))
        ps = lambda n, s: ctx.enter_context(nc.psum_tensor(core.named(n), s, F32))
        rows = 64 if head_dim == 64 else 32
        self.rows = head_dim
        self.qT = sb("qT", [P, 2, q_chunks, P])
        self.kT = sb("kT", [P, 2, q_chunks, self.W])
        self.v = sb("v", [P, 2, key_tiles, heads, self.vw])
        self.mx = sb("mx", [P, 2, self.hc])
        self.negmax = sb("negmax", [P, 2, self.hc])
        self.probs = sb("probs", [P, 2, self.hc, self.W])
        self.pT = sb("pT", [P, 2, self.hc * key_tiles, P])
        self.inv = sb("inv", [P, 2, heads])
        if null is not None:
            self.snull, self.pnull_arg = sb("snull", [P, 2, heads]), sb("pnull_arg", [P, 2, self.hc])
            self.mx_all = sb("mx_all", [P, 2, self.hc])
            self.pnull, self.sums = sb("pnull", [P, 2, heads]), sb("sums", [P, 2, heads])
            self.tot = sb("tot", [P, 2, heads])
            self.null_v = sb("null_v", [P, 2, heads, head_dim])
            self.o_sum = sb("o_sum", [P, 2, heads, head_dim])
        self.a = sb("a", [P, 2, heads * head_dim])
        self.AC = heads * head_dim // P
        self.aT = sb("aT", [P, 2, self.AC, P])
        if bias is not None:
            self.biased = sb("biased", [P, 2, self.hc, self.W])
        self.bank_a, self.bank_b = ps("bank_a", [P, 4, P]), ps("bank_b", [P, 4, P])
        self.s_ps = [ps(f"s_ps{i}", [P, self.hc, self.W]) if self.hc * self.W == 512 else
                     ps(f"s_ps{i}", [P, 512]) for i in range(2)]
        self.t_ps = [ps(f"t_ps{i}", [P, 4, P]) for i in range(2)]
        self.o_ps = ps("o_ps", [P, 512])
        c = core.count
        (self.a_made, self.a_taken, self.b_made, self.b_taken) = (
            c("bank_a_made"), c("bank_a_taken"), c("bank_b_made"), c("bank_b_taken"))
        self.scored, self.biased_done, self.max_done, self.negmax_done = (
            c("scored"), c("biased_done"), c("max_done"), c("negmax_done"))
        self.exp_done, self.p_turned, self.weighed = c("exp_done"), c("p_turned"), c("weighed")
        self.pT_ready = [c("pT_even_ready"), c("pT_odd_ready")]
        self.inv_ready, self.a_ready = c("inv_ready"), c("a_ready")
        self.max_all, self.null_arg, self.tot_ready, self.null_v_ready, self.o_summed = (
            c("max_all"), c("null_arg"), c("tot_ready"), c("null_v_ready"), c("o_summed"))

    def end(self):
        for c, items in ((self.a_made, self.NA + self.parts), (self.a_taken, self.NA + self.parts),
                         (self.b_made, self.NB), (self.b_taken, self.NB),
                         (self.scored, self.n), (self.max_done, self.n), (self.negmax_done, self.n),
                         (self.exp_done, self.n), (self.p_turned, self.n), (self.pT_ready[0], self.n // 2), (self.pT_ready[1], self.n // 2),
                         (self.weighed, self.n), (self.inv_ready, self.parts), (self.a_ready, self.parts)):
            c.advance(B * items)
        if self.null is not None:
            for c in (self.max_all, self.null_arg):
                c.advance(B * self.n)
            for c in (self.tot_ready, self.null_v_ready, self.o_summed):
                c.advance(B * self.parts)
        if self.bias is not None:
            self.biased_done.advance(B * self.n)
        self.f.end()

    def heads_of(self, t, j, n):
        heads = [h for cc, h in self.chunks[n][1]]
        step = heads[1] - heads[0]
        return t[:, j, heads[0]:heads[-1] + 1:step]

    def use_a(self, i, j, m):
        return i * 2 * (self.NA + self.parts) + j * self.NA + m

    def use_aT(self, i, j, part):
        return i * 2 * (self.NA + self.parts) + 2 * self.NA + j * self.parts + part

    def use_b(self, i, j, m):
        return i * 2 * self.NB + j * self.NB + m

    def claim_a(self, pe, use):
        pe.wait_ge(self.a_taken.sem, self.a_taken.freed(use, 1))

    def claim_b(self, pe, use):
        pe.wait_ge(self.b_taken.sem, self.b_taken.freed(use, 1))

    def operands_free(self, eng, b):
        eng.wait_ge(self.weighed.sem, self.weighed.done(self.n * (b - 2) + self.n - 1))

    def heads_shape(self, t):
        if self.hc * self.W == 512:
            return t[:, :, :]
        return t[:, 0:self.hc * self.W].rearrange("p (h k) -> p h k", h=self.hc)

    def half(self, i, j, n):
        return self.n // 2 * (2 * i + j) + n // 2

    def score(self, pe, i, j, n):
        b = 2 * i + j
        g = self.n * b + n
        row, heads = self.chunks[n]
        slot = n % 2
        if n == 0:
            pe.wait_ge(self.a_taken.sem, self.a_taken.done(self.use_a(i, j, self.NA - 1)))
            pe.wait_ge(self.b_taken.sem, self.b_taken.done(self.use_b(i, j, self.NB - 1)))
        pe.wait_ge(self.exp_done.sem, self.exp_done.freed(g))
        if self.bias is not None:
            pe.wait_ge(self.biased_done.sem, self.biased_done.freed(g))
        s = self.heads_shape(self.s_ps[slot])
        extra = self.mask is not None
        for k, (cc, h) in enumerate(heads):
            last = pe.matmul(s[:, k, :], self.qT[row:row + self.rows, j, cc, :], self.kT[row:row + self.rows, j, cc, :],
                             start=True, stop=not extra)
            if self.mask is not None:
                last = pe.matmul(s[:, k, :], self.core.ident_bf[:, :], self.mask(b), start=False, stop=True)
        last.then_inc(self.scored.sem, 1)

    def turn_probs(self, pe, i, j, n):
        g = self.n * (2 * i + j) + n
        slot = n % 2
        pe.wait_ge(self.exp_done.sem, self.exp_done.done(g))
        copied = self.pT_ready[slot]
        pe.wait_ge(copied.sem, copied.freed(self.half(i, j, n), 1))
        for k in range(self.hc):
            for t in range(self.kt):
                last = pe.transpose(self.t_ps[slot][:, k * self.kt + t, :],
                                    self.probs[:, slot, k, t * P:(t + 1) * P], self.core.ident[:, :])
        last.then_inc(self.p_turned.sem, 1)

    def weigh(self, pe, i, j, n):
        b = 2 * i + j
        g = self.n * b + n
        slot = n % 2
        pe.wait_ge(self.pT_ready[slot].sem, self.pT_ready[slot].done(self.half(i, j, n)))
        if n % self.per_part == 0:
            pe.wait_ge(self.a_ready.sem, self.a_ready.freed(b * self.parts + n // self.per_part, 1))
        for k, (cc, h) in enumerate(self.chunks[n][1]):
            for t in range(self.kt):
                o = (h % self.PH) * self.vw
                last = pe.matmul(self.o_ps[:, o:o + self.vw], self.pT[:, slot, k * self.kt + t, :],
                                 self.v[:, j, t, h, :], start=(t == 0), stop=(t == self.kt - 1))
        last.then_inc(self.weighed.sem, 1)

    def turn_result(self, pe, i, j, part):
        b = 2 * i + j
        pe.wait_ge(self.a_ready.sem, self.a_ready.done(b * self.parts + part))
        self.claim_a(pe, self.use_aT(i, j, part))
        per = self.AC // self.parts
        for c in range(per):
            at = part * per + c
            last = pe.transpose(self.bank_a[:, c, :], self.a[:, j, at * P:(at + 1) * P], self.core.ident[:, :])
        last.then_inc(self.a_made.sem, 1)

    def exponentiate(self, act, i, j, n):
        g = self.n * (2 * i + j) + n
        slot = n % 2
        act.wait_ge(self.negmax_done.sem, self.negmax_done.done(g))
        act.wait_ge(self.p_turned.sem, self.p_turned.freed(g))
        src = self.heads_shape(self.s_ps[slot]) if self.bias is None else self.biased[:, slot]
        scale = self.scale if self.bias is None else 1.0
        for k, (cc, h) in enumerate(self.chunks[n][1]):
            last = act.activation(self.probs[:, slot, k, :], src[:, k, :], ACT.Exp,
                                  bias=self.negmax[:, slot, k:k + 1], scale=scale,
                                  accum_out=self.sums[:, j, h:h + 1] if self.null is not None else None)
        if self.null is not None:
            act.wait_ge(self.null_arg.sem, self.null_arg.done(g))
            last = act.activation(self.heads_of(self.pnull, j, n), self.pnull_arg[:, slot, :], ACT.Exp)
        last.then_inc(self.exp_done.sem, 1)

    def copy_probs(self, eng, i, j, n):
        g = self.n * (2 * i + j) + n
        slot = n % 2
        eng.wait_ge(self.p_turned.sem, self.p_turned.done(g))
        eng.wait_ge(self.weighed.sem, self.weighed.freed(g))
        used = self.hc * self.kt
        out, src = self.pT[:, slot, :, :], self.t_ps[slot][:, 0:used, :]
        last = eng.tensor_copy(out, src) if n % 2 else eng.activation(out, src, ACT.Copy)
        last.then_inc(self.pT_ready[slot].sem, 1)

    def copy_result(self, act, i, j, part):
        b = 2 * i + j
        act.wait_ge(self.a_made.sem, self.a_made.done(self.use_aT(i, j, part)))
        act.wait_ge(self.f.out_ready.sem, self.f.out_ready.freed(b))
        per = self.AC // self.parts
        act.activation(self.aT[:, j, part * per:(part + 1) * per, :], self.bank_a[:, 0:per, :], ACT.Copy
                       ).then_inc(self.a_taken.sem, 1)

    def row_max(self, dve, i, j, n):
        g = self.n * (2 * i + j) + n
        slot = n % 2
        s = self.heads_shape(self.s_ps[slot])
        dve.wait_ge(self.scored.sem, self.scored.done(g))
        if self.bias is not None:
            dve.wait_ge(self.exp_done.sem, self.exp_done.freed(g))
            dve.scalar_tensor_tensor(out=self.biased[:, slot], in0=s, scalar=self.scale, in1=self.bias[:, n],
                                     op0=ALU.mult, op1=ALU.add).then_inc(self.biased_done.sem, 1)
            dve.wait_ge(self.biased_done.sem, self.biased_done.done(g))
            s = self.biased[:, slot]
        dve.tensor_reduce(self.mx[:, slot, :], s, AX.X, ALU.max).then_inc(self.max_done.sem, 1)
        dve.wait_ge(self.max_done.sem, self.max_done.done(g))
        mx = self.mx
        if self.null is not None:
            mx = self.mx_all
            dve.tensor_tensor(mx[:, slot, :], self.mx[:, slot, :], self.heads_of(self.snull, j, n), ALU.max
                              ).then_inc(self.max_all.sem, 1)
            dve.wait_ge(self.max_all.sem, self.max_all.done(g))
        dve.wait_ge(self.exp_done.sem, self.exp_done.freed(g))
        dve.tensor_scalar(self.negmax[:, slot, :], mx[:, slot, :],
                          -self.scale if self.bias is None else -1.0, None, ALU.mult).then_inc(self.negmax_done.sem, 1)
        if self.null is not None:
            dve.wait_ge(self.negmax_done.sem, self.negmax_done.done(g))
            dve.scalar_tensor_tensor(out=self.pnull_arg[:, slot, :], in0=self.heads_of(self.snull, j, n),
                                     scalar=self.scale, in1=self.negmax[:, slot, :], op0=ALU.mult, op1=ALU.add
                                     ).then_inc(self.null_arg.sem, 1)

    def normalise(self, dve, i, j, part):
        b = 2 * i + j
        g = b * self.parts + part
        h0, h1 = part * self.PH, (part + 1) * self.PH
        o = self.o_ps[:, 0:self.PH * self.vw].rearrange("p (h d) -> p h d", h=self.PH)
        out = self.a[:, j, :].rearrange("p (h d) -> p h d", h=self.H)[:, h0:h1, :]
        dve.wait_ge(self.weighed.sem, self.weighed.done(self.n * b + self.per_part * (part + 1) - 1))
        if self.null is not None:
            dve.wait_ge(self.exp_done.sem, self.exp_done.done(self.n * b + self.per_part * (part + 1) - 1))
            dve.tensor_tensor(self.tot[:, j, h0:h1], self.sums[:, j, h0:h1], self.pnull[:, j, h0:h1], ALU.add
                              ).then_inc(self.tot_ready.sem, 1)
            dve.wait_ge(self.tot_ready.sem, self.tot_ready.done(g))
            dve.reciprocal(self.inv[:, j, h0:h1], self.tot[:, j, h0:h1]).then_inc(self.inv_ready.sem, 1)
            dve.wait_ge(self.null_v_ready.sem, self.null_v_ready.done(g))
            dve.tensor_tensor(self.o_sum[:, j, h0:h1, :], o, self.null_v[:, j, h0:h1, :], ALU.add
                              ).then_inc(self.o_summed.sem, 1)
            dve.wait_ge(self.o_summed.sem, self.o_summed.done(g))
            o = self.o_sum[:, j, h0:h1, :]
        else:
            dve.reciprocal(self.inv[:, j, :], o[:, :, self.hd]).then_inc(self.inv_ready.sem, 1)
        dve.wait_ge(self.inv_ready.sem, self.inv_ready.done(g))
        dve.wait_ge(self.a_made.sem, self.a_made.done(self.use_aT(i - 1, j, part)))
        dve.tensor_tensor(out, o[:, :, 0:self.hd],
                          self.inv[:, j, h0:h1].unsqueeze(2).broadcast_to([P, self.PH, self.hd]), ALU.mult
                          ).then_inc(self.a_ready.sem, 1)

    def weigh_null(self, pool, i, j, part):
        b = 2 * i + j
        h0, h1 = part * self.PH, (part + 1) * self.PH
        pool.wait_ge(self.exp_done.sem, self.exp_done.done(self.n * b + self.per_part * (part + 1) - 1))
        pool.wait_ge(self.o_summed.sem, self.o_summed.done((b - 2) * self.parts + part))
        pool.tensor_tensor(self.null_v[:, j, h0:h1, :],
                           self.pnull[:, j, h0:h1].unsqueeze(2).broadcast_to([P, self.PH, self.hd]),
                           self.null.unsqueeze(1).broadcast_to([P, self.PH, self.hd]), ALU.mult
                           ).then_inc(self.null_v_ready.sem, 1)

    def steps(self):
        total = 2 * self.n
        order = [("head", 0, 0), ("head", 1, 0), ("project", 0, 0)]
        for s in range(total + 2):
            if s == self.n - 2:
                order.append(("project", 1, 0))
            if s < total:
                order.append(("score", s // self.n, s % self.n))
            if 1 <= s <= total:
                order.append(("turn", (s - 1) // self.n, (s - 1) % self.n))
            if 2 <= s:
                order.append(("weigh", (s - 2) // self.n, (s - 2) % self.n))
            done = s - 1
            for part in range(self.parts):
                if done == self.per_part * (part + 1):
                    order.append(("normalise", 0, part))
                if done == self.n + self.per_part * (part + 1):
                    order.append(("normalise", 1, part))
                if done == min(self.per_part * (part + 1), self.n) + 2:
                    order.append(("turn_result", 0, part))
            if s == self.n + 4:
                order.append(("out", 0, 0))
        if self.n + 4 > total + 1:
            order.append(("out", 0, 0))
        return order + [("turn_result", 1, part) for part in range(self.parts)] + [("out", 1, 0)]

    def run(self, block, project, take_a, take_b, out_products, sync=None, pool_before=None, pool_head=None,
            pe_before=None, act_before=None, dve_before=None, act_scale=None, act_shift=None):
        f, order = self.f, self.steps()

        if sync is not None:
            block.sync(sync)

        @block.gpsimd
        def _(pool):
            if pool_before:
                pool_before(pool)
            with pool.Fori(0, B // 2) as i:
                for step, j, n in order:
                    if step == "head":
                        f.fetch(pool, 2 * i + j, j)
                        if pool_head:
                            pool_head(pool, i, j)
                    if step == "normalise" and self.null is not None:
                        self.weigh_null(pool, i, j, n)
                    if step == "out" and f.norm:
                        f.rstd_out(pool, 2 * i + j, j)

        @block.tensor
        def _(pe):
            pe_before(pe)
            with pe.Fori(0, B // 2) as i:
                for step, j, n in order:
                    if step == "head":
                        f.turn(pe, 2 * i + j, j)
                    if step == "project":
                        pe.wait_ge(f.xT_ready.sem, f.xT_ready.done(2 * i + j))
                        project(pe, i, j)
                    if step == "score":
                        self.score(pe, i, j, n)
                    if step == "turn":
                        self.turn_probs(pe, i, j, n)
                    if step == "weigh":
                        self.weigh(pe, i, j, n)
                    if step == "turn_result":
                        self.turn_result(pe, i, j, n)
                    if step == "out":
                        pe.wait_ge(self.a_taken.sem, self.a_taken.done(self.use_aT(i, j, self.parts - 1)))
                        f.claim_bank(pe, 2 * i + j, j)
                        out_products(pe, i, j).then_inc(f.out_ready.sem, 1)

        @block.scalar
        def _(act):
            if act_before:
                act_before(act)
            with act.Fori(0, B // 2) as i:
                for step, j, n in order:
                    if step == "head":
                        f.copy_turned(act, 2 * i + j, j, act_scale, act_shift)
                    if step == "project":
                        self.operands_free(act, 2 * i + j)
                        take_a(act, i, j)
                    if step == "score":
                        self.exponentiate(act, i, j, n)
                    if step == "turn" and n % 2 == 0:
                        self.copy_probs(act, i, j, n)
                    if step == "turn_result":
                        self.copy_result(act, i, j, n)

        @block.vector
        def _(dve):
            if dve_before:
                dve_before(dve)
            with dve.Fori(0, B // 2) as i:
                for step, j, n in order:
                    if step == "head":
                        f.normalise_in(dve, 2 * i + j, j)
                    if step == "project":
                        self.operands_free(dve, 2 * i + j)
                        take_b(dve, i, j)
                    if step == "score":
                        self.row_max(dve, i, j, n)
                    if step == "turn" and n % 2 == 1:
                        self.copy_probs(dve, i, j, n)
                    if step == "normalise":
                        self.normalise(dve, i, j, n)
                    if step == "out":
                        f.finish(dve, 2 * i + j, j)
                        if f.norm:
                            f.save_normed(dve, 2 * i + j, j)


HEADS, HEAD_DIM, ROWS = 16, 16, 32


def spread_heads(chunks_of=4, per_chunk=4):
    return [(ROWS * r, [(cc, 4 * cc + r) for cc in range(first, first + per_chunk)])
            for r in range(4) for first in range(0, chunks_of, per_chunk)]


def self_attention_stage(core, wq, wk, wv, wo, qkv_bias=None, out_bias=None, causal=False, alibi=None,
                         pre_norm=None, target=None, norm=True, context=None):
    nc, loads, setup = core.nc, core.loads, core.setup
    with ExitStack() as ctx:
        sb = lambda n, s, t=F32: ctx.enter_context(nc.sbuf_tensor(core.named(n), s, t))
        ob = sb("out_bias", [P, D]) if out_bias is not None else None
        f = Frame(core, ctx, pre_norm=pre_norm is not None, out_bias=None if ob is None else ob[:, :], target=target,
                  norm=norm)
        wq_sb, wk_sb = sb("wq", [P, DC, 4, 4, ROWS]), sb("wk", [P, DC, 4, 4, ROWS])
        wv_sb, wo_sb = sb("wv", [P, DC, D]), sb("wo", [P, DC, D])
        mask = sb("mask", [P, P], BF16) if causal else None
        bias_tab = None
        if alibi is not None:
            bias_tab = sb("alibi", [P, 4, 4, P])
            distance, absolute = sb("distance", [P, P]), sb("absolute", [P, P])
        if qkv_bias is not None:
            bq_sb, bk_sb, bv_sb = sb("bq", [P, 4]), sb("bk", [P, 4]), sb("bv", [P, D])
        if pre_norm is not None:
            n_scale, n_shift = sb("norm_scale", [P, DC]), sb("norm_shift", [P, DC])
        kt = 1 if context is None else 2
        chunks = spread_heads(4, 4 // kt)
        at = Attention(core, ctx, f, HEADS, HEAD_DIM, chunks, HEAD_DIM ** -0.5, key_tiles=kt,
                       a_items=1 if context is None else 2, b_items=2,
                       mask=None if mask is None else (lambda b: mask[:, :]), bias=bias_tab)
        if context is not None:
            c_in = sb("c_in", [P, 2, CTX])
            c_pad = sb("c_pad", [P, 2, 4, 4, ROWS])
            c_spread, c_used = core.count("c_spread"), core.count("c_v_copied")
        zeroed, consts, table = core.count("pads_zeroed"), core.count("constants_made"), core.count("table_made")
        pads = 2 if qkv_bias is None else 4
        steps_of_consts = 1 + (2 if causal else 0) + (1 if alibi is not None else 0)
        n_loads = [0]

        def load(sp, dst, src):
            sp.dma_start(dst, src).then_inc(loads.sem, 16)
            n_loads[0] += 16

        def sync(sp):
            sp.wait_ge(zeroed.sem, zeroed.done(pads - 1))
            for c in range(DC):
                for dst, src in ((wq_sb, wq), (wk_sb, wk)):
                    for cc in range(4):
                        load(sp, dst[:, c, cc, :, 0:HEAD_DIM],
                             src[c * P:(c + 1) * P, cc * 64:(cc + 1) * 64].rearrange("p (r d) -> p r d", r=4))
            load(sp, wv_sb[:, :, :], chunked(wv))
            load(sp, wo_sb[:, :, :], chunked(wo))
            if out_bias is not None:
                load(sp, ob[:, :], row_everywhere(out_bias))
            if qkv_bias is not None:
                bq, bk, bv = qkv_bias
                for dst, src in ((bq_sb, bq), (bk_sb, bk)):
                    for r in range(4):
                        load(sp, dst[ROWS * r:ROWS * r + HEAD_DIM, :],
                             src[HEAD_DIM * r:HEAD_DIM * (r + 1), :])
                load(sp, bv_sb[:, :], row_everywhere(bv))
            if pre_norm is not None:
                load(sp, n_scale[:, :], pre_norm[0][:, :])
                load(sp, n_shift[:, :], pre_norm[1][:, :])
            if context is not None:
                with sp.Fori(0, B // 2) as i:
                    for j in range(2):
                        b = 2 * i + j
                        sp.wait_ge(c_used.sem, c_used.freed(b))
                        sp.dma_start(c_in[:, j, :], context[b]).then_inc(c_landed[j].sem, 16)

        total = 16 * (2 * DC * 4 + 2 + (out_bias is not None) + (9 if qkv_bias is not None else 0)
                      + (2 if pre_norm is not None else 0))
        weights = loads.base + total
        if context is not None:
            c_landed = [core.count("c_landed0"), core.count("c_landed1")]

        def pool_before(pool):
            last = pool.memset(at.v[:, :, :, :, HEAD_DIM:], 1.0)
            if context is not None:
                last = pool.memset(c_pad[:, :, :, :, :], 0.0)
            last.then_inc(consts.sem, 1)
            if causal:
                pool.memset(mask[:, :], 0.0).then_inc(consts.sem, 1)
                pool.wait_ge(consts.sem, consts.done(1))
                pool.affine_select(out=mask[:, :], in_=mask[:, :], compare_op=ALU.is_ge, fill=MASKED, base=0,
                                   pattern=[[-1, P]], channel_multiplier=1).then_inc(consts.sem, 1)
            if alibi is not None:
                pool.iota(distance[:, :], pattern=[[-1, P]], base=0, channel_multiplier=1,
                          allow_small_or_imprecise_dtypes=True).then_inc(consts.sem, 1)
            if context is not None:
                pool.wait_ge(consts.sem, consts.done(0))
            if out_bias is not None:
                pool.wait_ge(loads.sem, weights)

        def pool_head(pool, i, j):
            if context is None:
                return
            b = 2 * i + j
            cl = c_landed[j]
            pool.wait_ge(cl.sem, cl.base + 16 * (i + 1))
            pool.wait_ge(at.a_made.sem, at.a_made.done(at.use_a(i - 1, j, 0)))
            pool.sem_inc(f.passed.sem, 1)
            pool.tensor_copy(c_pad[:, j, :, :, 0:HEAD_DIM],
                             c_in[:, j, 0:D].rearrange("p (c r d) -> p c r d", c=4, r=4)
                             ).then_inc(c_spread.sem, 1)
            at.operands_free(pool, b)
            pool.sem_inc(f.passed.sem, 1)
            pool.tensor_copy(at.v[:, j, 0, :, 0:HEAD_DIM],
                             c_in[:, j, D:CTX].rearrange("p (h d) -> p h d", h=HEADS)
                             ).then_inc(c_used.sem, 1)

        def dve_before(dve):
            dve.memset(wq_sb[:, :, :, :, :], 0.0).then_inc(zeroed.sem, 1)
            dve.memset(wk_sb[:, :, :, :, :], 0.0).then_inc(zeroed.sem, 1)
            if qkv_bias is not None:
                dve.memset(bq_sb[:, :], 0.0).then_inc(zeroed.sem, 1)
                dve.memset(bk_sb[:, :], 0.0).then_inc(zeroed.sem, 1)
            if alibi is not None:
                dve.wait_ge(consts.sem, consts.done(1))
                dve.scalar_tensor_tensor(out=absolute[:, :], in0=distance[:, :], scalar=-1.0, in1=distance[:, :],
                                         op0=ALU.mult, op1=ALU.max).then_inc(table.sem, 1)
                dve.wait_ge(table.sem, table.done(0))
                for r in range(4):
                    for cc in range(4):
                        slope = float(np.float32(2.0 ** (-8.0 * (4 * cc + r) / HEADS)))
                        last = dve.tensor_scalar(bias_tab[:, r, cc, :], absolute[:, :], -slope, None, ALU.mult)
                last.then_inc(table.sem, 1)
                dve.wait_ge(table.sem, table.done(1))
            dve.wait_ge(loads.sem, weights)

        def act_before(act):
            act.wait_ge(loads.sem, weights)

        def pe_before(pe):
            pe.wait_ge(loads.sem, weights)
            pe.wait_ge(consts.sem, consts.done(steps_of_consts - 1))

        def project(pe, i, j):
            b = 2 * i + j
            xT = f.xT[:, j]
            if context is not None:
                pe.wait_ge(c_spread.sem, c_spread.done(b))
                pe.wait_ge(c_used.sem, c_used.done(b))
                at.claim_a(pe, at.use_a(i, j, 0))
                flat = c_pad[:, j].rearrange("p c r d -> p c (r d)")
                for cc in range(4):
                    last = pe.transpose(at.bank_a[:, cc, :], flat[:, cc, :], core.ident[:, :])
                last.then_inc(at.a_made.sem, 1)
            at.claim_b(pe, at.use_b(i, j, 0))
            for cc in range(4):
                for c in range(DC):
                    last = pe.matmul(at.bank_b[:, cc, :], wk_sb[:, c, cc].rearrange("p r d -> p (r d)"), xT[:, c, :],
                                     start=(c == 0), stop=(c == DC - 1))
            last.then_inc(at.b_made.sem, 1)
            at.claim_a(pe, at.use_a(i, j, at.NA - 1))
            for cc in range(4):
                for c in range(DC):
                    last = pe.matmul(at.bank_a[:, cc, :], wq_sb[:, c, cc].rearrange("p r d -> p (r d)"), xT[:, c, :],
                                     start=(c == 0), stop=(c == DC - 1))
            last.then_inc(at.a_made.sem, 1)
            at.claim_b(pe, at.use_b(i, j, 1))
            v_ps = at.bank_b[:, 0:2, :].rearrange("p a b -> p (a b)")
            for c in range(DC):
                last = pe.matmul(v_ps, xT[:, c, :], wv_sb[:, c, :], start=(c == 0), stop=(c == DC - 1))
            last.then_inc(at.b_made.sem, 1)

        def take_a(act, i, j):
            if context is not None:
                act.wait_ge(at.a_made.sem, at.a_made.done(at.use_a(i, j, 0)))
                act.activation(at.kT[:, j, :, 0:P], at.bank_a[:, :, :], ACT.Copy).then_inc(at.a_taken.sem, 1)
            act.wait_ge(at.a_made.sem, at.a_made.done(at.use_a(i, j, at.NA - 1)))
            if qkv_bias is None:
                last = act.activation(at.qT[:, j], at.bank_a[:, :, :], ACT.Copy)
            else:
                for cc in range(4):
                    last = act.activation(at.qT[:, j, cc, :], at.bank_a[:, cc, :], ACT.Identity,
                                          bias=bq_sb[:, cc:cc + 1])
            last.then_inc(at.a_taken.sem, 1)

        def take_b(dve, i, j):
            dve.wait_ge(at.b_made.sem, at.b_made.done(at.use_b(i, j, 0)))
            out = at.kT[:, j, :, (kt - 1) * P:kt * P]
            if qkv_bias is None:
                last = dve.tensor_copy(out, at.bank_b[:, :, :])
            else:
                last = dve.tensor_tensor(out, at.bank_b[:, :, :],
                                         bk_sb[:, :].unsqueeze(2).broadcast_to([P, 4, P]), ALU.add)
            last.then_inc(at.b_taken.sem, 1)
            dve.wait_ge(at.b_made.sem, at.b_made.done(at.use_b(i, j, 1)))
            out = at.v[:, j, kt - 1, :, 0:HEAD_DIM]
            v_ps = at.bank_b[:, 0:2, :].rearrange("p a (h d) -> p (a h) d", d=HEAD_DIM)
            if qkv_bias is None:
                last = dve.tensor_copy(out, v_ps)
            else:
                last = dve.tensor_tensor(out, v_ps, bv_sb[:, :].rearrange("p (h d) -> p h d", h=HEADS), ALU.add)
            last.then_inc(at.b_taken.sem, 1)

        def out_products(pe, i, j):
            for c in range(DC):
                last = pe.matmul(f.out_ps, at.aT[:, j, c, :], wo_sb[:, c, :], start=(c == 0), stop=(c == DC - 1))
            return last

        with nc.Block() as block:
            at.run(block, project, take_a, take_b, out_products, sync=sync, pool_before=pool_before,
                   pool_head=pool_head, pe_before=pe_before, act_before=act_before, dve_before=dve_before,
                   act_scale=None if pre_norm is None else n_scale,
                   act_shift=None if pre_norm is None else n_shift)
        assert n_loads[0] == total
        loads.advance(total)
        zeroed.advance(pads)
        consts.advance(steps_of_consts)
        if alibi is not None:
            table.advance(2)
        if context is not None:
            for c in (c_spread, c_used):
                c.advance(B)
            for c in c_landed:
                c.advance(16 * B // 2)
        at.end()



class ContextFeed:

    def __init__(self, core, ctx, at, context):
        nc = core.nc
        self.core, self.at, self.context = core, at, context
        self.c_in = ctx.enter_context(nc.sbuf_tensor(core.named("c_in"), [P, 2, CTX], F32))
        self.cT = ctx.enter_context(nc.sbuf_tensor(core.named("cT"), [P, 2, CC, P], F32))
        self.landed = [core.count("c_landed0"), core.count("c_landed1")]

    def end(self):
        for c in self.landed:
            c.advance(16 * B // 2)

    def load(self, sp):
        at = self.at
        with sp.Fori(0, B // 2) as i:
            for j in range(2):
                sp.wait_ge(at.a_made.sem, at.a_made.done(at.use_a(i - 1, j, 0)))
                sp.dma_start(self.c_in[:, j, :], self.context[2 * i + j]).then_inc(self.landed[j].sem, 16)

    def turn(self, pe, i, j):
        at = self.at
        landed = self.landed[j]
        pe.wait_ge(landed.sem, landed.base + 16 * (i + 1))
        at.claim_a(pe, at.use_a(i, j, 0))
        for c in range(CC):
            last = pe.transpose(at.bank_a[:, c, :], self.c_in[:, j, c * P:(c + 1) * P], self.core.ident[:, :])
        last.then_inc(at.a_made.sem, 1)

    def take(self, act, i, j):
        at = self.at
        act.wait_ge(at.a_made.sem, at.a_made.done(at.use_a(i, j, 0)))
        act.activation(self.cT[:, j], at.bank_a[:, :, :], ACT.Copy).then_inc(at.a_taken.sem, 1)


def masked_context_stage(core, context, mask, mask_cols, w_src, b_src_k, b_src_v, w_tgt, b_tgt, w_out, b_out):
    nc, loads = core.nc, core.loads
    HEADS8, HD = 8, 32
    with ExitStack() as ctx:
        sb = lambda n, s, t=F32: ctx.enter_context(nc.sbuf_tensor(core.named(n), s, t))
        ob = sb("out_bias", [P, D])
        f = Frame(core, ctx, out_bias=ob[:, :])
        ws, wt, wo = sb("w_src", [P, CC, CTX]), sb("w_tgt", [P, DC, D]), sb("w_out", [P, CC, D])
        bk, bt, bv = sb("b_k", [P, DC]), sb("b_t", [P, DC]), sb("b_v", [P, D])
        mrow, mcol = sb("mask_row", [P, B, P]), sb("mask_col", [P, B, 1])
        left_out = sb("left_out", [P, B, P], BF16)
        chunks = [(32 * r, [(cc, 4 * cc + r) for cc in range(2)]) for r in range(4)]
        at = Attention(core, ctx, f, HEADS8, HD, chunks, HD ** -0.5, a_items=1, b_items=3, q_chunks=2,
                       mask=lambda b: left_out[:, b, :])
        feed = ContextFeed(core, ctx, at, context)
        consts, v_raw = core.count("constants_made"), core.count("v_raw")
        plain = ((ws[:, :, :], chunked(w_src)), (wt[:, :, :], chunked(w_tgt)), (wo[:, :, :], chunked(w_out)),
                 (bk[:, :], b_src_k[:, :]), (bt[:, :], b_tgt[:, :]), (bv[:, :], row_everywhere(b_src_v)),
                 (ob[:, :], row_everywhere(b_out)), (mcol[:, :, 0], mask_cols[:, :]),
                 (mrow[:, :, :], mask.rearrange("(o b) t -> o b t", o=1).broadcast_to([P, B, P])))
        weights = loads.base + 16 * len(plain)

        def sync(sp):
            for dst, src in plain:
                sp.dma_start(dst, src).then_inc(loads.sem, 16)
            feed.load(sp)

        def pool_before(pool):
            pool.memset(at.v[:, :, :, :, HD:], 1.0).then_inc(consts.sem, 1)
            pool.wait_ge(loads.sem, weights)

        def dve_before(dve):
            dve.wait_ge(loads.sem, weights)
            dve.tensor_scalar(left_out[:, :, :], mrow[:, :, :], 0.0, MASKED, ALU.is_equal, ALU.mult
                              ).then_inc(v_raw.sem, 1)

        def pe_before(pe):
            pe.wait_ge(loads.sem, weights)
            pe.wait_ge(consts.sem, consts.done(0))
            pe.wait_ge(v_raw.sem, v_raw.done(0))

        def project(pe, i, j):
            xT, cT = f.xT[:, j], feed.cT[:, j]
            feed.turn(pe, i, j)
            at.claim_b(pe, at.use_b(i, j, 0))
            for m in range(DC):
                for c in range(DC):
                    last = pe.matmul(at.bank_b[:, m, :], wt[:, c, m * P:(m + 1) * P], xT[:, c, :],
                                     start=(c == 0), stop=(c == DC - 1))
            last.then_inc(at.b_made.sem, 1)
            pe.wait_ge(at.a_taken.sem, at.a_taken.done(at.use_a(i, j, 0)))
            at.claim_b(pe, at.use_b(i, j, 1))
            for m in range(DC):
                for c in range(CC):
                    last = pe.matmul(at.bank_b[:, m, :], ws[:, c, m * P:(m + 1) * P], cT[:, c, :],
                                     start=(c == 0), stop=(c == CC - 1))
            last.then_inc(at.b_made.sem, 1)
            at.claim_b(pe, at.use_b(i, j, 2))
            v_ps = at.bank_b[:, 0:2, :].rearrange("p a b -> p (a b)")
            for c in range(CC):
                last = pe.matmul(v_ps, cT[:, c, :], ws[:, c, D:CTX], start=(c == 0), stop=(c == CC - 1))
            last.then_inc(at.b_made.sem, 1)

        def take_a(act, i, j):
            feed.take(act, i, j)

        def take_b(dve, i, j):
            b = 2 * i + j
            for use, dst, bias in ((0, at.qT, bt), (1, at.kT, bk)):
                dve.wait_ge(at.b_made.sem, at.b_made.done(at.use_b(i, j, use)))
                for m in range(DC):
                    last = dve.scalar_tensor_tensor(out=dst[:, j, m, :], in0=at.bank_b[:, m, :],
                                                    scalar=bias[:, m:m + 1], in1=mrow[:, b, :],
                                                    op0=ALU.add, op1=ALU.mult)
                last.then_inc(at.b_taken.sem, 1)
            dve.wait_ge(at.b_made.sem, at.b_made.done(at.use_b(i, j, 2)))
            v = at.v[:, j, 0, :, 0:HD]
            dve.tensor_tensor(v, at.bank_b[:, 0:2, :].rearrange("p a (h d) -> p (a h) d", d=HD),
                              bv[:, :].rearrange("p (h d) -> p h d", d=HD), ALU.add).then_inc(v_raw.sem, 1)
            dve.wait_ge(v_raw.sem, v_raw.done(1 + b))
            dve.tensor_scalar(v, v, mcol[:, b, :], None, ALU.mult).then_inc(at.b_taken.sem, 1)

        def out_products(pe, i, j):
            for c in range(CC):
                lhs = f.xT[:, j, c, :] if c < DC else at.aT[:, j, c - DC, :]
                last = pe.matmul(f.out_ps, lhs, wo[:, c, :], start=(c == 0), stop=(c == CC - 1))
            return last

        with nc.Block() as block:
            at.run(block, project, take_a, take_b, out_products, sync=sync, pool_before=pool_before,
                   pe_before=pe_before, dve_before=dve_before)
        loads.advance(16 * len(plain))
        consts.advance(1)
        v_raw.advance(1 + B)
        feed.end()
        at.end()


def wide_context_stage(core, context, wq, wkv, null_kv, wo, ln_scale, ln_bias):
    nc, loads = core.nc, core.loads
    HEADS64, HD = 16, 64
    INNER = HEADS64 * HD
    IC = INNER // P
    with ExitStack() as ctx:
        sb = lambda n, s, t=F32: ctx.enter_context(nc.sbuf_tensor(core.named(n), s, t))
        ob, ls = sb("ln_bias", [P, D]), sb("ln_scale", [P, D])
        f = Frame(core, ctx, out_bias=ob[:, :], inner_norm=ls[:, :])
        wq_sb, wkv_sb, wo_sb = sb("wq", [P, DC, INNER]), sb("wkv", [P, CC, 2 * INNER]), sb("wo", [P, IC, D])
        null_k, null_v = sb("null_k", [P, 2]), sb("null_v_row", [P, HD])
        chunks = [(64 * r, [(cc, 2 * cc + r) for cc in range(first, first + 4)]) for first in (0, 4) for r in range(2)]
        at = Attention(core, ctx, f, HEADS64, HD, chunks, HD ** -0.5, a_items=5, b_items=3, q_chunks=IC, parts=2,
                       null=null_v[:, :])
        feed = ContextFeed(core, ctx, at, context)
        consts = core.count("constants_made")
        plain = ((wq_sb[:, :, :], chunked(wq)), (wkv_sb[:, :, :], chunked(wkv)), (wo_sb[:, :, :], chunked(wo)),
                 (null_v[:, :], null_kv[1:2, :].broadcast_to([P, HD])),
                 (null_k[0:HD, 0:1], null_kv[0:1, :].rearrange("o d -> d o")),
                 (null_k[HD:P, 1:2], null_kv[0:1, :].rearrange("o d -> d o")),
                 (ob[:, :], row_everywhere(ln_bias)), (ls[:, :], row_everywhere(ln_scale)))
        weights = loads.base + 16 * len(plain)

        def sync(sp):
            sp.wait_ge(consts.sem, consts.done(1))
            with nc.allow_non_contiguous_dma(reason="64 values of the null key, once"):
                for dst, src in plain:
                    sp.dma_start(dst, src).then_inc(loads.sem, 16)
            feed.load(sp)

        def pool_before(pool):
            pool.memset(f.inner_eps[:, :], 1e-6).then_inc(consts.sem, 1)
            pool.memset(null_k[:, :], 0.0).then_inc(consts.sem, 1)
            pool.wait_ge(consts.sem, consts.done(1))
            pool.wait_ge(loads.sem, weights)

        def dve_before(dve):
            dve.wait_ge(loads.sem, weights)

        def pe_before(pe):
            pe.wait_ge(loads.sem, weights)

        def project(pe, i, j):
            xT, cT = f.xT[:, j], feed.cT[:, j]
            feed.turn(pe, i, j)

            def columns_of(bank, w, first, src, chunks_in, made):
                for m in range(4):
                    col = first + m * P
                    for c in range(chunks_in):
                        last = pe.matmul(bank[:, m, :], w[:, c, col:col + P], src[:, c, :],
                                         start=(c == 0), stop=(c == chunks_in - 1))
                last.then_inc(made.sem, 1)

            def values_of(bank, first, made):
                out = bank[:, :, :].rearrange("p a b -> p (a b)")
                for c in range(CC):
                    last = pe.matmul(out, cT[:, c, :], wkv_sb[:, c, INNER + first:INNER + first + 4 * P],
                                     start=(c == 0), stop=(c == CC - 1))
                last.then_inc(made.sem, 1)

            at.claim_b(pe, at.use_b(i, j, 0))
            columns_of(at.bank_b, wq_sb, INNER // 2, xT, DC, at.b_made)
            at.claim_a(pe, at.use_a(i, j, 1))
            columns_of(at.bank_a, wq_sb, 0, xT, DC, at.a_made)
            at.claim_b(pe, at.use_b(i, j, 1))
            columns_of(at.bank_b, wkv_sb, INNER // 2, cT, CC, at.b_made)
            at.claim_a(pe, at.use_a(i, j, 2))
            columns_of(at.bank_a, wkv_sb, 0, cT, CC, at.a_made)
            at.claim_b(pe, at.use_b(i, j, 2))
            values_of(at.bank_b, INNER // 2, at.b_made)
            at.claim_a(pe, at.use_a(i, j, 3))
            values_of(at.bank_a, 0, at.a_made)
            at.claim_a(pe, at.use_a(i, j, 4))
            for cc in range(IC):
                last = pe.matmul(at.bank_a[:, 0, 2 * cc:2 * cc + 2], at.qT[:, j, cc, :], null_k[:, :],
                                 start=True, stop=True)
            last.then_inc(at.a_made.sem, 1)

        def take_a(act, i, j):
            feed.take(act, i, j)
            for use, out in ((1, at.qT[:, j, 0:4, :]), (2, at.kT[:, j, 0:4, :]), (3, at.v[:, j, 0, 0:8, :]),
                             (4, at.snull[:, j, :])):
                act.wait_ge(at.a_made.sem, at.a_made.done(at.use_a(i, j, use)))
                src = at.bank_a[:, :, :]
                if use == 3:
                    src = src.rearrange("p a (h d) -> p (a h) d", d=HD)
                if use == 4:
                    src = at.bank_a[:, 0, 0:HEADS64]
                act.activation(out, src, ACT.Copy).then_inc(at.a_taken.sem, 1)

        def take_b(dve, i, j):
            for use, out in ((0, at.qT[:, j, 4:8, :]), (1, at.kT[:, j, 4:8, :]), (2, at.v[:, j, 0, 8:16, :])):
                dve.wait_ge(at.b_made.sem, at.b_made.done(at.use_b(i, j, use)))
                src = at.bank_b[:, :, :]
                if use == 2:
                    src = src.rearrange("p a (h d) -> p (a h) d", d=HD)
                dve.tensor_copy(out, src).then_inc(at.b_taken.sem, 1)
            dve.wait_ge(at.a_taken.sem, at.a_taken.done(at.use_a(i, j, 4)))

        def out_products(pe, i, j):
            for c in range(IC):
                last = pe.matmul(f.out_ps, at.aT[:, j, c, :], wo_sb[:, c, :], start=(c == 0), stop=(c == IC - 1))
            return last

        with nc.Block() as block:
            at.run(block, project, take_a, take_b, out_products, sync=sync, pool_before=pool_before,
                   pe_before=pe_before, dve_before=dve_before)
        loads.advance(16 * len(plain))
        consts.advance(2)
        feed.end()
        at.end()



def linear_attention_stage(core, wq, wk, wv, wo, bo):
    nc, loads = core.nc, core.loads
    H, HD = 8, 64
    INNER = H * HD
    IC = INNER // P
    with ExitStack() as ctx:
        sb = lambda n, s, t=F32: ctx.enter_context(nc.sbuf_tensor(core.named(n), s, t))
        ps = lambda n: ctx.enter_context(nc.psum_tensor(core.named(n), [P, IC, P], F32))
        ob = sb("out_bias", [P, D])
        f = Frame(core, ctx, out_bias=ob[:, :])
        wq_sb, wk_sb, wv_sb, wo_sb = (sb("wq", [P, DC, INNER]), sb("wk", [P, DC, INNER]), sb("wv", [P, DC, INNER]),
                                      sb("wo", [P, IC, D]))
        q_max, q_sum, q_inv = sb("q_max", [P, 2, H]), sb("q_sum", [P, 2, H]), sb("q_inv", [P, 2, H])
        q_low, q_exp, q = sb("q_low", [P, 2, H, HD]), sb("q_exp", [P, 2, H, HD]), sb("q", [P, 2, H, HD])
        k_max, k_neg, k_sum, k_inv = (sb("k_max", [P, 2, IC]), sb("k_neg", [P, 2, IC]), sb("k_sum", [P, 2, IC]),
                                      sb("k_inv", [P, 2, IC]))
        k_exp = sb("k_exp", [P, 2, IC, P])
        v = sb("v", [P, 2, IC, P])
        qT, k_tok = sb("qT", [P, 2, IC, P]), sb("k_tok", [P, 2, IC, P])
        blocks = sb("blocks", [P, 2, IC, P])
        aT = sb("aT", [P, 2, IC, P])
        q_ps, k_ps, v_ps, qT_ps, kt_ps, c_ps, a_ps = (ps(n) for n in ("q_ps", "k_ps", "v_ps", "qT_ps", "kt_ps",
                                                                     "c_ps", "a_ps"))
        c = core.count
        (q_made, k_made, v_made, q_maxed, q_lowered, q_exped, q_summed, q_inverted, q_ready, q_turned, qT_ready,
         k_maxed, k_negated, k_exped, k_inverted, k_turned, k_ready, v_ready, c_made, blocks_ready, a_made,
         aT_ready) = names = (
            c("q_made"), c("k_made"), c("v_made"), c("q_maxed"), c("q_lowered"), c("q_exped"), c("q_summed"),
            c("q_inverted"), c("q_ready"), c("q_turned"), c("qT_ready"), c("k_maxed"), c("k_negated"),
            c("k_exped"), c("k_inverted"), c("k_turned"), c("k_ready"), c("v_ready"), c("c_made"),
            c("blocks_ready"), c("a_made"), c("aT_ready"))
        consts = core.count("constants_made")
        plain = ((wq_sb[:, :, :], chunked(wq)), (wk_sb[:, :, :], chunked(wk)), (wv_sb[:, :, :], chunked(wv)),
                 (wo_sb[:, :, :], chunked(wo)), (ob[:, :], row_everywhere(bo)))
        weights = loads.base + 16 * len(plain)
        with nc.Block() as block:
            @block.sync
            def _(sp):
                for dst, src in plain:
                    sp.dma_start(dst, src).then_inc(loads.sem, 16)

            @block.gpsimd
            def _(pool):
                pool.memset(blocks[:, :, :, :], 0.0).then_inc(consts.sem, 1)
                pool.wait_ge(loads.sem, weights)
                with pool.Fori(0, B // 2) as i:
                    for j in range(2):
                        f.fetch(pool, 2 * i + j, j)
                    for j in range(2):
                        f.rstd_out(pool, 2 * i + j, j)

            @block.tensor
            def _(pe):
                pe.wait_ge(loads.sem, weights)
                with pe.Fori(0, B // 2) as i:
                    for j in range(2):
                        f.turn(pe, 2 * i + j, j)
                    for j in range(2):
                        b = 2 * i + j
                        xT = f.xT[:, j]
                        pe.wait_ge(f.xT_ready.sem, f.xT_ready.done(b))
                        pe.wait_ge(k_exped.sem, k_exped.freed(b, 1))
                        for m in range(IC):
                            for cc in range(DC):
                                last = pe.matmul(k_ps[:, m, :], wk_sb[:, cc, m * P:(m + 1) * P], xT[:, cc, :],
                                                 start=(cc == 0), stop=(cc == DC - 1))
                        last.then_inc(k_made.sem, 1)
                        pe.wait_ge(q_lowered.sem, q_lowered.freed(b, 1))
                        for cc in range(DC):
                            last = pe.matmul(q_ps[:, :, :].rearrange("p a b -> p (a b)"), xT[:, cc, :], wq_sb[:, cc, :],
                                             start=(cc == 0), stop=(cc == DC - 1))
                        last.then_inc(q_made.sem, 1)
                        pe.wait_ge(v_ready.sem, v_ready.freed(b, 1))
                        for cc in range(DC):
                            last = pe.matmul(v_ps[:, :, :].rearrange("p a b -> p (a b)"), xT[:, cc, :], wv_sb[:, cc, :],
                                             start=(cc == 0), stop=(cc == DC - 1))
                        last.then_inc(v_made.sem, 1)
                    for j in range(2):
                        b = 2 * i + j
                        pe.wait_ge(k_exped.sem, k_exped.done(b))
                        pe.wait_ge(k_ready.sem, k_ready.freed(b, 1))
                        for m in range(IC):
                            last = pe.transpose(kt_ps[:, m, :], k_exp[:, j, m, :], core.ident[:, :])
                        last.then_inc(k_turned.sem, 1)
                        pe.wait_ge(q_ready.sem, q_ready.done(b))
                        pe.wait_ge(qT_ready.sem, qT_ready.freed(b, 1))
                        for m in range(IC):
                            last = pe.transpose(qT_ps[:, m, :],
                                                q[:, j, 2 * m:2 * m + 2, :].rearrange("p h d -> p (h d)"),
                                                core.ident[:, :])
                        last.then_inc(q_turned.sem, 1)
                    for j in range(2):
                        b = 2 * i + j
                        pe.wait_ge(k_ready.sem, k_ready.done(b))
                        pe.wait_ge(v_ready.sem, v_ready.done(b))
                        pe.wait_ge(blocks_ready.sem, blocks_ready.freed(b, 1))
                        for m in range(IC):
                            last = pe.matmul(c_ps[:, m, :], k_tok[:, j, m, :], v[:, j, m, :], start=True, stop=True)
                        last.then_inc(c_made.sem, 1)
                    for j in range(2):
                        b = 2 * i + j
                        pe.wait_ge(blocks_ready.sem, blocks_ready.done(b))
                        pe.wait_ge(qT_ready.sem, qT_ready.done(b))
                        pe.wait_ge(aT_ready.sem, aT_ready.freed(b, 1))
                        for m in range(IC):
                            last = pe.matmul(a_ps[:, m, :], blocks[:, j, m, :], qT[:, j, m, :], start=True, stop=True)
                        last.then_inc(a_made.sem, 1)
                    for j in range(2):
                        b = 2 * i + j
                        pe.wait_ge(aT_ready.sem, aT_ready.done(b))
                        f.claim_bank(pe, b, j)
                        for m in range(IC):
                            last = pe.matmul(f.out_ps, aT[:, j, m, :], wo_sb[:, m, :], start=(m == 0), stop=(m == IC - 1))
                        last.then_inc(f.out_ready.sem, 1)

            @block.scalar
            def _(act):
                with act.Fori(0, B // 2) as i:
                    for j in range(2):
                        f.copy_turned(act, 2 * i + j, j)
                    for j in range(2):
                        b = 2 * i + j
                        act.wait_ge(k_negated.sem, k_negated.done(b))
                        act.wait_ge(k_turned.sem, k_turned.freed(b))
                        for m in range(IC):
                            last = act.activation(k_exp[:, j, m, :], k_ps[:, m, :], ACT.Exp,
                                                  bias=k_neg[:, j, m:m + 1], accum_out=k_sum[:, j, m:m + 1])
                        last.then_inc(k_exped.sem, 1)
                        act.wait_ge(q_lowered.sem, q_lowered.done(b))
                        act.wait_ge(q_ready.sem, q_ready.freed(b))
                        act.activation(q_exp[:, j], q_low[:, j], ACT.Exp).then_inc(q_exped.sem, 1)
                        act.wait_ge(v_made.sem, v_made.done(b))
                        act.wait_ge(c_made.sem, c_made.freed(b))
                        act.activation(v[:, j], v_ps[:, :, :], ACT.Copy).then_inc(v_ready.sem, 1)
                    for j in range(2):
                        b = 2 * i + j
                        act.wait_ge(k_turned.sem, k_turned.done(b))
                        act.wait_ge(c_made.sem, c_made.freed(b))
                        act.activation(k_tok[:, j], kt_ps[:, :, :], ACT.Copy).then_inc(k_ready.sem, 1)
                        act.wait_ge(q_turned.sem, q_turned.done(b))
                        act.wait_ge(a_made.sem, a_made.freed(b))
                        act.activation(qT[:, j], qT_ps[:, :, :], ACT.Copy).then_inc(qT_ready.sem, 1)
                    for j in range(2):
                        b = 2 * i + j
                        act.wait_ge(a_made.sem, a_made.done(b))
                        act.wait_ge(f.out_ready.sem, f.out_ready.freed(b))
                        act.activation(aT[:, j], a_ps[:, :, :], ACT.Copy).then_inc(aT_ready.sem, 1)

            @block.vector
            def _(dve):
                dve.wait_ge(consts.sem, consts.done(0))
                with dve.Fori(0, B // 2) as i:
                    for j in range(2):
                        b = 2 * i + j
                        q_bank = q_ps[:, :, :].rearrange("p a (h d) -> p (a h) d", d=HD)
                        dve.wait_ge(k_made.sem, k_made.done(b))
                        dve.tensor_reduce(k_max[:, j, :], k_ps[:, :, :], AX.X, ALU.max).then_inc(k_maxed.sem, 1)
                        dve.wait_ge(k_maxed.sem, k_maxed.done(b))
                        dve.wait_ge(k_exped.sem, k_exped.freed(b))
                        dve.tensor_scalar(k_neg[:, j, :], k_max[:, j, :], -1.0, None, ALU.mult
                                          ).then_inc(k_negated.sem, 1)
                        dve.wait_ge(q_made.sem, q_made.done(b))
                        dve.tensor_reduce(q_max[:, j, :], q_bank, AX.X, ALU.max).then_inc(q_maxed.sem, 1)
                        dve.wait_ge(q_maxed.sem, q_maxed.done(b))
                        dve.wait_ge(q_exped.sem, q_exped.freed(b))
                        dve.tensor_tensor(q_low[:, j], q_bank, q_max[:, j, :].unsqueeze(2).broadcast_to([P, H, HD]),
                                          ALU.subtract).then_inc(q_lowered.sem, 1)
                    for j in range(2):
                        b = 2 * i + j
                        dve.wait_ge(q_exped.sem, q_exped.done(b))
                        dve.tensor_reduce(q_sum[:, j, :], q_exp[:, j], AX.X, ALU.add).then_inc(q_summed.sem, 1)
                        dve.wait_ge(q_summed.sem, q_summed.done(b))
                        dve.reciprocal(q_inv[:, j, :], q_sum[:, j, :]).then_inc(q_inverted.sem, 1)
                        dve.wait_ge(q_inverted.sem, q_inverted.done(b))
                        dve.wait_ge(q_turned.sem, q_turned.freed(b))
                        dve.tensor_tensor(q[:, j], q_exp[:, j], q_inv[:, j, :].unsqueeze(2).broadcast_to([P, H, HD]),
                                          ALU.mult).then_inc(q_ready.sem, 1)
                        dve.wait_ge(k_exped.sem, k_exped.done(b))
                        dve.reciprocal(k_inv[:, j, :], k_sum[:, j, :]).then_inc(k_inverted.sem, 1)
                    for j in range(2):
                        b = 2 * i + j
                        dve.wait_ge(c_made.sem, c_made.done(b))
                        dve.wait_ge(k_inverted.sem, k_inverted.done(b))
                        dve.wait_ge(a_made.sem, a_made.freed(b))
                        for r in range(2):
                            rows = slice(HD * r, HD * (r + 1))
                            for m in range(IC):
                                last = dve.tensor_scalar(blocks[rows, j, m, rows], c_ps[rows, m, rows],
                                                         k_inv[rows, j, m:m + 1], HD ** -0.5, ALU.mult, ALU.mult)
                        last.then_inc(blocks_ready.sem, 1)
                    for j in range(2):
                        f.finish(dve, 2 * i + j, j)
                    for j in range(2):
                        f.save_normed(dve, 2 * i + j, j)
        for n in names:
            n.advance(B)
        loads.advance(16 * len(plain))
        consts.advance(1)
        f.end()



def gate_stage(core, hT_all, weight_all, gate_w, experts, top, norm_scale=None, norm_shift=None, x_from=None):
    nc, loads = core.nc, core.loads
    pre = norm_scale is not None
    E = experts
    with ExitStack() as ctx:
        sb = lambda n, s, t=F32: ctx.enter_context(nc.sbuf_tensor(core.named(n), s, t))
        f = Frame(core, ctx, pre_norm=pre, feeds_only=True)
        src_x = core.x if x_from is None else x_from
        gw = sb("gate_w", [P, DC, E])
        if pre:
            ns, nh = sb("norm_scale", [P, DC]), sb("norm_shift", [P, DC])
        number = sb("expert_number", [P, E])
        s_sb, best, which, which_f = (sb("scores", [P, 2, E]), sb("best", [P, 2, 8]), sb("which", [P, 2, 8], U32),
                                      sb("which_f", [P, 2, 2]))
        low, ex, tot, inv = (sb("low", [P, 2, E]), sb("ex", [P, 2, E]), sb("tot", [P, 2, 1]), sb("inv", [P, 2, 1]))
        pick = sb("pick", [P, 2, 2, E])
        g_ps = ctx.enter_context(nc.psum_tensor(core.named("g_ps"), [P, 512], F32))
        c = core.count
        names = (g_made, s_ready, best_found, which_found, which_cast, lowered, exped, picked, picked2, summed,
                 inverted, weighted) = (
            c("g_made"), c("s_ready"), c("best_found"), c("which_found"), c("which_cast"), c("lowered"),
            c("exped"), c("picked"), c("picked2"), c("summed"), c("inverted"), c("weighted"))
        chosen, kept = c("chosen"), c("hT_kept")
        names = names + (kept,) + ((chosen,) if top == 2 else ())
        consts = core.count("constants_made")
        plain = [(gw[:, :, :], chunked(gate_w))]
        if pre:
            plain += [(ns[:, :], norm_scale[:, :]), (nh[:, :], norm_shift[:, :])]
        weights = loads.base + 16 * len(plain)
        with nc.Block() as block:
            @block.sync
            def _(sp):
                for dst, src in plain:
                    sp.dma_start(dst, src).then_inc(loads.sem, 16)

            @block.gpsimd
            def _(pool):
                pool.iota(number[:, :], pattern=[[1, E]], base=0, channel_multiplier=0,
                          allow_small_or_imprecise_dtypes=True).then_inc(consts.sem, 1)
                with pool.Fori(0, B // 2) as i:
                    for j in range(2):
                        f.fetch(pool, 2 * i + j, j, src_x)

            @block.tensor
            def _(pe):
                pe.wait_ge(loads.sem, weights)
                with pe.Fori(0, B // 2) as i:
                    for j in range(2):
                        f.turn(pe, 2 * i + j, j)
                    for j in range(2):
                        b = 2 * i + j
                        pe.wait_ge(f.xT_ready.sem, f.xT_ready.done(b))
                        pe.wait_ge(s_ready.sem, s_ready.freed(b, 1))
                        for cc in range(DC):
                            last = pe.matmul(g_ps[:, 0:E], f.xT[:, j, cc, :], gw[:, cc, :],
                                             start=(cc == 0), stop=(cc == DC - 1))
                        last.then_inc(g_made.sem, 1)

            @block.scalar
            def _(act):
                act.wait_ge(loads.sem, weights)
                with act.Fori(0, B // 2) as i:
                    for j in range(2):
                        b = 2 * i + j
                        act.wait_ge(g_made.sem, g_made.freed(b))
                        f.copy_turned(act, b, j, ns if pre else None, nh if pre else None)
                        act.wait_ge(f.xT_ready.sem, f.xT_ready.done(b))
                        act.activation(hT_all[:, :, b, :], f.xT[:, j], ACT.Copy).then_inc(kept.sem, 1)
                    for j in range(2):
                        b = 2 * i + j
                        act.wait_ge(lowered.sem, lowered.done(b))
                        act.wait_ge(weighted.sem, weighted.freed(b))
                        act.activation(ex[:, j, :], low[:, j, :], ACT.Exp).then_inc(exped.sem, 1)

            @block.vector
            def _(dve):
                dve.wait_ge(consts.sem, consts.done(0))
                with dve.Fori(0, B // 2) as i:
                    for j in range(2):
                        f.normalise_in(dve, 2 * i + j, j)
                    for j in range(2):
                        b = 2 * i + j
                        dve.wait_ge(g_made.sem, g_made.done(b))
                        dve.tensor_copy(s_sb[:, j, :], g_ps[:, 0:E]).then_inc(s_ready.sem, 1)
                        dve.wait_ge(s_ready.sem, s_ready.done(b))
                        dve.sem_inc(f.passed.sem, 1)
                        dve.max(best[:, j, :], s_sb[:, j, :]).then_inc(best_found.sem, 1)
                        dve.wait_ge(best_found.sem, best_found.done(b))
                        dve.sem_inc(f.passed.sem, 1)
                        dve.max_index(which[:, j, :], best[:, j, :], s_sb[:, j, :]).then_inc(which_found.sem, 1)
                        dve.wait_ge(exped.sem, exped.freed(b))
                        dve.tensor_scalar(low[:, j, :], s_sb[:, j, :], best[:, j, 0:1], None, ALU.subtract
                                          ).then_inc(lowered.sem, 1)
                        dve.wait_ge(which_found.sem, which_found.done(b))
                        dve.tensor_copy(which_f[:, j, :], which[:, j, 0:2]).then_inc(which_cast.sem, 1)
                        dve.wait_ge(which_cast.sem, which_cast.done(b))
                        for k in range(2):
                            last = dve.tensor_scalar(pick[:, j, k, :], number[:, :], which_f[:, j, k:k + 1], None,
                                                     ALU.is_equal)
                        last.then_inc(picked.sem, 1)
                        dve.wait_ge(picked.sem, picked.done(b))
                        if top == 2:
                            dve.tensor_tensor(pick[:, j, 0, :], pick[:, j, 0, :], pick[:, j, 1, :], ALU.add
                                              ).then_inc(picked2.sem, 1)
                            dve.wait_ge(picked2.sem, picked2.done(b))
                            dve.wait_ge(exped.sem, exped.done(b))
                            dve.tensor_tensor(pick[:, j, 1, :], pick[:, j, 0, :], ex[:, j, :], ALU.mult
                                              ).then_inc(chosen.sem, 1)
                            dve.wait_ge(chosen.sem, chosen.done(b))
                            dve.tensor_reduce(tot[:, j, :], pick[:, j, 1, :], AX.X, ALU.add).then_inc(summed.sem, 1)
                        else:
                            dve.wait_ge(exped.sem, exped.done(b))
                            dve.tensor_tensor(pick[:, j, 1, :], pick[:, j, 0, :], ex[:, j, :], ALU.mult
                                              ).then_inc(picked2.sem, 1)
                            dve.wait_ge(picked2.sem, picked2.done(b))
                            dve.tensor_reduce(tot[:, j, :], ex[:, j, :], AX.X, ALU.add).then_inc(summed.sem, 1)
                        dve.wait_ge(summed.sem, summed.done(b))
                        dve.reciprocal(inv[:, j, :], tot[:, j, :]).then_inc(inverted.sem, 1)
                        dve.wait_ge(inverted.sem, inverted.done(b))
                        dve.tensor_scalar(weight_all[:, :, b, 0], pick[:, j, 1, :], inv[:, j, :], None, ALU.mult
                                          ).then_inc(weighted.sem, 1)
        for n in names:
            n.advance(B)
        loads.advance(16 * len(plain))
        consts.advance(1)
        f.end()


def expert_stage(core, hT_all, weight_all, acc, w_up, w_down, w_gate=None, b_up=None):
    nc, loads = core.nc, core.loads
    E, _, HID = w_up.shape
    HC = HID // P
    G, S = 4, B // 4
    units = 2 * G
    gated = w_gate is not None
    with ExitStack() as ctx:
        sb = lambda n, s, t=F32: ctx.enter_context(nc.sbuf_tensor(core.named(n), s, t))
        up_sb, down_sb = sb("w_up", [P, 2, DC, HID]), sb("w_down", [P, 2, HC, D])
        gate_sb = sb("w_gate", [P, 2, DC, HID]) if gated else None
        bias_sb = sb("b_up", [P, 2, HC]) if b_up is not None else None
        hid = sb("hid", [P, 2, HC, S * P])
        silu = sb("silu", [P, 2, S * P]) if gated else None
        up_ps = [ctx.enter_context(nc.psum_tensor(core.named(f"up_ps{k}"), [P, S * P], F32)) for k in range(2)]
        gate_ps = [ctx.enter_context(nc.psum_tensor(core.named(f"gate_ps{k}"), [P, S * P], F32)) for k in range(2)] if gated else None
        out_ps = [ctx.enter_context(nc.psum_tensor(core.named(f"e_out_ps{k}"), [P, 2, D], F32)) for k in range(2)]
        c = core.count
        upped, gated_done, silued, hid_ready, downed, added = (
            c("upped"), c("gate_made"), c("silued"), c("hid_ready"), c("downed"), c("added"))
        cleared = c("acc_cleared")
        landed = [c("expert_landed0"), c("expert_landed1")]
        per_load = 2 + gated + (b_up is not None)
        with nc.Block() as block:
            @block.sync
            def _(sp):
                with sp.Fori(0, E // 2) as i:
                    for k in range(2):
                        e = 2 * i + k
                        sp.wait_ge(downed.sem, downed.done(2 * (units * i + G * k - G) - 1))
                        pairs = [(up_sb[:, k], w_up[e]), (down_sb[:, k], w_down[e])]
                        if gated:
                            pairs.append((gate_sb[:, k], w_gate[e]))
                        for dst, src in pairs:
                            sp.dma_start(dst, chunked(src)).then_inc(landed[k].sem, 16)
                        if b_up is not None:
                            sp.dma_start(bias_sb[:, k], b_up[e]).then_inc(landed[k].sem, 16)

            @block.gpsimd
            def _(pool):
                pool.memset(acc[:, :, :], 0.0).then_inc(cleared.sem, 1)

            @block.tensor
            def _(pe):
                with pe.Fori(0, E // 2) as i:
                    for n in range(units + 1):
                        if n < units:
                            k, g = n // G, n % G
                            if g == 0:
                                pe.wait_ge(landed[k].sem, landed[k].base + 16 * per_load * (i + 1))
                            for m in range(HC):
                                u = HC * (units * i + n) + m
                                for ps, w, used, made in (((gate_ps, gate_sb, silued, gated_done),) if gated else ()) + (
                                        (up_ps, up_sb, hid_ready, upped),):
                                    pe.wait_ge(used.sem, used.freed(u))
                                    for cc in range(DC):
                                        last = pe.matmul(ps[m % 2][:, :], w[:, k, cc, m * P:(m + 1) * P],
                                                         hT_all[:, cc, S * g:S * (g + 1), :].rearrange("p b t -> p (b t)"),
                                                         start=(cc == 0), stop=(cc == DC - 1))
                                    last.then_inc(made.sem, 1)
                        if n >= 1:
                            q = n - 1
                            unit = units * i + q
                            pe.wait_ge(hid_ready.sem, hid_ready.done(HC * unit + HC - 1))
                            for t in range(S):
                                if t % 2 == 0:
                                    half = 2 * unit + t // 2
                                    pe.wait_ge(added.sem, added.freed(half))
                                for m in range(HC):
                                    last = pe.matmul(out_ps[t // 2][:, t % 2, :], hid[:, q % 2, m, t * P:(t + 1) * P],
                                                     down_sb[:, q // G, m, :], start=(m == 0), stop=(m == HC - 1))
                                if t % 2:
                                    last.then_inc(downed.sem, 1)

            @block.scalar
            def _(act):
                with act.Fori(0, E // 2) as i:
                    for n in range(units):
                        k = n // G
                        if b_up is not None and n % G == 0:
                            act.wait_ge(landed[k].sem, landed[k].base + 16 * per_load * (i + 1))
                        for m in range(HC):
                            u = HC * (units * i + n) + m
                            if gated:
                                act.wait_ge(gated_done.sem, gated_done.done(u))
                                act.wait_ge(hid_ready.sem, hid_ready.freed(u))
                                act.activation(silu[:, m % 2, :], gate_ps[m % 2][:, :], ACT.Silu
                                               ).then_inc(silued.sem, 1)
                            else:
                                act.wait_ge(upped.sem, upped.done(u))
                                if m == 0:
                                    act.wait_ge(downed.sem, downed.done(2 * (units * i + n - 2) + 1))
                                act.activation(hid[:, n % 2, m, :], up_ps[m % 2][:, :], ACT.Relu,
                                               bias=bias_sb[:, k, m:m + 1]).then_inc(hid_ready.sem, 1)

            @block.vector
            def _(dve):
                dve.wait_ge(cleared.sem, cleared.done(0))
                with dve.Fori(0, E // 2) as i:
                    for n in range(units + 1):
                        for m in range(HC if gated and n < units else 0):
                            u = HC * (units * i + n) + m
                            dve.wait_ge(silued.sem, silued.done(u))
                            dve.wait_ge(upped.sem, upped.done(u))
                            if m == 0:
                                dve.wait_ge(downed.sem, downed.done(2 * (units * i + n - 2) + 1))
                            dve.tensor_tensor(hid[:, n % 2, m, :], up_ps[m % 2][:, :], silu[:, m % 2, :], ALU.mult
                                              ).then_inc(hid_ready.sem, 1)
                        if n >= 1:
                            q = n - 1
                            for t in range(S):
                                half = 2 * (units * i + q) + t // 2
                                b = S * (q % G) + t
                                if t % 2 == 0:
                                    dve.wait_ge(downed.sem, downed.done(half))
                                    dve.wait_ge(added.sem, added.done(half - 2 * G))
                                last = dve.scalar_tensor_tensor(
                                    out=acc[:, b, :], in0=out_ps[t // 2][:, t % 2, :],
                                    scalar=weight_all[:, 2 * i + q // G, b, :], in1=acc[:, b, :],
                                    op0=ALU.mult, op1=ALU.add)
                                if t % 2:
                                    last.then_inc(added.sem, 1)
        total = E * G
        for n, items in ((upped, HC), (hid_ready, HC), (downed, 2), (added, 2)):
            n.advance(total * items)
        if gated:
            gated_done.advance(total * HC)
            silued.advance(total * HC)
        cleared.advance(1)
        for n in landed:
            n.advance(16 * per_load * E // 2)


def merge_stage(core, acc, residual=None, weight_all=None, bias=None):
    nc, loads = core.nc, core.loads
    with ExitStack() as ctx:
        sb = lambda n, s, t=F32: ctx.enter_context(nc.sbuf_tensor(core.named(n), s, t))
        with_bias = bias is not None
        more = acc if with_bias else residual
        f = Frame(core, ctx, out_bias=lambda b: more[:, b, :])
        if with_bias:
            E = bias.shape[0]
            bias_sb, w_tok, wT = sb("bias", [E, D]), sb("w_tok", [P, 2, E]), sb("wT", [E, 2, P])
            picked = core.count("w_picked")
            with nc.Block() as block:
                @block.sync
                def _(sp):
                    sp.dma_start(bias_sb[:, :], bias[:, :]).then_inc(loads.sem, 16)

                @block.gpsimd
                def _(pool):
                    with pool.Fori(0, B // 2) as i:
                        for j in range(2):
                            f.fetch(pool, 2 * i + j, j)
                            pool.tensor_copy(w_tok[:, j, :], weight_all[:, :, 2 * i + j, 0]).then_inc(picked.sem, 1)
                        for j in range(2):
                            f.rstd_out(pool, 2 * i + j, j)

                @block.tensor
                def _(pe):
                    pe.wait_ge(loads.sem, loads.base + 16)
                    with pe.Fori(0, B // 2) as i:
                        for j in range(2):
                            b = 2 * i + j
                            pe.wait_ge(picked.sem, picked.done(b))
                            pe.wait_ge(f.out_used.sem, f.out_used.freed(b, 1))
                            pe.transpose(f.xT_ps[0:E, 0, :], w_tok[:, j, :], core.ident[:, :]
                                         ).then_inc(f.xT_turned.sem, 1)
                            pe.wait_ge(f.xT_ready.sem, f.xT_ready.done(b))
                            pe.matmul(f.out_ps, wT[:, j, :], bias_sb[:, :], start=True, stop=True
                                      ).then_inc(f.out_ready.sem, 1)

                @block.scalar
                def _(act):
                    with act.Fori(0, B // 2) as i:
                        for j in range(2):
                            b = 2 * i + j
                            act.wait_ge(f.xT_turned.sem, f.xT_turned.done(b))
                            act.wait_ge(f.out_ready.sem, f.out_ready.freed(b))
                            act.activation(wT[:, j, :], f.xT_ps[0:E, 0, :], ACT.Copy).then_inc(f.xT_ready.sem, 1)

                @block.vector
                def _(dve):
                    with dve.Fori(0, B // 2) as i:
                        for j in range(2):
                            f.finish(dve, 2 * i + j, j)
                            f.save_normed(dve, 2 * i + j, j)
            loads.advance(16)
            picked.advance(B)
            f.end()
        else:
            with nc.Block() as block:
                @block.gpsimd
                def _(pool):
                    with pool.Fori(0, B // 2) as i:
                        for j in range(2):
                            f.fetch(pool, 2 * i + j, j)
                        for j in range(2):
                            f.rstd_out(pool, 2 * i + j, j)

                @block.vector
                def _(dve):
                    with dve.Fori(0, B // 2) as i:
                        for j in range(2):
                            b = 2 * i + j
                            dve.wait_ge(f.xres_ready.sem, f.xres_ready.done(b))
                            dve.tensor_tensor(f.y[:, j, :], acc[:, b, :], f.xres[:, j, :], ALU.add
                                              ).then_inc(f.out_used.sem, 1)
                            dve.wait_ge(f.out_used.sem, f.out_used.done(b))
                            f.layernorm(dve, b, j)
                        for j in range(2):
                            f.save_normed(dve, 2 * i + j, j)
            for n in (f.x_in_ready, f.xres_ready, f.out_used, f.y_stats, f.y_mv, f.y_var, f.y_rstd, f.x_saved):
                n.advance(B)



def depool_constants():
    logp = np.float32(-0.001)
    dt = np.float32(-np.log(-np.expm1(logp)))
    decay = np.exp(-np.float64(dt))
    gap = np.arange(P)[:, None] - np.arange(P)[None, :]
    table = np.where(gap >= 0, decay ** np.maximum(gap, 0), 0.0).astype(np.float32)
    return table, float(np.float32(1.0) / dt), float(np.float32(dt * np.exp(logp)))


def depool_stage(core, context, patch_lens, decay, upto, w_in, b_in, g_res, g_init):
    nc, loads = core.nc, core.loads
    _, over_dt, times_dt = depool_constants()
    with ExitStack() as ctx:
        sb = lambda n, s, t=F32: ctx.enter_context(nc.sbuf_tensor(core.named(n), s, t))
        ob = sb("out_bias", [P, D])
        f = Frame(core, ctx, out_bias=ob[:, :], own_input=True)
        w_sb, gr, gi, gi2 = sb("w_in", [P, DC, D]), sb("g_res", [P, DC]), sb("g_init", [P, D]), sb("g_init2", [P, D])
        lens_i, lens, ends = sb("lens_i", [P, B, P], I32), sb("lens", [P, B, P]), sb("ends", [P, B, P])
        hit, hits, hit_col = sb("hit", [P, B, P]), sb("hits", [P, 2, B]), sb("hit_col", [P, B])
        decay_sb, upto_sb = sb("decay", [P, P]), sb("upto", [P, P])
        zeros, token, token1, token2 = sb("zeros", [P, P]), sb("token", [P, 1]), sb("token1", [P, 1]), sb("token2", [P, 1])
        plug, spread = sb("plug", [P, B, P]), sb("spread", [P, B, P])
        c_in = sb("c_in", [P, 2, CTX])
        sq, ss, ms, rs = sb("sq", [P, CTX]), sb("ss", [P, 2, 2]), sb("ms", [P, 2, 2]), sb("rs", [P, 2, 2])
        over_n, rms_eps = sb("over_n", [P, 2]), sb("rms_eps", [P, 2])
        half2 = sb("half2", [P, 2])
        u, spread_in = sb("u", [P, 2, D]), sb("spread_in", [P, 2, P])
        wide_ps = ctx.enter_context(nc.psum_tensor(core.named("wide_ps"), [P, 4, 4, P], F32))
        c = core.count
        consts, prep, prep_pe, prep_act = c("constants_made"), c("prep_done"), c("prep_products"), c("prep_copied")
        landed = [c("c_landed0"), c("c_landed1")]
        prep_hits, squared_x = c("prep_hits"), c("squared_x")
        squared, ms1, ms2, rs_ready, u_ready, spread_ready = (c("squared"), c("ms1_done"), c("ms2_done"), c("rs_ready"),
                                                               c("u_ready"), c("spread_ready"))
        plain = ((w_sb[:, :, :], chunked(w_in)), (gr[:, :], g_res[:, :]), (gi[:, :], row_everywhere(g_init[0:D])),
                 (ob[:, :], row_everywhere(b_in)), (decay_sb[:, :], decay[:, :]), (upto_sb[:, :], upto[:, :]),
                 (lens_i[:, :, :], patch_lens.rearrange("(o b) t -> o b t", o=1).broadcast_to([P, B, P])))
        weights = loads.base + 16 * len(plain)
        with nc.Block() as block:
            @block.sync
            def _(sp):
                for dst, src in plain:
                    sp.dma_start(dst, src).then_inc(loads.sem, 16)
                with sp.Fori(0, B // 2) as i:
                    for j in range(2):
                        b = 2 * i + j
                        sp.wait_ge(u_ready.sem, u_ready.freed(b))
                        sp.dma_start(c_in[:, j, :], context[b]).then_inc(landed[j].sem, 16)

            @block.gpsimd
            def _(pool):
                pool.memset(zeros[:, :], 0.0)
                pool.memset(over_n[:, 0:1], 1.0 / D)
                pool.memset(over_n[:, 1:2], 1.0 / CTX)
                pool.memset(rms_eps[:, :], 1e-5)
                pool.memset(half2[:, :], -0.5)
                pool.iota(token[:, :], pattern=[[0, 1]], base=0, channel_multiplier=1,
                          allow_small_or_imprecise_dtypes=True)
                pool.iota(token1[:, :], pattern=[[0, 1]], base=1, channel_multiplier=1,
                          allow_small_or_imprecise_dtypes=True)
                pool.iota(token2[:, :], pattern=[[0, 1]], base=1 - P, channel_multiplier=1,
                          allow_small_or_imprecise_dtypes=True).then_inc(consts.sem, 1)
                pool.wait_ge(consts.sem, consts.done(0))
                pool.wait_ge(loads.sem, weights)
                pool.wait_ge(prep_act.sem, prep_act.done(0))
                with pool.Fori(0, B // 2) as i:
                    for j in range(2):
                        b = 2 * i + j
                        f.fetch(pool, b, j)
                        pool.wait_ge(f.out_ready.sem, f.out_ready.freed(b))
                        pool.tensor_copy(spread_in[:, j, :], spread[:, b, :]).then_inc(spread_ready.sem, 1)
                        pool.wait_ge(squared.sem, squared.done(b))
                        pool.tensor_tensor(ms[:, j, :], ss[:, j, :], over_n[:, :], ALU.mult).then_inc(ms1.sem, 1)
                        pool.wait_ge(ms1.sem, ms1.done(b))
                        pool.tensor_tensor(ms[:, j, :], ms[:, j, :], rms_eps[:, :], ALU.add).then_inc(ms2.sem, 1)
                        pool.wait_ge(ms2.sem, ms2.done(b))
                        pool.tensor_tensor(rs[:, j, :], ms[:, j, :], half2[:, :], ALU.pow).then_inc(rs_ready.sem, 1)
                    for j in range(2):
                        f.rstd_out(pool, 2 * i + j, j)

            @block.scalar
            def _(act):
                act.wait_ge(prep_pe.sem, prep_pe.done(1))
                act.activation(spread[:, :, :].rearrange("p (g s) t -> p g s t", g=4), wide_ps[:, :, :, :], ACT.Copy
                               ).then_inc(prep_act.sem, 1)
                act.wait_ge(loads.sem, weights)
                with act.Fori(0, B // 2) as i:
                    for j in range(2):
                        b = 2 * i + j
                        act.wait_ge(f.x_in_ready.sem, f.x_in_ready.done(b))
                        act.wait_ge(ms1.sem, ms1.freed(b))
                        act.activation(sq[:, 0:D], f.x_in[:, j, :], ACT.Square, accum_out=ss[:, j, 0:1]
                                       ).then_inc(squared_x.sem, 1)
                        act.wait_ge(landed[j].sem, landed[j].base + 16 * (i + 1))
                        act.wait_ge(squared_x.sem, squared_x.done(b))
                        act.activation(sq[:, :], c_in[:, j, :], ACT.Square, accum_out=ss[:, j, 1:2]
                                       ).then_inc(squared.sem, 1)
                    for j in range(2):
                        f.copy_turned(act, 2 * i + j, j, scale=gr)

            @block.tensor
            def _(pe):
                wide = lambda t: t[:, :, :].rearrange("p (g s) t -> p g (s t)", g=4)
                pe.wait_ge(loads.sem, weights)
                pe.wait_ge(prep.sem, prep.done(6))
                for g in range(4):
                    last = pe.matmul(wide_ps[:, g].rearrange("p s t -> p (s t)"), core.ones[:, :], wide(hit)[:, g, :],
                                     start=True, stop=True)
                last.then_inc(prep_pe.sem, 1)
                pe.wait_ge(prep.sem, prep.done(8))
                for g in range(4):
                    last = pe.matmul(wide_ps[:, g].rearrange("p s t -> p (s t)"), decay_sb[:, :], wide(plug)[:, g, :],
                                     start=True, stop=True)
                last.then_inc(prep_pe.sem, 1)
                with pe.Fori(0, B // 2) as i:
                    for j in range(2):
                        f.turn(pe, 2 * i + j, j)
                    for j in range(2):
                        b = 2 * i + j
                        f.claim_bank(pe, b, j)
                        pe.wait_ge(f.xT_ready.sem, f.xT_ready.done(b))
                        pe.wait_ge(u_ready.sem, u_ready.done(b))
                        pe.wait_ge(spread_ready.sem, spread_ready.done(b))
                        for cc in range(DC):
                            pe.matmul(f.out_ps, f.xT[:, j, cc, :], w_sb[:, cc, :], start=(cc == 0), stop=False)
                        pe.matmul(f.out_ps, spread_in[:, j, :], u[:, j, :], start=False, stop=True
                                  ).then_inc(f.out_ready.sem, 1)

            @block.vector
            def _(dve):
                def step(instruction, n):
                    instruction.then_inc(prep.sem, 1)
                    dve.wait_ge(prep.sem, prep.done(n))

                dve.wait_ge(loads.sem, weights)
                dve.wait_ge(consts.sem, consts.done(0))
                step(dve.tensor_copy(lens[:, :, :], lens_i[:, :, :]), 0)
                for b in range(B):
                    last = dve.tensor_tensor_scan(ends[:, b, :], lens[:, b, :], zeros[:, :], 0.0, ALU.add, ALU.add)
                step(last, 1)
                step(dve.tensor_scalar(hit[:, :, :], ends[:, :, :], token1[:, :], None, ALU.is_equal), 2)
                step(dve.tensor_reduce(hits[:, 0, :], hit[:, :, :], AX.X, ALU.max), 3)
                step(dve.tensor_scalar(hit[:, :, :], ends[:, :, :], token2[:, :], None, ALU.is_equal), 4)
                dve.tensor_reduce(hits[:, 1, :], hit[:, :, :], AX.X, ALU.max).then_inc(prep_hits.sem, 1)
                dve.wait_ge(prep_hits.sem, prep_hits.done(0))
                step(dve.tensor_tensor(hit_col[:, :], hits[:, 0, :], hits[:, 1, :], ALU.max), 5)
                step(dve.tensor_tensor(hit[:, :, :], hit_col[:, :].unsqueeze(2).broadcast_to([P, B, P]),
                                       upto_sb[:, :].unsqueeze(1).broadcast_to([P, B, P]), ALU.mult), 6)
                dve.wait_ge(prep_pe.sem, prep_pe.done(0))
                step(dve.tensor_scalar(plug[:, :, :].rearrange("p (g s) t -> p g s t", g=4), wide_ps[:, :, :, :],
                                       -1.0, 0.0, ALU.add, ALU.max), 7)
                step(dve.tensor_scalar(plug[:, :, :], plug[:, :, :], float(P - 1), token[:, :], ALU.min,
                                       ALU.is_equal), 8)
                step(dve.tensor_scalar(gi2[:, :], gi[:, :], over_dt, times_dt, ALU.mult, ALU.mult), 9)
                with dve.Fori(0, B // 2) as i:
                    for j in range(2):
                        b = 2 * i + j
                        dve.wait_ge(rs_ready.sem, rs_ready.done(b))
                        dve.wait_ge(f.xT_turned.sem, f.xT_turned.freed(b))
                        dve.tensor_scalar(f.h_in[:, j, :], f.x_in[:, j, :], rs[:, j, 0:1], None, ALU.mult
                                          ).then_inc(f.pre[4].sem, 1)
                        dve.wait_ge(f.out_ready.sem, f.out_ready.freed(b))
                        dve.scalar_tensor_tensor(out=u[:, j, :], in0=c_in[:, j, 0:D], scalar=rs[:, j, 1:2],
                                                 in1=gi2[:, :], op0=ALU.mult, op1=ALU.mult).then_inc(u_ready.sem, 1)
                    for j in range(2):
                        f.finish(dve, 2 * i + j, j)
                    for j in range(2):
                        f.save_normed(dve, 2 * i + j, j)
        loads.advance(16 * len(plain))
        consts.advance(1)
        prep.advance(10)
        prep_hits.advance(1)
        prep_pe.advance(2)
        prep_act.advance(1)
        for n in (squared, squared_x, ms1, ms2, rs_ready, u_ready, spread_ready):
            n.advance(B)
        for n in landed:
            n.advance(16 * B // 2)
        f.end()



def ternary_stage(core, weight, gamma, beta):
    nc, loads = core.nc, core.loads
    QB, EPS = 128.0, 1e-5
    LIMIT = float(np.float32(QB - EPS))
    ROUND = 1.5 * 2.0 ** 23
    with ExitStack() as ctx:
        sb = lambda n, s, t=F32: ctx.enter_context(nc.sbuf_tensor(core.named(n), s, t))
        gb = sb("out_scale", [P, 1])
        f = Frame(core, ctx, own_input=True, out_scale=gb[:, :])
        w, wq, g_row, b_row = sb("w", [P, DC, D]), sb("w_q", [P, DC, D]), sb("gamma", [P, D]), sb("beta", [P, D])
        w_abs, w_sum, w_tot, mean_w, inv_w = (sb("w_abs", [P, DC, D]), sb("w_sum", [P, 1]), sb("w_tot", [P, 1]),
                                              sb("mean_w", [P, 1]), sb("inv_w", [P, 1]))
        xn = sb("xn", [P, B, D])
        stats, mv, var, rstd = sb("n_stats", [P, 2, 6]), sb("n_mv", [P, 2, 2]), sb("n_var", [P, 2, 1]), sb("n_rstd", [P, 2, 1])
        n_eps, centred, scaled, mag = sb("n_eps", [P, 1]), sb("centred", [P, 2, D]), sb("scaled", [P, 2, D]), sb("mag", [P, 2, D])
        largest, of_part, of_all, inv_g, up = (sb("largest", [P, B, 1]), sb("of_part", [P, 1]), sb("of_all", [P, 1]),
                                               sb("inv_g", [P, 1]), sb("up", [P, 1]))
        xs = sb("xs", [P, 2, D])
        c = core.count
        consts, prep, prep_pool = c("constants_made"), c("prep_done"), c("prep_pool")
        n1 = (stats_done, mv_done, var_done, rstd_done, centred_done, scaled_done, xn_done, mag_done, largest_done) = (
            c("n_stats_done"), c("n_mv_done"), c("n_var_done"), c("n_rstd_done"), c("centred_done"), c("scaled_done"),
            c("xn_done"), c("mag_done"), c("largest_done"))
        xs_done = c("xs_done")
        plain = ((w[:, :, :], chunked(weight)), (g_row[:, :], row_everywhere(gamma)), (b_row[:, :], row_everywhere(beta)))
        weights = loads.base + 16 * len(plain)
        with nc.Block() as block:
            @block.sync
            def _(sp):
                for dst, src in plain:
                    sp.dma_start(dst, src).then_inc(loads.sem, 16)

            @block.gpsimd
            def _(pool):
                pool.memset(n_eps[:, :], 1e-3).then_inc(consts.sem, 1)
                pool.wait_ge(consts.sem, consts.done(0))
                with pool.Fori(0, B // 2) as i:
                    for j in range(2):
                        b = 2 * i + j
                        pool.wait_ge(mv_done.sem, mv_done.done(b))
                        pool.tensor_tensor(var[:, j, :], mv[:, j, 1:2], n_eps[:, :], ALU.add).then_inc(var_done.sem, 1)
                        pool.wait_ge(var_done.sem, var_done.done(b))
                        pool.tensor_tensor(rstd[:, j, :], var[:, j, :], core.minus_half[:, :], ALU.pow
                                           ).then_inc(rstd_done.sem, 1)
                pool.wait_ge(prep.sem, prep.done(1))
                pool.partition_all_reduce(w_tot[:, :], w_sum[:, :], P, bass.bass_isa.ReduceOp.add
                                          ).then_inc(prep_pool.sem, 1)
                pool.wait_ge(prep.sem, prep.done(2))
                pool.partition_all_reduce(of_all[:, :], of_part[:, :], P, bass.bass_isa.ReduceOp.max
                                          ).then_inc(prep_pool.sem, 1)
                with pool.Fori(0, B // 2) as i:
                    for j in range(2):
                        f.fetch(pool, 2 * i + j, j)
                    for j in range(2):
                        f.rstd_out(pool, 2 * i + j, j)

            @block.tensor
            def _(pe):
                pe.wait_ge(prep.sem, prep.done(8))
                with pe.Fori(0, B // 2) as i:
                    for j in range(2):
                        f.turn(pe, 2 * i + j, j)
                    for j in range(2):
                        b = 2 * i + j
                        f.claim_bank(pe, b, j)
                        pe.wait_ge(f.xT_ready.sem, f.xT_ready.done(b))
                        for cc in range(DC):
                            last = pe.matmul(f.out_ps, f.xT[:, j, cc, :], wq[:, cc, :], start=(cc == 0), stop=(cc == DC - 1))
                        last.then_inc(f.out_ready.sem, 1)

            @block.scalar
            def _(act):
                with act.Fori(0, B // 2) as i:
                    for j in range(2):
                        f.copy_turned(act, 2 * i + j, j)

            @block.vector
            def _(dve):
                def step(instruction, n):
                    instruction.then_inc(prep.sem, 1)
                    dve.wait_ge(prep.sem, prep.done(n))

                dve.wait_ge(loads.sem, weights)
                with dve.Fori(0, B // 2) as i:
                    for j in range(2):
                        b = 2 * i + j
                        dve.bn_stats(stats[:, j, :], core.x[:, b, :]).then_inc(stats_done.sem, 1)
                        dve.wait_ge(stats_done.sem, stats_done.done(b))
                        dve.sem_inc(f.passed.sem, 1)
                        dve.bn_aggr(mv[:, j, :], stats[:, j, :]).then_inc(mv_done.sem, 1)
                    for j in range(2):
                        b = 2 * i + j
                        dve.wait_ge(mv_done.sem, mv_done.done(b))
                        dve.wait_ge(rstd_done.sem, rstd_done.done(b))
                        dve.tensor_scalar(centred[:, j, :], core.x[:, b, :], mv[:, j, 0:1], rstd[:, j, :],
                                          ALU.subtract, ALU.mult).then_inc(centred_done.sem, 1)
                        dve.wait_ge(centred_done.sem, centred_done.done(b))
                        dve.tensor_tensor(scaled[:, j, :], centred[:, j, :], g_row[:, :], ALU.mult
                                          ).then_inc(scaled_done.sem, 1)
                        dve.wait_ge(scaled_done.sem, scaled_done.done(b))
                        dve.tensor_tensor(xn[:, b, :], scaled[:, j, :], b_row[:, :], ALU.add).then_inc(xn_done.sem, 1)
                        dve.wait_ge(xn_done.sem, xn_done.done(b))
                        dve.scalar_tensor_tensor(out=mag[:, j, :], in0=xn[:, b, :], scalar=-1.0, in1=xn[:, b, :],
                                                 op0=ALU.mult, op1=ALU.max).then_inc(mag_done.sem, 1)
                        dve.wait_ge(mag_done.sem, mag_done.done(b))
                        dve.tensor_reduce(largest[:, b, :], mag[:, j, :], AX.X, ALU.max).then_inc(largest_done.sem, 1)
                dve.wait_ge(largest_done.sem, largest_done.done(B - 1))
                step(dve.scalar_tensor_tensor(out=w_abs[:, :, :], in0=w[:, :, :], scalar=-1.0, in1=w[:, :, :],
                                              op0=ALU.mult, op1=ALU.max), 0)
                step(dve.tensor_reduce(w_sum[:, :], w_abs[:, :, :], AX.XY, ALU.add), 1)
                step(dve.tensor_reduce(of_part[:, :], largest[:, :, 0], AX.X, ALU.max), 2)
                dve.wait_ge(prep_pool.sem, prep_pool.done(1))
                step(dve.tensor_scalar(mean_w[:, :], w_tot[:, :], 1.0 / (D * D), None, ALU.mult), 3)
                step(dve.tensor_scalar(inv_w[:, :], mean_w[:, :], EPS, None, ALU.add), 4)
                step(dve.reciprocal(inv_w[:, :], inv_w[:, :]), 5)
                step(dve.tensor_scalar(wq[:, :, :], w[:, :, :], inv_w[:, :], ROUND, ALU.mult, ALU.add), 6)
                step(dve.tensor_scalar(wq[:, :, :], wq[:, :, :], -ROUND, 1.0, ALU.add, ALU.min), 7)
                step(dve.tensor_scalar(wq[:, :, :], wq[:, :, :], -1.0, None, ALU.max), 8)
                step(dve.reciprocal(inv_g[:, :], of_all[:, :]), 9)
                step(dve.tensor_scalar(up[:, :], inv_g[:, :], QB, None, ALU.mult), 10)
                step(dve.tensor_scalar(gb[:, :], of_all[:, :], mean_w[:, :], 1.0 / QB, ALU.mult, ALU.mult), 11)
                with dve.Fori(0, B // 2) as i:
                    for j in range(2):
                        b = 2 * i + j
                        dve.tensor_scalar(xs[:, j, :], xn[:, b, :], up[:, :], LIMIT, ALU.mult, ALU.min
                                          ).then_inc(xs_done.sem, 1)
                        dve.wait_ge(xs_done.sem, xs_done.done(b))
                        dve.wait_ge(f.xT_turned.sem, f.xT_turned.freed(b))
                        dve.tensor_scalar(f.h_in[:, j, :], xs[:, j, :], -LIMIT, None, ALU.max
                                          ).then_inc(f.pre[4].sem, 1)
                    for j in range(2):
                        f.finish(dve, 2 * i + j, j)
                    for j in range(2):
                        f.save_normed(dve, 2 * i + j, j)
        loads.advance(16 * len(plain))
        consts.advance(1)
        prep.advance(12)
        prep_pool.advance(2)
        for n in n1 + (xs_done,):
            n.advance(B)
        f.end()



def mamba_stage(core, w_in, conv_w, conv_b, w_x, w_dt, b_dt, a_log, d_skip, w_out):
    nc, loads = core.nc, core.loads
    INNER, N, K, R = 512, 16, 4, 16
    IC = INNER // P
    XD = R + 2 * N
    with ExitStack() as ctx:
        sb = lambda n, s, t=F32: ctx.enter_context(nc.sbuf_tensor(core.named(n), s, t))
        ps = lambda n: ctx.enter_context(nc.psum_tensor(core.named(n), [P, IC, P], F32))
        f = Frame(core, ctx, ahead=True)
        w_in_sb, w_x_sb, w_dt_sb, w_out_sb = (sb("w_in", [P, DC, 2 * INNER]), sb("w_x", [P, IC, XD]),
                                              sb("w_dt", [R, INNER]), sb("w_out", [P, IC, D]))
        taps_w, conv_b_sb, b_dt_sb, d_sb, a_sb = (sb("taps_w", [P, IC, K]), sb("conv_b", [P, IC]), sb("b_dt", [P, IC]),
                                                  sb("d_skip", [P, IC]), sb("a", [P, IC, N]))
        taps, skip = sb("taps", [P, IC, K, P]), sb("skip", [P, IC, P])
        u = sb("u", [P, 1, IC, K - 1 + P])
        uc, sz, xd = sb("uc", [P, 2, IC, P]), sb("sz", [P, 2, IC, P]), sb("xd", [XD, 2, P])
        pre, low = sb("dt_pre", [P, IC, P]), sb("dt_low", [P, IC, P])
        dt, dtu = sb("dt", [P, 2, IC, P]), sb("dtu", [P, 2, IC, P])
        bc = sb("bc", [P, 2, 2 * N, P])
        da, dbu, h, hc = sb("da", [P, 2, N, P]), sb("dbu", [P, 2, N, P]), sb("h", [P, N, P]), sb("hc", [P, 2, N, P])
        yT = sb("yT", [P, 2, IC, P])
        u_ps, z_ps, v_ps, dt_ps, y_ps = ps("u_ps"), ps("z_ps"), ps("v_ps"), ps("dt_ps"), ps("y_ps")
        bc_ps = [ps("bc_ps0"), ps("bc_ps1")]
        c = core.count
        per_b = (u_made, z_made, u_ready, conv_made, uc_ready, sz_ready, xd_made, xd_ready, dt_made, pre_ready,
                 abs_done, dexp_done, low_ready, relu_done, dt_ready, dtu_ready, yT_ready) = (
            c("u_made"), c("z_made"), c("u_ready"), c("conv_made"), c("uc_ready"), c("sz_ready"), c("xd_made"),
            c("xd_ready"), c("dt_made"), c("pre_ready"), c("abs_done"), c("dexp_done"), c("low_ready"),
            c("relu_done"), c("dt_ready"), c("dtu_ready"), c("yT_ready"))
        bc_made, bc_ready = c("bc_made"), c("bc_ready")
        da_ready, dbu_ready, scanned, hc_ready, y_summed = (c("da_ready"), c("dbu_ready"), c("scanned"),
                                                            c("hc_ready"), c("y_summed"))
        consts, prep, prep_a = c("constants_made"), c("prep_done"), c("prep_a")
        plain = ((w_in_sb[:, :, :], chunked(w_in)), (w_x_sb[:, :, :], chunked(w_x)), (w_dt_sb[:, :], w_dt[:, :]),
                 (w_out_sb[:, :, :], chunked(w_out)), (taps_w[:, :, :], conv_w[:, :, :]), (conv_b_sb[:, :], conv_b[:, :]),
                 (b_dt_sb[:, :], b_dt[:, :]), (d_sb[:, :], d_skip[:, :]), (a_sb[:, :, :], a_log[:, :, :]))
        weights = loads.base + 16 * len(plain)
        BCN = 2 * N // IC

        def every_sequence(eng, unit):
            unit(0, 0, True, False)
            with eng.Fori(0, B // 2 - 1) as i:
                unit(2 * i + 1, 1, False, False)
                unit(2 * i + 2, 0, False, False)
            unit(B - 1, 1, False, True)

        with nc.Block() as block:
            @block.sync
            def _(sp):
                for dst, src in plain:
                    sp.dma_start(dst, src).then_inc(loads.sem, 16)

            @block.gpsimd
            def _(pool):
                pool.memset(u[:, :, :, 0:K - 1], 0.0)
                pool.memset(da[:, :, :, 0:1], 0.0).then_inc(consts.sem, 1)

                def front(b, j):
                    pool.wait_ge(low_ready.sem, low_ready.done(b))
                    pool.wait_ge(scanned.sem, scanned.done(IC * (b - 2) + IC - 1))
                    pool.sem_inc(f.passed.sem, 1)
                    pool.tensor_scalar(dt[:, j], pre[:, :, :], 0.0, None, ALU.max).then_inc(relu_done.sem, 1)
                    pool.wait_ge(relu_done.sem, relu_done.done(b))
                    pool.tensor_tensor(dt[:, j], dt[:, j], low[:, :, :], ALU.add).then_inc(dt_ready.sem, 1)
                    pool.wait_ge(dt_ready.sem, dt_ready.done(b))
                    pool.wait_ge(uc_ready.sem, uc_ready.done(b))
                    pool.wait_ge(dbu_ready.sem, dbu_ready.done(IC * (b - 2) + IC - 1))
                    pool.tensor_tensor(dtu[:, j], dt[:, j], uc[:, j], ALU.mult).then_inc(dtu_ready.sem, 1)

                def unit(b, j, first, last):
                    if not last:
                        f.fetch(pool, b + 1, 1 - j)
                    for m in range(IC):
                        if m == 0:
                            pool.wait_ge(dtu_ready.sem, dtu_ready.done(b))
                            pool.wait_ge(bc_ready.sem, bc_ready.done(BCN * b + BCN - 1))
                        pool.wait_ge(scanned.sem, scanned.freed(IC * b + m))
                        pool.tensor_tensor(dbu[:, m % 2], dtu[:, j, m, :].unsqueeze(1).broadcast_to([P, N, P]),
                                           bc[:, j, 0:N, :], ALU.mult).then_inc(dbu_ready.sem, 1)
                        if m == 2 and not first:
                            f.rstd_out(pool, b - 1, 1 - j)
                    if not last:
                        front(b + 1, 1 - j)
                    else:
                        f.rstd_out(pool, b, j)

                f.fetch(pool, 0, 0)
                front(0, 0)
                every_sequence(pool, unit)

            @block.tensor
            def _(pe):
                def turn(b, j):
                    pe.wait_ge(f.x_in_ready.sem, f.x_in_ready.done(b))
                    pe.wait_ge(f.out_used.sem, f.out_used.freed(b))
                    for cc in range(DC):
                        last = pe.transpose(f.xT_ps[:, cc, :], f.x_in[:, j, cc * P:(cc + 1) * P], core.ident[:, :])
                    last.then_inc(f.xT_turned.sem, 1)

                def front(b, j):
                    pe.wait_ge(f.xT_ready.sem, f.xT_ready.done(b))
                    for half, (bank, used, made) in enumerate(((u_ps, u_ready, u_made), (z_ps, sz_ready, z_made))):
                        pe.wait_ge(used.sem, used.freed(b, 1))
                        for m in range(IC):
                            col = half * INNER + m * P
                            for cc in range(DC):
                                last = pe.matmul(bank[:, m, :], w_in_sb[:, cc, col:col + P], f.xT[:, j, cc, :],
                                                 start=(cc == 0), stop=(cc == DC - 1))
                        last.then_inc(made.sem, 1)
                    pe.wait_ge(u_ready.sem, u_ready.done(b))
                    pe.wait_ge(xd_ready.sem, xd_ready.freed(b, 1))
                    for m in range(IC):
                        for k in range(K):
                            last = pe.matmul(v_ps[:, m, :], taps[:, m, k, :], u[:, 0, m, k:k + P],
                                             start=(k == 0), stop=(k == K - 1))
                    last.then_inc(conv_made.sem, 1)
                    pe.wait_ge(uc_ready.sem, uc_ready.done(b))
                    for m in range(IC):
                        last = pe.matmul(v_ps[0:XD, 0, :], w_x_sb[:, m, :], uc[:, j, m, :],
                                         start=(m == 0), stop=(m == IC - 1))
                    last.then_inc(xd_made.sem, 1)
                    pe.wait_ge(xd_ready.sem, xd_ready.done(b))
                    pe.wait_ge(pre_ready.sem, pre_ready.freed(b, 1))
                    for m in range(IC):
                        last = pe.matmul(dt_ps[:, m, :], w_dt_sb[:, m * P:(m + 1) * P], xd[0:R, j, :],
                                         start=True, stop=True)
                    last.then_inc(dt_made.sem, 1)
                    for q in range(BCN):
                        pe.wait_ge(bc_ready.sem, bc_ready.freed(BCN * b + q))
                        for r in range(IC):
                            row = R + IC * q + r
                            last = pe.matmul(bc_ps[q % 2][:, r, :], core.ident[0:XD, row:row + 1].broadcast_to([XD, P]),
                                             xd[:, j, :], start=True, stop=True)
                        last.then_inc(bc_made.sem, 1)

                def sum_states(b, j, m):
                    if m == 0:
                        pe.wait_ge(yT_ready.sem, yT_ready.freed(b, 1))
                    pe.wait_ge(hc_ready.sem, hc_ready.done(IC * b + m))
                    pe.matmul(y_ps[:, m, :], skip[:, m, :], uc[:, j, m, :], start=True, stop=False)
                    for n in range(N):
                        last = pe.matmul(y_ps[:, m, :], core.ident[:, :], hc[:, m % 2, n, :], start=False,
                                         stop=(n == N - 1))
                    last.then_inc(y_summed.sem, 1)

                def out(b, j, turned):
                    pe.wait_ge(yT_ready.sem, yT_ready.done(b))
                    pe.wait_ge(f.xT_ready.sem, f.xT_ready.done(turned))
                    pe.wait_ge(f.out_used.sem, f.out_used.freed(b, 1))
                    for m in range(IC):
                        last = pe.matmul(f.out_ps, yT[:, j, m, :], w_out_sb[:, m, :], start=(m == 0), stop=(m == IC - 1))
                    last.then_inc(f.out_ready.sem, 1)

                def unit(b, j, first, last):
                    sum_states(b, j, 0)
                    if not first:
                        out(b - 1, 1 - j, b)
                    if not last:
                        turn(b + 1, 1 - j)
                    sum_states(b, j, 1)
                    if not last:
                        front(b + 1, 1 - j)
                    sum_states(b, j, 2)
                    sum_states(b, j, 3)
                    if last:
                        out(b, j, b)

                pe.wait_ge(loads.sem, weights)
                pe.wait_ge(prep.sem, prep.done(1))
                turn(0, 0)
                front(0, 0)
                every_sequence(pe, unit)

            @block.scalar
            def _(act):
                def front(b, j):
                    act.wait_ge(f.xT_turned.sem, f.xT_turned.done(b))
                    act.wait_ge(z_made.sem, z_made.freed(b))
                    act.activation(f.xT[:, j], f.xT_ps, ACT.Copy).then_inc(f.xT_ready.sem, 1)
                    act.wait_ge(u_made.sem, u_made.done(b))
                    act.wait_ge(conv_made.sem, conv_made.freed(b, 1))
                    act.activation(u[:, 0, :, K - 1:], u_ps[:, :, :], ACT.Copy).then_inc(u_ready.sem, 1)
                    act.wait_ge(z_made.sem, z_made.done(b))
                    act.wait_ge(yT_ready.sem, yT_ready.freed(b))
                    act.activation(sz[:, j], z_ps[:, :, :], ACT.Silu).then_inc(sz_ready.sem, 1)
                    act.wait_ge(conv_made.sem, conv_made.done(b))
                    act.wait_ge(y_summed.sem, y_summed.done(IC * (b - 2) + IC - 1))
                    for m in range(IC):
                        last = act.activation(uc[:, j, m, :], v_ps[:, m, :], ACT.Silu, bias=conv_b_sb[:, m:m + 1])
                    last.then_inc(uc_ready.sem, 1)
                    act.wait_ge(xd_made.sem, xd_made.done(b))
                    act.wait_ge(bc_made.sem, bc_made.done(BCN * (b - 2) + BCN - 1))
                    act.activation(xd[:, j, :], v_ps[0:XD, 0, :], ACT.Copy).then_inc(xd_ready.sem, 1)
                    act.wait_ge(dt_made.sem, dt_made.done(b))
                    act.wait_ge(dt_ready.sem, dt_ready.freed(b, 1))
                    for m in range(IC):
                        last = act.activation(pre[:, m, :], dt_ps[:, m, :], ACT.Identity, bias=b_dt_sb[:, m:m + 1])
                    last.then_inc(pre_ready.sem, 1)
                    act.wait_ge(pre_ready.sem, pre_ready.done(b))
                    act.activation(low[:, :, :], pre[:, :, :], ACT.Abs).then_inc(abs_done.sem, 1)
                    act.wait_ge(abs_done.sem, abs_done.done(b))
                    act.activation(low[:, :, :], low[:, :, :], ACT.Exp, scale=-1.0).then_inc(dexp_done.sem, 1)
                    act.wait_ge(dexp_done.sem, dexp_done.done(b))
                    act.activation(low[:, :, :], low[:, :, :], ACT.Ln, bias=1.0).then_inc(low_ready.sem, 1)
                    act.wait_ge(hc_ready.sem, hc_ready.done(IC * (b - 2) + IC - 1))
                    for q in range(BCN):
                        act.wait_ge(bc_made.sem, bc_made.done(BCN * b + q))
                        act.activation(bc[:, j, IC * q:IC * (q + 1), :], bc_ps[q % 2][:, :, :], ACT.Copy
                                       ).then_inc(bc_ready.sem, 1)

                def unit(b, j, first, last_unit):
                    act.wait_ge(dt_ready.sem, dt_ready.done(b))
                    for m in range(IC):
                        act.wait_ge(scanned.sem, scanned.freed(IC * b + m))
                        for n in range(N):
                            last = act.activation(da[:, m % 2, n, 1:P], dt[:, j, m, 1:P], ACT.Exp,
                                                  scale=a_sb[:, m, n:n + 1])
                        last.then_inc(da_ready.sem, 1)
                    if not last_unit:
                        front(b + 1, 1 - j)

                act.wait_ge(loads.sem, weights)
                act.wait_ge(consts.sem, consts.done(0))
                act.activation(a_sb[:, :, :], a_sb[:, :, :], ACT.Exp).then_inc(prep_a.sem, 1)
                act.wait_ge(prep.sem, prep.done(2))
                front(0, 0)
                every_sequence(act, unit)

            @block.vector
            def _(dve):
                dve.wait_ge(loads.sem, weights)
                for m in range(IC):
                    for k in range(K):
                        last = dve.tensor_scalar(taps[:, m, k, :], core.ident[:, :], taps_w[:, m, k:k + 1], None, ALU.mult)
                last.then_inc(prep.sem, 1)
                for m in range(IC):
                    last = dve.tensor_scalar(skip[:, m, :], core.ident[:, :], d_sb[:, m:m + 1], None, ALU.mult)
                last.then_inc(prep.sem, 1)
                dve.wait_ge(prep_a.sem, prep_a.done(0))
                dve.tensor_scalar(a_sb[:, :, :], a_sb[:, :, :], -1.0, None, ALU.mult).then_inc(prep.sem, 1)

                def gate(b, j):
                    dve.wait_ge(y_summed.sem, y_summed.done(IC * b + IC - 1))
                    dve.wait_ge(sz_ready.sem, sz_ready.done(b))
                    dve.wait_ge(f.out_ready.sem, f.out_ready.freed(b))
                    dve.tensor_tensor(yT[:, j], y_ps[:, :, :], sz[:, j], ALU.mult).then_inc(yT_ready.sem, 1)

                def unit(b, j, first, last):
                    flat = lambda t: t.rearrange("p n t -> p (n t)")
                    for m in range(IC):
                        g = IC * b + m
                        dve.wait_ge(da_ready.sem, da_ready.done(g))
                        dve.wait_ge(dbu_ready.sem, dbu_ready.done(g))
                        dve.wait_ge(hc_ready.sem, hc_ready.freed(g, 1))
                        dve.tensor_tensor_scan(flat(h[:, :, :]), flat(da[:, m % 2]), flat(dbu[:, m % 2]), 0.0,
                                               ALU.mult, ALU.add).then_inc(scanned.sem, 1)
                        if m == 0 and not first:
                            gate(b - 1, 1 - j)
                        dve.wait_ge(scanned.sem, scanned.done(g))
                        dve.wait_ge(y_summed.sem, y_summed.freed(g))
                        dve.tensor_tensor(hc[:, m % 2], h[:, :, :], bc[:, j, N:2 * N, :], ALU.mult
                                          ).then_inc(hc_ready.sem, 1)
                        if m == 2 and not first:
                            f.finish(dve, b - 1, 1 - j)
                        if m == 3 and not first:
                            f.save_normed(dve, b - 1, 1 - j)
                    if last:
                        gate(b, j)
                        f.finish(dve, b, j)
                        f.save_normed(dve, b, j)

                every_sequence(dve, unit)
        for n in per_b:
            n.advance(B)
        for n in (bc_made, bc_ready):
            n.advance(B * BCN)
        for n in (da_ready, dbu_ready, scanned, hc_ready, y_summed):
            n.advance(B * IC)
        loads.advance(16 * len(plain))
        consts.advance(1)
        prep.advance(3)
        prep_a.advance(1)
        f.end()



COUNTS = (
    "x_in_ready", "xT_turned", "xT_ready", "xres_ready", "out_ready", "out_used", "y_stats", "y_mv", "y_var",
    "y_rstd", "x_saved", "waits_passed", "in_stats_done", "in_mv_done", "in_var_done", "in_rstd_done",
    "z_scaled_done", "y_ready", "pre_stats_done", "pre_mv_done", "pre_var_done", "pre_rstd_done", "h_ready",
    "gate_ready", "up_ready", "silu_done", "hT_ready", "bank_a_made", "bank_a_taken", "bank_b_made",
    "bank_b_taken", "scored", "biased_done", "max_done", "negmax_done", "exp_done", "p_turned", "weighed",
    "pT_even_ready", "pT_odd_ready", "inv_ready", "a_ready", "max_all", "null_arg", "tot_ready", "null_v_ready",
    "o_summed", "c_spread", "c_v_copied", "pads_zeroed", "constants_made", "table_made", "c_landed0", "c_landed1",
    "v_raw", "q_made", "k_made", "v_made", "q_maxed", "q_lowered", "q_exped", "q_summed", "q_inverted", "q_ready",
    "q_turned", "qT_ready", "k_maxed", "k_negated", "k_exped", "k_inverted", "k_turned", "k_ready", "v_ready",
    "c_made", "blocks_ready", "a_made", "aT_ready", "g_made", "s_ready", "best_found", "which_found", "which_cast",
    "lowered", "exped", "picked", "picked2", "summed", "inverted", "weighted", "chosen", "hT_kept", "upped",
    "gate_made", "silued", "hid_ready", "downed", "added", "acc_cleared", "expert_landed0", "expert_landed1",
    "w_picked", "prep_done", "prep_products", "prep_copied", "prep_hits", "squared_x", "squared", "ms1_done",
    "ms2_done", "rs_ready", "u_ready", "spread_ready", "prep_pool", "n_stats_done", "n_mv_done", "n_var_done",
    "n_rstd_done", "centred_done", "scaled_done", "xn_done", "mag_done", "largest_done", "xs_done", "u_made",
    "z_made", "conv_made", "uc_ready", "sz_ready", "xd_made", "xd_ready", "dt_made", "pre_ready", "abs_done",
    "dexp_done", "low_ready", "relu_done", "dt_ready", "dtu_ready", "yT_ready", "bc_made", "bc_ready", "da_ready",
    "dbu_ready", "scanned", "hc_ready", "y_summed", "prep_a",
)


def build(nc, a, out):
    with ExitStack() as ctx:
        core = Core(nc, ctx)
        for name in COUNTS:
            core.count(name)
        setup_stage(core)
        load_stage(core, a["x"])
        mamba_stage(core, a["L0_attn_W_in"], a["L0_attn_conv_w"], a["L0_attn_conv_b"], a["L0_attn_W_x"],
                    a["L0_attn_W_dt"], a["L0_attn_b_dt"], a["L0_attn_A_log"], a["L0_attn_D"], a["L0_attn_W_out"])
        depool_stage(core, a["ctx_2048"], a["mask_BxS2_if0"], a["decay"], a["upto"], a["L0_xattn_W_in"],
                     a["L0_xattn_b_in"], a["L0_xattn_g_res"], a["L0_xattn_g_init"])
        ternary_stage(core, a["L0_ffn_weight"], a["L0_ffn_ln_gamma"], a["L0_ffn_ln_beta"])
        linear_attention_stage(core, a["L1_attn_Wq"], a["L1_attn_Wk"], a["L1_attn_Wv"], a["L1_attn_Wo"],
                               a["L1_attn_bo"])
        self_attention_stage(core, a["L1_xattn_w_qkv"][:, 0:D], a["L1_xattn_w_qkv"][:, D:2 * D],
                             a["L1_xattn_w_qkv"][:, 2 * D:], a["L1_xattn_w_proj"],
                             out_bias=a["L1_xattn_b_proj"], context=a["ctx_2048"])
        with ExitStack() as moe:
            x1 = moe.enter_context(nc.sbuf_tensor(core.named("x1"), [P, B, D], F32))
            self_attention_stage(core, a["L1_ffn_wq"], a["L1_ffn_wk"], a["L1_ffn_wv"], a["L1_ffn_wo"],
                                 out_bias=a["L1_ffn_bo"], causal=True, target=x1, norm=False,
                                 pre_norm=(a["L1_ffn_ln1_scale"], a["L1_ffn_ln1_shift"]))
            hT_all = moe.enter_context(nc.sbuf_tensor(core.named("hT_all"), [P, DC, B, P], F32))
            weight_all = moe.enter_context(nc.sbuf_tensor(core.named("weight_all"), [P, 8, B, 1], F32))
            acc = moe.enter_context(nc.sbuf_tensor(core.named("acc"), [P, B, D], F32))
            gate_stage(core, hT_all, weight_all, a["L1_ffn_gate_w"], 8, 2, a["L1_ffn_ln2_scale"],
                       a["L1_ffn_ln2_shift"], x_from=x1)
            expert_stage(core, hT_all, weight_all, acc, a["L1_ffn_w2"], a["L1_ffn_w3"], w_gate=a["L1_ffn_w1"])
            merge_stage(core, acc, residual=x1)
        w = a["L2_attn_W_qkv"]
        self_attention_stage(core, w[:, 0:D], w[:, D:2 * D], w[:, 2 * D:], a["L2_attn_W_out"],
                             qkv_bias=(a["L2_attn_bq"], a["L2_attn_bk"], a["L2_attn_bv"]), out_bias=a["L2_attn_b_out"],
                             alibi=True)
        wide_context_stage(core, a["ctx_2048"], a["L2_xattn_Wq"], a["L2_xattn_Wkv"], a["L2_xattn_null_kv"],
                           a["L2_xattn_Wout"], a["L2_xattn_ln_scale"], a["L2_xattn_ln_bias"])
        with ExitStack() as moe:
            hT_all = moe.enter_context(nc.sbuf_tensor(core.named("hT_all"), [P, DC, B, P], F32))
            weight_all = moe.enter_context(nc.sbuf_tensor(core.named("weight_all"), [P, 8, B, 1], F32))
            acc = moe.enter_context(nc.sbuf_tensor(core.named("acc"), [P, B, D], F32))
            gate_stage(core, hT_all, weight_all, a["L2_ffn_gate_w"], 8, 1)
            expert_stage(core, hT_all, weight_all, acc, a["L2_ffn_w1"], a["L2_ffn_w2"], b_up=a["L2_ffn_b1"])
            merge_stage(core, acc, weight_all=weight_all, bias=a["L2_ffn_b2"])
        self_attention_stage(core, a["L3_attn_Wq"], a["L3_attn_Wk"], a["L3_attn_Wv"], a["L3_attn_Wo"],
                             qkv_bias=(a["L3_attn_bq"], a["L3_attn_bk"], a["L3_attn_bv"]),
                             out_bias=a["L3_attn_bo"], causal=True)
        masked_context_stage(core, a["ctx_2048"], a["mask_BxS2_fk1"], a["mask_cols"], a["L3_xattn_W_src"],
                             a["L3_xattn_b_src_k"], a["L3_xattn_b_src_v"], a["L3_xattn_W_tgt"],
                             a["L3_xattn_b_tgt"], a["L3_xattn_W_out"], a["L3_xattn_b_out"])
        int_mlp_stage(core, a["L3_ffn_w_gate"], a["L3_ffn_w_up"], a["L3_ffn_w_down"])
        store_stage(core, out)


TURNED = ("L0_attn_W_in", "L0_attn_W_x", "L0_attn_W_dt", "L0_attn_W_out", "L0_xattn_W_in", "L2_ffn_gate_w", "L3_xattn_W_src", "L3_xattn_W_tgt", "L3_xattn_W_out", "L1_xattn_w_qkv", "L1_xattn_w_proj", "L2_attn_W_qkv", "L2_attn_W_out", "L3_ffn_w_gate", "L3_ffn_w_up", "L3_ffn_w_down")


COLUMNS = ("L0_attn_conv_b", "L0_attn_b_dt", "L0_attn_D", "L0_xattn_g_res", "L3_xattn_b_src_k", "L3_xattn_b_tgt", "L1_ffn_ln1_scale", "L1_ffn_ln1_shift", "L1_ffn_ln2_scale", "L1_ffn_ln2_shift")

HEADWISE = ("L3_attn_Wq", "L3_attn_Wk", "L3_attn_Wv")


def columns(v, rows):
    return v.reshape(-1, rows).T


def laid_out(inputs):
    a = {name: np.asarray(v) for name, v in inputs.items()}
    for name in TURNED:
        a[name] = a[name].T
    for name in HEADWISE:
        a[name] = a[name].transpose(1, 0, 2).reshape(D, -1)
    qkv = a.pop("L2_attn_b_qkv")
    a["L2_attn_bq"], a["L2_attn_bk"], a["L2_attn_bv"] = columns(qkv[:D], 64), columns(qkv[D:2 * D], 64), qkv[2 * D:]
    a["L3_attn_bq"], a["L3_attn_bk"] = columns(a["L3_attn_bq"], 64), columns(a["L3_attn_bk"], 64)
    a["L3_attn_bv"] = a["L3_attn_bv"].reshape(-1)
    a["mask_cols"] = a["mask_BxS2_fk1"].T
    src = a.pop("L3_xattn_b_src")
    a["L3_xattn_b_src_k"], a["L3_xattn_b_src_v"] = src[:D], src[D:]
    b1 = a["L2_ffn_b1"]
    a["L2_ffn_b1"] = b1.reshape(b1.shape[0], -1, P).transpose(0, 2, 1)
    a["decay"] = depool_constants()[0]
    a["upto"] = np.triu(np.ones((P, P), np.float32))
    for name in ("L0_attn_conv_w", "L0_attn_A_log"):
        a[name] = a[name].reshape(-1, P, a[name].shape[1]).transpose(1, 0, 2)
    for name in COLUMNS:
        a[name] = columns(a[name], P)
    return {name: np.ascontiguousarray(v) for name, v in a.items()}


def kernel(**inputs):
    import concourse.bacc as bacc
    from concourse.bass_utils import run_bass_kernel_spmd

    nc = bacc.Bacc("TRN2", target_bir_lowering=False, num_devices=1)
    arrays, args = {}, {}
    for name, value in laid_out(inputs).items():
        arrays[f"in_{name}"] = value
        args[name] = nc.dram_tensor(f"in_{name}", value.shape, mybir.dt.from_np(value.dtype),
                                    kind="ExternalInput").ap()
    out = nc.dram_tensor("out", (B, P, D), F32, kind="ExternalOutput").ap()
    build(nc, args, out)
    return run_bass_kernel_spmd(nc, [arrays], core_ids=[0]).results[0]["out"]
```

```python
from contextlib import ExitStack

import numpy as np

import concourse.bass as bass
from concourse import mybir

ALU = mybir.AluOpType
ACT = mybir.ActivationFunctionType
AX = mybir.AxisListType
F32 = mybir.dt.float32
BF16 = mybir.dt.bfloat16
I32 = mybir.dt.int32
U32 = mybir.dt.uint32

P = 128
B = 16
D = 256
DC = D // P
CTX = 512
CC = CTX // P
LN_EPS = 1e-5
MASKED = -1e30


class Count:

    START = 24

    def __init__(self, sem):
        self.sem, self.base = sem, self.START

    def done(self, item):
        return self.base + item + 1

    def freed(self, item, deep=2):
        return self.base + item + 1 - deep

    def advance(self, items):
        self.base += items


class Core:

    def __init__(self, nc, ctx):
        self.nc, self.ctx = nc, ctx
        self.x = ctx.enter_context(nc.sbuf_tensor("x", [P, B, D], F32))
        self.ident = ctx.enter_context(nc.sbuf_tensor("ident", [P, P], F32))
        self.ident_bf = ctx.enter_context(nc.sbuf_tensor("ident_bf", [P, P], BF16))
        self.ones = ctx.enter_context(nc.sbuf_tensor("ones", [P, P], F32))
        self.ln_eps = ctx.enter_context(nc.sbuf_tensor("ln_eps", [P, 1], F32))
        self.minus_half = ctx.enter_context(nc.sbuf_tensor("minus_half", [P, 1], F32))
        self.counts, self.names = {}, {}
        self.loads = Count(ctx.enter_context(nc.semaphore("loads_landed")))
        self.loads.base = 0
        self.setup = Count(ctx.enter_context(nc.semaphore("setup_done")))
        self.setup.base = 0

    def named(self, name):
        self.names[name] = self.names.get(name, 0) + 1
        return f"{name}_{self.names[name]}"

    def count(self, name):
        if name not in self.counts:
            self.counts[name] = Count(self.ctx.enter_context(self.nc.semaphore(name)))
        return self.counts[name]


def chunked(w, rows=P):
    return w.rearrange("(c p) n -> p c n", p=rows)


def row_everywhere(v, parts=P):
    return v.rearrange("(o n) -> o n", o=1).broadcast_to([parts, v.shape[0]])



class Frame:

    def __init__(self, core, ctx, pre_norm=False, out_bias=None, target=None, norm=True,
                 inner_norm=None, own_input=False, feeds_only=False, out_scale=None,
                 ahead=False, rotated=False):
        nc = core.nc
        self.core, self.nc = core, nc
        self.target = target if target is not None else core.x
        self.pre_norm, self.out_bias, self.norm = pre_norm, out_bias, norm
        self.ahead, self.rotated = ahead, rotated
        self.own_input, self.feeds_only, self.out_scale = own_input, feeds_only, out_scale
        self.inner_norm = inner_norm
        sb = lambda n, s, t=F32: ctx.enter_context(nc.sbuf_tensor(core.named(n), s, t))
        self.x_in = sb("x_in", [P, 2, D])
        self.xT = sb("xT", [P, 2, DC, P])
        self.y = sb("y", [P, 2, D])
        self.stats = sb("stats", [P, 2, 6])
        self.mv = sb("mv", [P, 2, 2])
        self.var_eps = sb("var_eps", [P, 2, 1])
        self.rstd = sb("rstd", [P, 2, 1])
        self.xres = sb("xres", [P, 2, D]) if out_bias is not None else self.x_in
        self.residual_from_x = ahead or rotated and out_bias is None
        if own_input:
            self.h_in = sb("h_in", [P, 2, D])
        if pre_norm:
            self.pre_stats = sb("pre_stats", [P, 2, 6])
            self.pre_mv = sb("pre_mv", [P, 2, 2])
            self.pre_var = sb("pre_var", [P, 2, 1])
            self.pre_rstd = sb("pre_rstd", [P, 2, 1])
            self.h_in = sb("h_in", [P, 2, D])
        self.bank = ctx.enter_context(nc.psum_tensor(core.named("frame_bank"), [P, 2, D], F32))
        if inner_norm is not None:
            self.in_stats, self.in_mv = sb("in_stats", [P, 2, 6]), sb("in_mv", [P, 2, 2])
            self.in_var, self.in_rstd = sb("in_var", [P, 2, 1]), sb("in_rstd", [P, 2, 1])
            self.inner_eps = sb("inner_eps", [P, 1])
            self.z, self.z_scaled = sb("z", [P, 2, D]), sb("z_scaled", [P, 2, D])
        self.xT_ps = self.bank[:, 0, :].rearrange("p (c t) -> p c t", c=DC)
        self.out_ps = self.bank[:, 1, :]
        c = core.count
        self.x_in_ready, self.xT_turned, self.xT_ready = c("x_in_ready"), c("xT_turned"), c("xT_ready")
        self.xres_ready = c("xres_ready")
        self.out_ready, self.out_used = c("out_ready"), c("out_used")
        self.y_stats, self.y_mv, self.y_var, self.y_rstd, self.x_saved = (
            c("y_stats"), c("y_mv"), c("y_var"), c("y_rstd"), c("x_saved"))
        self.passed = c("waits_passed")
        self.inner = [c("in_stats_done"), c("in_mv_done"), c("in_var_done"), c("in_rstd_done"), c("z_scaled_done"),
                      c("y_ready")]
        self.pre = [c("pre_stats_done"), c("pre_mv_done"), c("pre_var_done"), c("pre_rstd_done"), c("h_ready")]

    def end(self):
        if self.feeds_only:
            for c in [self.x_in_ready, self.xT_turned, self.xT_ready] + (self.pre if self.pre_norm else []):
                c.advance(B)
            return
        if self.own_input:
            self.pre[4].advance(B)
        for c in (self.x_in_ready, self.xT_turned, self.xT_ready, self.out_ready, self.out_used, self.x_saved):
            c.advance(B)
        if self.norm:
            for c in (self.y_stats, self.y_mv, self.y_var, self.y_rstd):
                c.advance(B)
        if self.out_bias is not None:
            self.xres_ready.advance(B)
        if self.inner_norm is not None:
            for c in self.inner:
                c.advance(B)
        if self.pre_norm:
            for c in self.pre:
                c.advance(B)

    def fetch(self, pool, b, j, source=None):
        through = self.xT_turned if self.feeds_only or self.ahead or self.rotated else self.x_saved
        pool.wait_ge(through.sem, through.freed(b))
        source = self.core.x if source is None else source
        pool.tensor_copy(self.x_in[:, j, :], source[:, b, :]).then_inc(self.x_in_ready.sem, 1)
        if self.out_bias is not None and not self.rotated:
            pool.wait_ge(self.x_in_ready.sem, self.x_in_ready.done(b))
            bias = self.out_bias(b) if callable(self.out_bias) else self.out_bias
            pool.tensor_tensor(self.xres[:, j, :], self.x_in[:, j, :], bias, ALU.add
                               ).then_inc(self.xres_ready.sem, 1)
        if self.pre_norm:
            _, mv, var, rstd, _ = self.pre
            pool.wait_ge(mv.sem, mv.done(b))
            pool.tensor_tensor(self.pre_var[:, j, :], self.pre_mv[:, j, 1:2], self.core.ln_eps[:, :], ALU.add
                               ).then_inc(var.sem, 1)
            pool.wait_ge(var.sem, var.done(b))
            pool.tensor_tensor(self.pre_rstd[:, j, :], self.pre_var[:, j, :], self.core.minus_half[:, :], ALU.pow
                               ).then_inc(rstd.sem, 1)

    def bias_residual(self, pool, b, j):
        pool.wait_ge(self.x_saved.sem, self.x_saved.freed(b))
        pool.sem_inc(self.passed.sem, 1)
        pool.tensor_tensor(self.xres[:, j, :], self.core.x[:, b, :], self.out_bias, ALU.add
                           ).then_inc(self.xres_ready.sem, 1)

    def normalise_in(self, dve, b, j):
        if not self.pre_norm:
            return
        stats, mv, _, rstd, h = self.pre
        dve.wait_ge(self.x_in_ready.sem, self.x_in_ready.done(b))
        dve.bn_stats(self.pre_stats[:, j, :], self.x_in[:, j, :]).then_inc(stats.sem, 1)
        dve.wait_ge(stats.sem, stats.done(b))
        dve.sem_inc(self.passed.sem, 1)
        dve.bn_aggr(self.pre_mv[:, j, :], self.pre_stats[:, j, :]).then_inc(mv.sem, 1)
        dve.wait_ge(rstd.sem, rstd.done(b))
        dve.wait_ge(mv.sem, mv.done(b))
        dve.wait_ge(self.xT_turned.sem, self.xT_turned.freed(b))
        dve.tensor_scalar(self.h_in[:, j, :], self.x_in[:, j, :], self.pre_mv[:, j, 0:1], self.pre_rstd[:, j, :],
                          ALU.subtract, ALU.mult).then_inc(h.sem, 1)

    def turn(self, pe, b, j):
        own = self.pre_norm or self.own_input
        src = self.h_in if own else self.x_in
        ready = self.pre[4] if own else self.x_in_ready
        pe.wait_ge(ready.sem, ready.done(b))
        if self.feeds_only:
            pe.wait_ge(self.xT_ready.sem, self.xT_ready.freed(b, 1))
        elif self.rotated:
            pe.wait_ge(self.out_used.sem, self.out_used.freed(b))
        elif j == 0:
            pe.wait_ge(self.out_used.sem, self.out_used.freed(b, 1))
        else:
            pe.wait_ge(self.xT_ready.sem, self.xT_ready.done(b - 1))
        for c in range(DC):
            last = pe.transpose(self.xT_ps[:, c, :], src[:, j, c * P:(c + 1) * P], self.core.ident[:, :])
        last.then_inc(self.xT_turned.sem, 1)

    def claim_bank(self, pe, b, j, last=False):
        if self.rotated:
            turned = b if last and j == 1 else b + 1
            pe.wait_ge(self.xT_ready.sem, self.xT_ready.done(turned))
            pe.wait_ge(self.out_used.sem, self.out_used.freed(b, 1))
        elif j == 0:
            pe.wait_ge(self.xT_ready.sem, self.xT_ready.done(b + 1))
        else:
            pe.wait_ge(self.out_used.sem, self.out_used.done(b - 1))

    def copy_turned(self, act, b, j, scale=None, shift=None):
        act.wait_ge(self.xT_turned.sem, self.xT_turned.done(b))
        if not self.feeds_only:
            act.wait_ge(self.out_ready.sem, self.out_ready.freed(b))
        out = self.xT[:, j]
        if scale is None:
            last = act.activation(out, self.xT_ps, ACT.Copy)
        else:
            for c in range(DC):
                last = act.activation(out[:, c, :], self.xT_ps[:, c, :], ACT.Identity,
                                      bias=0.0 if shift is None else shift[:, c:c + 1],
                                      scale=scale[:, c:c + 1])
        last.then_inc(self.xT_ready.sem, 1)

    def finish(self, dve, b, j, result=None):
        dve.wait_ge(self.out_ready.sem, self.out_ready.done(b))
        if self.out_bias is not None:
            dve.wait_ge(self.xres_ready.sem, self.xres_ready.done(b))
        elif not self.rotated:
            dve.wait_ge(self.x_in_ready.sem, self.x_in_ready.done(b))
        src = self.out_ps if result is None else result
        if self.inner_norm is not None:
            stats, mv, _, rstd, scaled, y_ready = self.inner
            dve.bn_stats(self.in_stats[:, j, :], src).then_inc(stats.sem, 1)
            dve.wait_ge(stats.sem, stats.done(b))
            dve.sem_inc(self.passed.sem, 1)
            dve.bn_aggr(self.in_mv[:, j, :], self.in_stats[:, j, :]).then_inc(mv.sem, 1)
            return
        if not self.norm:
            residual = self.core.x[:, b, :] if self.residual_from_x else self.xres[:, j, :]
            dve.tensor_tensor(self.target[:, b, :], src, residual, ALU.add
                              ).then_inc(self.out_used.sem, 1)
            dve.wait_ge(self.out_used.sem, self.out_used.done(b))
            dve.sem_inc(self.x_saved.sem, 1)
            return
        if self.out_scale is not None:
            dve.scalar_tensor_tensor(out=self.y[:, j, :], in0=src, scalar=self.out_scale, in1=self.xres[:, j, :],
                                     op0=ALU.mult, op1=ALU.add).then_inc(self.out_used.sem, 1)
        else:
            residual = self.core.x[:, b, :] if self.residual_from_x else self.xres[:, j, :]
            dve.tensor_tensor(self.y[:, j, :], src, residual, ALU.add).then_inc(self.out_used.sem, 1)
        dve.wait_ge(self.out_used.sem, self.out_used.done(b))
        self.layernorm(dve, b, j)

    def finish_inner(self, dve, b, j):
        _, mv, _, rstd, scaled, y_ready = self.inner
        dve.wait_ge(mv.sem, mv.done(b))
        dve.wait_ge(rstd.sem, rstd.done(b))
        dve.tensor_scalar(self.z[:, j, :], self.out_ps, self.in_mv[:, j, 0:1], self.in_rstd[:, j, :],
                          ALU.subtract, ALU.mult).then_inc(self.out_used.sem, 1)
        dve.wait_ge(self.out_used.sem, self.out_used.done(b))
        dve.tensor_tensor(self.z_scaled[:, j, :], self.z[:, j, :], self.inner_norm, ALU.mult
                          ).then_inc(scaled.sem, 1)
        dve.wait_ge(scaled.sem, scaled.done(b))
        dve.tensor_tensor(self.y[:, j, :], self.z_scaled[:, j, :], self.xres[:, j, :], ALU.add
                          ).then_inc(y_ready.sem, 1)
        dve.wait_ge(y_ready.sem, y_ready.done(b))
        self.layernorm(dve, b, j)

    def layernorm(self, dve, b, j):
        dve.bn_stats(self.stats[:, j, :], self.y[:, j, :]).then_inc(self.y_stats.sem, 1)
        dve.wait_ge(self.y_stats.sem, self.y_stats.done(b))
        dve.sem_inc(self.passed.sem, 1)
        dve.bn_aggr(self.mv[:, j, :], self.stats[:, j, :]).then_inc(self.y_mv.sem, 1)

    def rstd_inner(self, pool, b, j):
        _, mv, var, rstd, _, _ = self.inner
        pool.wait_ge(mv.sem, mv.done(b))
        pool.tensor_tensor(self.in_var[:, j, :], self.in_mv[:, j, 1:2], self.inner_eps[:, :], ALU.add
                           ).then_inc(var.sem, 1)
        pool.wait_ge(var.sem, var.done(b))
        pool.tensor_tensor(self.in_rstd[:, j, :], self.in_var[:, j, :], self.core.minus_half[:, :], ALU.pow
                           ).then_inc(rstd.sem, 1)

    def rstd_out(self, pool, b, j):
        pool.wait_ge(self.y_mv.sem, self.y_mv.done(b))
        pool.tensor_tensor(self.var_eps[:, j, :], self.mv[:, j, 1:2], self.core.ln_eps[:, :], ALU.add
                           ).then_inc(self.y_var.sem, 1)
        pool.wait_ge(self.y_var.sem, self.y_var.done(b))
        pool.tensor_tensor(self.rstd[:, j, :], self.var_eps[:, j, :], self.core.minus_half[:, :], ALU.pow
                           ).then_inc(self.y_rstd.sem, 1)

    def save_normed(self, dve, b, j):
        dve.wait_ge(self.y_rstd.sem, self.y_rstd.done(b))
        dve.wait_ge(self.y_mv.sem, self.y_mv.done(b))
        dve.tensor_scalar(self.target[:, b, :], self.y[:, j, :], self.mv[:, j, 0:1], self.rstd[:, j, :],
                          ALU.subtract, ALU.mult).then_inc(self.x_saved.sem, 1)


def setup_stage(core):
    nc = core.nc
    n = core.setup
    with nc.Block() as block:
        @block.gpsimd
        def _(pool):
            for c in core.counts.values():
                pool.sem_inc(c.sem, Count.START)
            pool.memset(core.ident[:, :], 0.0).then_inc(n.sem, 1)
            pool.memset(core.ones[:, :], 1.0).then_inc(n.sem, 1)
            pool.memset(core.minus_half[:, :], -0.5).then_inc(n.sem, 1)
            pool.memset(core.ln_eps[:, :], LN_EPS).then_inc(n.sem, 1)
            pool.wait_ge(n.sem, 4)
            pool.affine_select(out=core.ident[:, :], in_=core.ident[:, :], compare_op=ALU.not_equal, fill=1.0,
                               base=0, pattern=[[-1, P]], channel_multiplier=1).then_inc(n.sem, 1)
            pool.wait_ge(n.sem, 5)
            pool.tensor_copy(core.ident_bf[:, :], core.ident[:, :]).then_inc(n.sem, 1)
            pool.wait_ge(n.sem, 6)
    n.advance(6)


def load_stage(core, x):
    nc, loads = core.nc, core.loads
    with nc.Block() as block:
        @block.sync
        def _(sp):
            sp.dma_start(core.x[:, :, :], x.rearrange("b t d -> t b d")).then_inc(loads.sem, 16)
            sp.wait_ge(loads.sem, loads.base + 16)
    loads.advance(16)


def store_stage(core, out):
    nc, loads = core.nc, core.loads
    with nc.Block() as block:
        @block.sync
        def _(sp):
            sp.dma_start(out.rearrange("b t d -> t b d"), core.x[:, :, :]).then_inc(loads.sem, 16)
            sp.wait_ge(loads.sem, loads.base + 16)
    loads.advance(16)



def int_mlp_stage(core, w_gate_t, w_up_t, w_down_t):
    nc, loads, setup = core.nc, core.loads, core.setup
    H = w_gate_t.shape[1]
    HC = H // P
    with ExitStack() as ctx:
        f = Frame(core, ctx)
        sb = lambda n, s, t=F32: ctx.enter_context(nc.sbuf_tensor(core.named(n), s, t))
        w_int = [sb("wg_int", [P, DC, H], I32), sb("wu_int", [P, DC, H], I32), sb("wd_int", [P, HC, D], I32)]
        wg, wu, wd = sb("wg", [P, DC, H]), sb("wu", [P, DC, H]), sb("wd", [P, HC, D])
        silu = sb("silu", [P, 2, HC, P])
        hT = sb("hT", [P, 2, HC, P])
        gate_ps = ctx.enter_context(nc.psum_tensor(core.named("gate_ps"), [P, 8, P], F32))
        up_ps = ctx.enter_context(nc.psum_tensor(core.named("up_ps"), [P, 8, P], F32))
        weights = setup.base + 3
        gate_ready, up_ready = core.count("gate_ready"), core.count("up_ready")
        silu_done, hT_ready = core.count("silu_done"), core.count("hT_ready")
        with nc.Block() as block:
            @block.sync
            def _(sp):
                for dst, src in zip(w_int, (w_gate_t, w_up_t, w_down_t)):
                    sp.dma_start(dst[:, :, :], chunked(src)).then_inc(loads.sem, 16)

            @block.gpsimd
            def _(pool):
                with pool.Fori(0, B // 2) as i:
                    for j in range(2):
                        f.fetch(pool, 2 * i + j, j)
                    for j in range(2):
                        f.rstd_out(pool, 2 * i + j, j)

            @block.tensor
            def _(pe):
                pe.wait_ge(setup.sem, weights)
                with pe.Fori(0, B // 2) as i:
                    for j in range(2):
                        f.turn(pe, 2 * i + j, j)
                    for j in range(2):
                        b = 2 * i + j
                        pe.wait_ge(f.xT_ready.sem, f.xT_ready.done(b))
                        for ps, w, used, ready in ((gate_ps, wg, silu_done, gate_ready), (up_ps, wu, hT_ready, up_ready)):
                            pe.wait_ge(used.sem, used.freed(b, 1))
                            for m in range(HC):
                                for c in range(DC):
                                    last = pe.matmul(ps[:, m, :], w[:, c, m * P:(m + 1) * P], f.xT[:, j, c, :],
                                                     start=(c == 0), stop=(c == DC - 1))
                            last.then_inc(ready.sem, 1)
                    for j in range(2):
                        b = 2 * i + j
                        pe.wait_ge(hT_ready.sem, hT_ready.done(b))
                        f.claim_bank(pe, b, j)
                        for m in range(HC):
                            last = pe.matmul(f.out_ps, hT[:, j, m, :], wd[:, m, :],
                                             start=(m == 0), stop=(m == HC - 1))
                        last.then_inc(f.out_ready.sem, 1)

            @block.scalar
            def _(act):
                with act.Fori(0, B // 2) as i:
                    for j in range(2):
                        f.copy_turned(act, 2 * i + j, j)
                    for j in range(2):
                        b = 2 * i + j
                        act.wait_ge(gate_ready.sem, gate_ready.done(b))
                        act.wait_ge(hT_ready.sem, hT_ready.freed(b))
                        act.activation(silu[:, j], gate_ps[:, 0:HC, :], ACT.Silu).then_inc(silu_done.sem, 1)

            @block.vector
            def _(dve):
                dve.wait_ge(loads.sem, loads.base + 48)
                for dst, src in zip((wg, wu, wd), w_int):
                    dve.tensor_scalar(dst[:, :, :], src[:, :, :], float(np.float32(1.0 / 127.0)), None, ALU.mult
                                      ).then_inc(setup.sem, 1)
                with dve.Fori(0, B // 2) as i:
                    for j in range(2):
                        b = 2 * i + j
                        dve.wait_ge(silu_done.sem, silu_done.done(b))
                        dve.wait_ge(up_ready.sem, up_ready.done(b))
                        dve.wait_ge(f.out_ready.sem, f.out_ready.freed(b))
                        dve.tensor_tensor(hT[:, j], up_ps[:, 0:HC, :], silu[:, j], ALU.mult
                                          ).then_inc(hT_ready.sem, 1)
                    for j in range(2):
                        f.finish(dve, 2 * i + j, j)
                    for j in range(2):
                        f.save_normed(dve, 2 * i + j, j)
        for c in (gate_ready, up_ready, silu_done, hT_ready):
            c.advance(B)
        f.end()
        setup.advance(3)
        loads.advance(48)



class Attention:

    def __init__(self, core, ctx, frame, heads, head_dim, chunks, scale, key_tiles=1, a_items=1, b_items=2,
                 mask=None, bias=None, null=None, q_chunks=4, parts=1):
        nc = core.nc
        self.core, self.nc, self.f = core, nc, frame
        self.H, self.hd, self.chunks, self.scale, self.kt = heads, head_dim, chunks, scale, key_tiles
        self.NA, self.NB = a_items, b_items
        self.mask, self.bias, self.null = mask, bias, null
        self.n = len(chunks)
        self.parts, self.per_part = parts, len(chunks) // parts
        self.PH = heads // parts
        self.hc = len(chunks[0][1])
        self.W = key_tiles * P
        self.vw = head_dim + (0 if null is not None else 1)
        order, self.beside = [h for row, heads_in in chunks for cc, h in heads_in], {}
        self.spare = max(0, min(P // self.vw - 1, 512 // self.vw - heads)) if parts == 1 else 0
        for at, h in enumerate(order):
            wide = 1
            while ((wide + 1) * self.vw <= P and ((h + wide) % self.PH or self.spare)
                   and (h + wide in order[at:] or heads <= h + wide < heads + self.spare)):
                wide += 1
            self.beside[h] = wide
        sb = lambda n, s, t=F32: ctx.enter_context(nc.sbuf_tensor(core.named(n), s, t))
        ps = lambda n, s: ctx.enter_context(nc.psum_tensor(core.named(n), s, F32))
        rows = 64 if head_dim == 64 else 32
        self.rows = head_dim
        self.qT = sb("qT", [P, 2, q_chunks, P])
        self.kT = sb("kT", [P, 2, q_chunks, self.W])
        self.v = sb("v", [P, 2, key_tiles, heads + self.spare, self.vw])
        self.spare_zeroed = core.count("spare_heads_zeroed")
        self.mx = sb("mx", [P, 2, self.hc])
        self.negmax = sb("negmax", [P, 2, self.hc])
        self.probs = sb("probs", [P, 2, self.hc, self.W])
        self.pT = sb("pT", [P, 2, self.hc * key_tiles, P])
        self.inv = sb("inv", [P, 2, heads])
        if null is not None:
            self.snull, self.pnull_arg = sb("snull", [P, 2, heads]), sb("pnull_arg", [P, 2, self.hc])
            self.mx_all = sb("mx_all", [P, 2, self.hc])
            self.pnull, self.sums = sb("pnull", [P, 2, heads]), sb("sums", [P, 2, heads])
            self.tot = sb("tot", [P, 2, heads])
            self.null_v = sb("null_v", [P, 2, heads, head_dim])
            self.o_sum = sb("o_sum", [P, 2, heads, head_dim])
        self.a = sb("a", [P, 2, heads * head_dim])
        self.AC = heads * head_dim // P
        self.aT = sb("aT", [P, 2, self.AC, P])
        if bias is not None:
            self.biased = sb("biased", [P, 2, self.hc, self.W])
        self.bank_a, self.bank_b = ps("bank_a", [P, 4, P]), ps("bank_b", [P, 4, P])
        self.s_ps = [ps(f"s_ps{i}", [P, self.hc, self.W]) if self.hc * self.W == 512 else
                     ps(f"s_ps{i}", [P, 512]) for i in range(2)]
        self.t_ps = [ps(f"t_ps{i}", [P, 4, P]) for i in range(2)]
        self.o_ps = ps("o_ps", [P, 512])
        c = core.count
        (self.a_made, self.a_taken, self.b_made, self.b_taken) = (
            c("bank_a_made"), c("bank_a_taken"), c("bank_b_made"), c("bank_b_taken"))
        self.r_made, self.r_taken = c("result_turned"), c("result_copied")
        self.scored, self.biased_done, self.max_done, self.negmax_done = (
            c("scored"), c("biased_done"), c("max_done"), c("negmax_done"))
        self.exp_done, self.p_turned, self.weighed = c("exp_done"), c("p_turned"), c("weighed")
        self.pT_ready = [c("pT_even_ready"), c("pT_odd_ready")]
        self.inv_ready, self.a_ready = c("inv_ready"), c("a_ready")
        self.max_all, self.null_arg, self.tot_ready, self.null_v_ready, self.o_summed = (
            c("max_all"), c("null_arg"), c("tot_ready"), c("null_v_ready"), c("o_summed"))

    def end(self):
        for c, items in ((self.a_made, self.NA), (self.a_taken, self.NA),
                         (self.r_made, self.parts), (self.r_taken, self.parts),
                         (self.b_made, self.NB), (self.b_taken, self.NB),
                         (self.scored, self.n), (self.max_done, self.n), (self.negmax_done, self.n),
                         (self.exp_done, self.n), (self.p_turned, self.n), (self.pT_ready[0], self.n // 2), (self.pT_ready[1], self.n // 2),
                         (self.weighed, self.n), (self.inv_ready, self.parts), (self.a_ready, self.parts)):
            c.advance(B * items)
        if self.spare:
            self.spare_zeroed.advance(1)
        if self.null is not None:
            for c in (self.max_all, self.null_arg):
                c.advance(B * self.n)
            for c in (self.tot_ready, self.null_v_ready, self.o_summed):
                c.advance(B * self.parts)
        if self.bias is not None:
            self.biased_done.advance(B * self.n)
        self.f.end()

    def heads_of(self, t, j, n):
        heads = [h for cc, h in self.chunks[n][1]]
        step = heads[1] - heads[0]
        return t[:, j, heads[0]:heads[-1] + 1:step]

    def use_a(self, b, m):
        return self.NA * b + m

    def use_b(self, b, m):
        return self.NB * b + m

    def result(self, b, part):
        return self.parts * b + part

    def claim_a(self, pe, b, j, m):
        pe.wait_ge(self.a_taken.sem, self.a_taken.done(self.use_a(b, m) - 1))
        if m == 0:
            pe.wait_ge(self.r_taken.sem, self.r_taken.done(
                self.result(b, 0) - 2 if j == 0 else self.result(b - 1, 0) - 1))

    def claim_b(self, pe, b, m):
        pe.wait_ge(self.b_taken.sem, self.b_taken.done(self.use_b(b, m) - 1))

    def operands_free(self, eng, b):
        eng.wait_ge(self.weighed.sem, self.weighed.done(self.n * (b - 2) + self.n - 1))

    def heads_shape(self, t):
        if self.hc * self.W == 512:
            return t[:, :, :]
        return t[:, 0:self.hc * self.W].rearrange("p (h k) -> p h k", h=self.hc)

    def half(self, i, j, n):
        return self.n // 2 * (2 * i + j) + n // 2

    def score(self, pe, i, j, n):
        b = 2 * i + j
        g = self.n * b + n
        row, heads = self.chunks[n]
        slot = n % 2
        if n == 0:
            pe.wait_ge(self.a_taken.sem, self.a_taken.done(self.use_a(b, self.NA - 1)))
            pe.wait_ge(self.b_taken.sem, self.b_taken.done(self.use_b(b, self.NB - 1)))
        pe.wait_ge(self.exp_done.sem, self.exp_done.freed(g))
        if self.bias is not None:
            pe.wait_ge(self.biased_done.sem, self.biased_done.freed(g))
        s = self.heads_shape(self.s_ps[slot])
        extra = self.mask is not None
        for k, (cc, h) in enumerate(heads):
            last = pe.matmul(s[:, k, :], self.qT[row:row + self.rows, j, cc, :], self.kT[row:row + self.rows, j, cc, :],
                             start=True, stop=not extra)
            if self.mask is not None:
                last = pe.matmul(s[:, k, :], self.core.ident_bf[:, :], self.mask(b), start=False, stop=True)
        last.then_inc(self.scored.sem, 1)

    def turn_probs(self, pe, i, j, n):
        g = self.n * (2 * i + j) + n
        slot = n % 2
        pe.wait_ge(self.exp_done.sem, self.exp_done.done(g))
        copied = self.pT_ready[slot]
        pe.wait_ge(copied.sem, copied.freed(self.half(i, j, n), 1))
        for k in range(self.hc):
            for t in range(self.kt):
                last = pe.transpose(self.t_ps[slot][:, k * self.kt + t, :],
                                    self.probs[:, slot, k, t * P:(t + 1) * P], self.core.ident[:, :])
        last.then_inc(self.p_turned.sem, 1)

    def weigh(self, pe, i, j, n):
        b = 2 * i + j
        g = self.n * b + n
        slot = n % 2
        pe.wait_ge(self.pT_ready[slot].sem, self.pT_ready[slot].done(self.half(i, j, n)))
        if n % self.per_part == 0:
            pe.wait_ge(self.a_ready.sem, self.a_ready.freed(b * self.parts + n // self.per_part, 1))
        for k, (cc, h) in enumerate(self.chunks[n][1]):
            for t in range(self.kt):
                o = (h % self.PH) * self.vw
                wide = self.beside[h]
                last = pe.matmul(self.o_ps[:, o:o + wide * self.vw], self.pT[:, slot, k * self.kt + t, :],
                                 self.v[:, j, t, h:h + wide, :].rearrange("p h d -> p (h d)"),
                                 start=(t == 0), stop=(t == self.kt - 1))
        last.then_inc(self.weighed.sem, 1)

    def turn_result(self, pe, i, j, part, last_pair=False):
        b = 2 * i + j
        pe.wait_ge(self.a_ready.sem, self.a_ready.done(b * self.parts + part))
        ahead = b if j == 1 and (last_pair or part < self.parts - 1) else b + 1
        pe.wait_ge(self.a_taken.sem, self.a_taken.done(self.use_a(ahead, self.NA - 1)))
        pe.wait_ge(self.r_taken.sem, self.r_taken.done(self.result(b, part) - 1))
        per = self.AC // self.parts
        for c in range(per):
            at = part * per + c
            last = pe.transpose(self.bank_a[:, c, :], self.a[:, j, at * P:(at + 1) * P], self.core.ident[:, :])
        last.then_inc(self.r_made.sem, 1)

    def exponentiate(self, act, i, j, n):
        g = self.n * (2 * i + j) + n
        slot = n % 2
        act.wait_ge(self.negmax_done.sem, self.negmax_done.done(g))
        act.wait_ge(self.p_turned.sem, self.p_turned.freed(g))
        src = self.heads_shape(self.s_ps[slot]) if self.bias is None else self.biased[:, slot]
        scale = self.scale if self.bias is None else 1.0
        for k, (cc, h) in enumerate(self.chunks[n][1]):
            last = act.activation(self.probs[:, slot, k, :], src[:, k, :], ACT.Exp,
                                  bias=self.negmax[:, slot, k:k + 1], scale=scale,
                                  accum_out=self.sums[:, j, h:h + 1] if self.null is not None else None)
        if self.null is not None:
            act.wait_ge(self.null_arg.sem, self.null_arg.done(g))
            last = act.activation(self.heads_of(self.pnull, j, n), self.pnull_arg[:, slot, :], ACT.Exp)
        last.then_inc(self.exp_done.sem, 1)

    def copy_probs(self, eng, i, j, n):
        g = self.n * (2 * i + j) + n
        slot = n % 2
        eng.wait_ge(self.p_turned.sem, self.p_turned.done(g))
        eng.wait_ge(self.weighed.sem, self.weighed.freed(g))
        used = self.hc * self.kt
        out, src = self.pT[:, slot, :, :], self.t_ps[slot][:, 0:used, :]
        last = eng.tensor_copy(out, src) if n % 2 else eng.activation(out, src, ACT.Copy)
        last.then_inc(self.pT_ready[slot].sem, 1)

    def copy_result(self, act, i, j, part):
        b = 2 * i + j
        act.wait_ge(self.r_made.sem, self.r_made.done(self.result(b, part)))
        act.wait_ge(self.f.out_ready.sem, self.f.out_ready.freed(b))
        per = self.AC // self.parts
        act.activation(self.aT[:, j, part * per:(part + 1) * per, :], self.bank_a[:, 0:per, :], ACT.Copy
                       ).then_inc(self.r_taken.sem, 1)

    def row_max(self, dve, i, j, n):
        g = self.n * (2 * i + j) + n
        slot = n % 2
        s = self.heads_shape(self.s_ps[slot])
        dve.wait_ge(self.scored.sem, self.scored.done(g))
        if self.bias is not None:
            dve.wait_ge(self.exp_done.sem, self.exp_done.freed(g))
            dve.scalar_tensor_tensor(out=self.biased[:, slot], in0=s, scalar=self.scale, in1=self.bias[:, n],
                                     op0=ALU.mult, op1=ALU.add).then_inc(self.biased_done.sem, 1)
            dve.wait_ge(self.biased_done.sem, self.biased_done.done(g))
            s = self.biased[:, slot]
        dve.tensor_reduce(self.mx[:, slot, :], s, AX.X, ALU.max).then_inc(self.max_done.sem, 1)
        dve.wait_ge(self.max_done.sem, self.max_done.done(g))
        mx = self.mx
        if self.null is not None:
            mx = self.mx_all
            dve.tensor_tensor(mx[:, slot, :], self.mx[:, slot, :], self.heads_of(self.snull, j, n), ALU.max
                              ).then_inc(self.max_all.sem, 1)
            dve.wait_ge(self.max_all.sem, self.max_all.done(g))
        dve.wait_ge(self.exp_done.sem, self.exp_done.freed(g))
        dve.tensor_scalar(self.negmax[:, slot, :], mx[:, slot, :],
                          -self.scale if self.bias is None else -1.0, None, ALU.mult).then_inc(self.negmax_done.sem, 1)
        if self.null is not None:
            dve.wait_ge(self.negmax_done.sem, self.negmax_done.done(g))
            dve.scalar_tensor_tensor(out=self.pnull_arg[:, slot, :], in0=self.heads_of(self.snull, j, n),
                                     scalar=self.scale, in1=self.negmax[:, slot, :], op0=ALU.mult, op1=ALU.add
                                     ).then_inc(self.null_arg.sem, 1)

    def normalise(self, dve, i, j, part):
        b = 2 * i + j
        g = b * self.parts + part
        h0, h1 = part * self.PH, (part + 1) * self.PH
        o = self.o_ps[:, 0:self.PH * self.vw].rearrange("p (h d) -> p h d", h=self.PH)
        out = self.a[:, j, :].rearrange("p (h d) -> p h d", h=self.H)[:, h0:h1, :]
        dve.wait_ge(self.weighed.sem, self.weighed.done(self.n * b + self.per_part * (part + 1) - 1))
        if self.null is not None:
            dve.wait_ge(self.exp_done.sem, self.exp_done.done(self.n * b + self.per_part * (part + 1) - 1))
            dve.tensor_tensor(self.tot[:, j, h0:h1], self.sums[:, j, h0:h1], self.pnull[:, j, h0:h1], ALU.add
                              ).then_inc(self.tot_ready.sem, 1)
            dve.wait_ge(self.tot_ready.sem, self.tot_ready.done(g))
            dve.reciprocal(self.inv[:, j, h0:h1], self.tot[:, j, h0:h1]).then_inc(self.inv_ready.sem, 1)
            dve.wait_ge(self.null_v_ready.sem, self.null_v_ready.done(g))
            dve.tensor_tensor(self.o_sum[:, j, h0:h1, :], o, self.null_v[:, j, h0:h1, :], ALU.add
                              ).then_inc(self.o_summed.sem, 1)
            dve.wait_ge(self.o_summed.sem, self.o_summed.done(g))
            o = self.o_sum[:, j, h0:h1, :]
        else:
            dve.reciprocal(self.inv[:, j, :], o[:, :, self.hd]).then_inc(self.inv_ready.sem, 1)
        dve.wait_ge(self.inv_ready.sem, self.inv_ready.done(g))
        dve.wait_ge(self.r_made.sem, self.r_made.done(self.result(b - 2, part)))
        dve.tensor_tensor(out, o[:, :, 0:self.hd],
                          self.inv[:, j, h0:h1].unsqueeze(2).broadcast_to([P, self.PH, self.hd]), ALU.mult
                          ).then_inc(self.a_ready.sem, 1)

    def weigh_null(self, pool, i, j, part):
        b = 2 * i + j
        h0, h1 = part * self.PH, (part + 1) * self.PH
        pool.wait_ge(self.exp_done.sem, self.exp_done.done(self.n * b + self.per_part * (part + 1) - 1))
        pool.wait_ge(self.o_summed.sem, self.o_summed.done((b - 2) * self.parts + part))
        pool.tensor_tensor(self.null_v[:, j, h0:h1, :],
                           self.pnull[:, j, h0:h1].unsqueeze(2).broadcast_to([P, self.PH, self.hd]),
                           self.null.unsqueeze(1).broadcast_to([P, self.PH, self.hd]), ALU.mult
                           ).then_inc(self.null_v_ready.sem, 1)

    def steps(self, lag=2):
        n, total = self.n, 2 * self.n
        ends = {j * n + self.per_part * (part + 1): (j, part) for j in range(2) for part in range(self.parts)}
        order = []
        for s in range(2, total + lag + 1):
            t, w = s - lag, s - lag - 1
            if s == max(2, n - 3):
                order.append(("head", 0, 1, 0))
            if s == n - 1:
                order.append(("project", 0, 1, 0))
            if s < total:
                order.append(("score", 0, s // n, s % n))
            if 0 <= t < total:
                order.append(("turn", 0, t // n, t % n))
            if w == n + 2:
                order.append(("keep", 0, 0, 0))
            if w == n - 1:
                order.append(("fetch", 1, 0, 0))
            if w == total - 1:
                order.append(("head", 1, 0, 0))
            if w in ends and w < total:
                order.append(("turn_result", 0) + ends[w])
            if 0 <= w:
                order.append(("weigh", 0, w // n, w % n))
            if w + 1 in ends:
                order.append(("normalise", 0) + ends[w + 1])
            if w == n + 1:
                order.append(("inner", 0, 0, 0))
            if w == n:
                order.append(("out", 0, 0, 0))
        return order + [("project", 1, 0, 0), ("fetch", 1, 1, 0), ("turn_result", 0, 1, self.parts - 1), ("out", 0, 1, 0),
                        ("score", 1, 0, 0), ("inner", 0, 1, 0), ("score", 1, 0, 1), ("keep", 0, 1, 0)]

    def every_pair(self, eng, take):
        order = self.steps()
        for step, ahead, j, n in order:
            if ahead:
                take(step, 0, j, n, False)
        with eng.Fori(0, B // 2 - 1) as i:
            for step, ahead, j, n in order:
                take(step, i + ahead if ahead else i, j, n, False)
        for step, ahead, j, n in order:
            if not ahead:
                take(step, B // 2 - 1, j, n, True)

    def run(self, block, project, take_a, take_b, out_products, sync=None, pool_before=None, pool_head=None,
            pe_before=None, act_before=None, dve_before=None, act_scale=None, act_shift=None):
        f = self.f

        if sync is not None:
            block.sync(sync)

        @block.gpsimd
        def _(pool):
            if self.spare:
                pool.memset(self.v[:, :, :, self.H:, 0:self.hd], 0.0).then_inc(self.spare_zeroed.sem, 1)
            if pool_before:
                pool_before(pool)

            def take(step, i, j, n, last_pair):
                if step == "fetch":
                    f.fetch(pool, 2 * i + j, j)
                if step == "head":
                    if f.out_bias is not None:
                        f.bias_residual(pool, 2 * i + j, j)
                    if pool_head:
                        pool_head(pool, i, j)
                if step == "turn" and (n + 1) % self.per_part == 0 and self.null is not None:
                    self.weigh_null(pool, i, j, n // self.per_part)
                if step == "out" and f.inner_norm is not None:
                    f.rstd_inner(pool, 2 * i + j, j)
                if step == ("out" if f.inner_norm is None else "inner") and f.norm:
                    f.rstd_out(pool, 2 * i + j, j)

            self.every_pair(pool, take)

        @block.tensor
        def _(pe):
            pe_before(pe)
            if self.spare:
                pe.wait_ge(self.spare_zeroed.sem, self.spare_zeroed.done(0))

            def take(step, i, j, n, last_pair):
                if step == "head":
                    f.turn(pe, 2 * i + j, j)
                if step == "project":
                    pe.wait_ge(f.xT_ready.sem, f.xT_ready.done(2 * i + j))
                    project(pe, i, j)
                if step == "score":
                    self.score(pe, i, j, n)
                if step == "turn":
                    self.turn_probs(pe, i, j, n)
                if step == "weigh":
                    self.weigh(pe, i, j, n)
                if step == "turn_result":
                    self.turn_result(pe, i, j, n, last_pair)
                if step == "out":
                    pe.wait_ge(self.r_taken.sem, self.r_taken.done(self.result(2 * i + j, self.parts - 1)))
                    f.claim_bank(pe, 2 * i + j, j, last_pair)
                    out_products(pe, i, j).then_inc(f.out_ready.sem, 1)

            self.every_pair(pe, take)

        @block.scalar
        def _(act):
            if act_before:
                act_before(act)

            def take(step, i, j, n, last_pair):
                if step == "head":
                    f.copy_turned(act, 2 * i + j, j, act_scale, act_shift)
                if step == "project":
                    self.operands_free(act, 2 * i + j)
                    take_a(act, i, j)
                if step == "score":
                    self.exponentiate(act, i, j, n)
                if step == "turn" and n % 2 == 0:
                    self.copy_probs(act, i, j, n)
                if step == "turn_result":
                    self.copy_result(act, i, j, n)

            self.every_pair(act, take)

        @block.vector
        def _(dve):
            if dve_before:
                dve_before(dve)

            def take(step, i, j, n, last_pair):
                if step == "fetch":
                    f.normalise_in(dve, 2 * i + j, j)
                if step == "project":
                    self.operands_free(dve, 2 * i + j)
                    take_b(dve, i, j)
                if step == "score":
                    self.row_max(dve, i, j, n)
                if step == "turn" and n % 2 == 1:
                    self.copy_probs(dve, i, j, n)
                if step == "normalise":
                    self.normalise(dve, i, j, n)
                if step == "out":
                    f.finish(dve, 2 * i + j, j)
                if step == "inner" and f.inner_norm is not None:
                    f.finish_inner(dve, 2 * i + j, j)
                if step == "keep" and f.norm:
                    f.save_normed(dve, 2 * i + j, j)

            self.every_pair(dve, take)


HEADS, HEAD_DIM, ROWS = 16, 16, 32


def spread_heads(chunks_of=4, per_chunk=4):
    return [(ROWS * r, [(cc, 4 * r + cc) for cc in range(first, first + per_chunk)])
            for r in range(4) for first in range(0, chunks_of, per_chunk)]


def self_attention_stage(core, wq, wk, wv, wo, qkv_bias=None, out_bias=None, causal=False, alibi=None,
                         pre_norm=None, target=None, norm=True, context=None):
    nc, loads, setup = core.nc, core.loads, core.setup
    with ExitStack() as ctx:
        sb = lambda n, s, t=F32: ctx.enter_context(nc.sbuf_tensor(core.named(n), s, t))
        ob = sb("out_bias", [P, D]) if out_bias is not None else None
        f = Frame(core, ctx, pre_norm=pre_norm is not None, out_bias=None if ob is None else ob[:, :], target=target,
                  norm=norm, rotated=True)
        wq_sb, wk_sb = sb("wq", [P, DC, 4, 4, ROWS]), sb("wk", [P, DC, 4, 4, ROWS])
        wv_sb, wo_sb = sb("wv", [P, DC, D]), sb("wo", [P, DC, D])
        mask = sb("mask", [P, P], BF16) if causal else None
        bias_tab = None
        if alibi is not None:
            bias_tab = sb("alibi", [P, 4, 4, P])
            distance, absolute = sb("distance", [P, P]), sb("absolute", [P, P])
        if qkv_bias is not None:
            bq_sb, bk_sb, bv_sb = sb("bq", [P, 4]), sb("bk", [P, 4]), sb("bv", [P, D])
        if pre_norm is not None:
            n_scale, n_shift = sb("norm_scale", [P, DC]), sb("norm_shift", [P, DC])
        kt = 1 if context is None else 2
        chunks = spread_heads(4, 4 // kt)
        at = Attention(core, ctx, f, HEADS, HEAD_DIM, chunks, HEAD_DIM ** -0.5, key_tiles=kt,
                       a_items=1 if context is None else 2, b_items=2,
                       mask=None if mask is None else (lambda b: mask[:, :]), bias=bias_tab)
        if context is not None:
            c_in = sb("c_in", [P, 2, CTX])
            c_pad = sb("c_pad", [P, 2, 4, 4, ROWS])
            c_spread, c_used = core.count("c_spread"), core.count("c_v_copied")
        zeroed, consts, table = core.count("pads_zeroed"), core.count("constants_made"), core.count("table_made")
        pads = 2 if qkv_bias is None else 4
        steps_of_consts = 1 + (2 if causal else 0) + (1 if alibi is not None else 0)
        n_loads = [0]

        def load(sp, dst, src):
            sp.dma_start(dst, src).then_inc(loads.sem, 16)
            n_loads[0] += 16

        def sync(sp):
            sp.wait_ge(zeroed.sem, zeroed.done(pads - 1))
            for c in range(DC):
                for dst, src in ((wq_sb, wq), (wk_sb, wk)):
                    for cc in range(4):
                        load(sp, dst[:, c, cc, :, 0:HEAD_DIM],
                             src[c * P:(c + 1) * P].rearrange("p (r c d) -> p c r d", r=4, c=4)[:, cc])
            load(sp, wv_sb[:, :, :], chunked(wv))
            load(sp, wo_sb[:, :, :], chunked(wo))
            if out_bias is not None:
                load(sp, ob[:, :], row_everywhere(out_bias))
            if qkv_bias is not None:
                bq, bk, bv = qkv_bias
                for dst, src in ((bq_sb, bq), (bk_sb, bk)):
                    for r in range(4):
                        load(sp, dst[ROWS * r:ROWS * r + HEAD_DIM, :],
                             src[HEAD_DIM * r:HEAD_DIM * (r + 1), :])
                load(sp, bv_sb[:, :], row_everywhere(bv))
            if pre_norm is not None:
                load(sp, n_scale[:, :], pre_norm[0][:, :])
                load(sp, n_shift[:, :], pre_norm[1][:, :])
            if context is not None:
                with sp.Fori(0, B // 2) as i:
                    for j in range(2):
                        b = 2 * i + j
                        sp.wait_ge(c_used.sem, c_used.freed(b))
                        sp.dma_start(c_in[:, j, :], context[b]).then_inc(c_landed[j].sem, 16)

        total = 16 * (2 * DC * 4 + 2 + (out_bias is not None) + (9 if qkv_bias is not None else 0)
                      + (2 if pre_norm is not None else 0))
        weights = loads.base + total
        if context is not None:
            c_landed = [core.count("c_landed0"), core.count("c_landed1")]

        def pool_before(pool):
            last = pool.memset(at.v[:, :, :, :, HEAD_DIM:], 1.0)
            if context is not None:
                last = pool.memset(c_pad[:, :, :, :, :], 0.0)
            last.then_inc(consts.sem, 1)
            if causal:
                pool.memset(mask[:, :], 0.0).then_inc(consts.sem, 1)
                pool.wait_ge(consts.sem, consts.done(1))
                pool.affine_select(out=mask[:, :], in_=mask[:, :], compare_op=ALU.is_ge, fill=MASKED, base=0,
                                   pattern=[[-1, P]], channel_multiplier=1).then_inc(consts.sem, 1)
            if alibi is not None:
                pool.iota(distance[:, :], pattern=[[-1, P]], base=0, channel_multiplier=1,
                          allow_small_or_imprecise_dtypes=True).then_inc(consts.sem, 1)
            if context is not None:
                pool.wait_ge(consts.sem, consts.done(0))
            if out_bias is not None:
                pool.wait_ge(loads.sem, weights)

        def pool_head(pool, i, j):
            if context is None:
                return
            b = 2 * i + j
            cl = c_landed[j]
            pool.wait_ge(cl.sem, cl.base + 16 * (i + 1))
            pool.wait_ge(at.a_made.sem, at.a_made.done(at.use_a(2 * i + j - 2, 0)))
            pool.sem_inc(f.passed.sem, 1)
            pool.tensor_copy(c_pad[:, j, :, :, 0:HEAD_DIM],
                             c_in[:, j, 0:D].rearrange("p (r c d) -> p c r d", c=4, r=4)
                             ).then_inc(c_spread.sem, 1)
            at.operands_free(pool, b)
            pool.sem_inc(f.passed.sem, 1)
            pool.tensor_copy(at.v[:, j, 0, 0:HEADS, 0:HEAD_DIM],
                             c_in[:, j, D:CTX].rearrange("p (h d) -> p h d", h=HEADS)
                             ).then_inc(c_used.sem, 1)

        def dve_before(dve):
            dve.memset(wq_sb[:, :, :, :, :], 0.0).then_inc(zeroed.sem, 1)
            dve.memset(wk_sb[:, :, :, :, :], 0.0).then_inc(zeroed.sem, 1)
            if qkv_bias is not None:
                dve.memset(bq_sb[:, :], 0.0).then_inc(zeroed.sem, 1)
                dve.memset(bk_sb[:, :], 0.0).then_inc(zeroed.sem, 1)
            if alibi is not None:
                dve.wait_ge(consts.sem, consts.done(1))
                dve.scalar_tensor_tensor(out=absolute[:, :], in0=distance[:, :], scalar=-1.0, in1=distance[:, :],
                                         op0=ALU.mult, op1=ALU.max).then_inc(table.sem, 1)
                dve.wait_ge(table.sem, table.done(0))
                for r in range(4):
                    for cc in range(4):
                        slope = float(np.float32(2.0 ** (-8.0 * (4 * r + cc) / HEADS)))
                        last = dve.tensor_scalar(bias_tab[:, r, cc, :], absolute[:, :], -slope, None, ALU.mult)
                last.then_inc(table.sem, 1)
                dve.wait_ge(table.sem, table.done(1))
            dve.wait_ge(loads.sem, weights)

        def act_before(act):
            act.wait_ge(loads.sem, weights)

        def pe_before(pe):
            pe.wait_ge(loads.sem, weights)
            pe.wait_ge(consts.sem, consts.done(steps_of_consts - 1))

        def project(pe, i, j):
            b = 2 * i + j
            xT = f.xT[:, j]
            if context is not None:
                pe.wait_ge(c_spread.sem, c_spread.done(b))
                pe.wait_ge(c_used.sem, c_used.done(b))
                at.claim_a(pe, 2 * i + j, j, 0)
                flat = c_pad[:, j].rearrange("p c r d -> p c (r d)")
                for cc in range(4):
                    last = pe.transpose(at.bank_a[:, cc, :], flat[:, cc, :], core.ident[:, :])
                last.then_inc(at.a_made.sem, 1)
            at.claim_b(pe, 2 * i + j, 0)
            for cc in range(4):
                for c in range(DC):
                    last = pe.matmul(at.bank_b[:, cc, :], wk_sb[:, c, cc].rearrange("p r d -> p (r d)"), xT[:, c, :],
                                     start=(c == 0), stop=(c == DC - 1))
            last.then_inc(at.b_made.sem, 1)
            at.claim_a(pe, 2 * i + j, j, at.NA - 1)
            for cc in range(4):
                for c in range(DC):
                    last = pe.matmul(at.bank_a[:, cc, :], wq_sb[:, c, cc].rearrange("p r d -> p (r d)"), xT[:, c, :],
                                     start=(c == 0), stop=(c == DC - 1))
            last.then_inc(at.a_made.sem, 1)
            at.claim_b(pe, 2 * i + j, 1)
            v_ps = at.bank_b[:, 0:2, :].rearrange("p a b -> p (a b)")
            for c in range(DC):
                last = pe.matmul(v_ps, xT[:, c, :], wv_sb[:, c, :], start=(c == 0), stop=(c == DC - 1))
            last.then_inc(at.b_made.sem, 1)

        def take_a(act, i, j):
            if context is not None:
                act.wait_ge(at.a_made.sem, at.a_made.done(at.use_a(2 * i + j, 0)))
                act.activation(at.kT[:, j, :, 0:P], at.bank_a[:, :, :], ACT.Copy).then_inc(at.a_taken.sem, 1)
            act.wait_ge(at.a_made.sem, at.a_made.done(at.use_a(2 * i + j, at.NA - 1)))
            if qkv_bias is None:
                last = act.activation(at.qT[:, j], at.bank_a[:, :, :], ACT.Copy)
            else:
                for cc in range(4):
                    last = act.activation(at.qT[:, j, cc, :], at.bank_a[:, cc, :], ACT.Identity,
                                          bias=bq_sb[:, cc:cc + 1])
            last.then_inc(at.a_taken.sem, 1)

        def take_b(dve, i, j):
            dve.wait_ge(at.b_made.sem, at.b_made.done(at.use_b(2 * i + j, 0)))
            out = at.kT[:, j, :, (kt - 1) * P:kt * P]
            if qkv_bias is None:
                last = dve.tensor_copy(out, at.bank_b[:, :, :])
            else:
                last = dve.tensor_tensor(out, at.bank_b[:, :, :],
                                         bk_sb[:, :].unsqueeze(2).broadcast_to([P, 4, P]), ALU.add)
            last.then_inc(at.b_taken.sem, 1)
            dve.wait_ge(at.b_made.sem, at.b_made.done(at.use_b(2 * i + j, 1)))
            out = at.v[:, j, kt - 1, 0:HEADS, 0:HEAD_DIM]
            v_ps = at.bank_b[:, 0:2, :].rearrange("p a (h d) -> p (a h) d", d=HEAD_DIM)
            if qkv_bias is None:
                last = dve.tensor_copy(out, v_ps)
            else:
                last = dve.tensor_tensor(out, v_ps, bv_sb[:, :].rearrange("p (h d) -> p h d", h=HEADS), ALU.add)
            last.then_inc(at.b_taken.sem, 1)

        def out_products(pe, i, j):
            for c in range(DC):
                last = pe.matmul(f.out_ps, at.aT[:, j, c, :], wo_sb[:, c, :], start=(c == 0), stop=(c == DC - 1))
            return last

        with nc.Block() as block:
            at.run(block, project, take_a, take_b, out_products, sync=sync, pool_before=pool_before,
                   pool_head=pool_head, pe_before=pe_before, act_before=act_before, dve_before=dve_before,
                   act_scale=None if pre_norm is None else n_scale,
                   act_shift=None if pre_norm is None else n_shift)
        assert n_loads[0] == total
        loads.advance(total)
        zeroed.advance(pads)
        consts.advance(steps_of_consts)
        if alibi is not None:
            table.advance(2)
        if context is not None:
            for c in (c_spread, c_used):
                c.advance(B)
            for c in c_landed:
                c.advance(16 * B // 2)
        at.end()



class ContextFeed:

    def __init__(self, core, ctx, at, context):
        nc = core.nc
        self.core, self.at, self.context = core, at, context
        self.c_in = ctx.enter_context(nc.sbuf_tensor(core.named("c_in"), [P, 2, CTX], F32))
        self.cT = ctx.enter_context(nc.sbuf_tensor(core.named("cT"), [P, 2, CC, P], F32))
        self.landed = [core.count("c_landed0"), core.count("c_landed1")]

    def end(self):
        for c in self.landed:
            c.advance(16 * B // 2)

    def load(self, sp):
        at = self.at
        with sp.Fori(0, B // 2) as i:
            for j in range(2):
                sp.wait_ge(at.a_made.sem, at.a_made.done(at.use_a(2 * i + j - 2, 0)))
                sp.dma_start(self.c_in[:, j, :], self.context[2 * i + j]).then_inc(self.landed[j].sem, 16)

    def turn(self, pe, i, j):
        at = self.at
        landed = self.landed[j]
        pe.wait_ge(landed.sem, landed.base + 16 * (i + 1))
        at.claim_a(pe, 2 * i + j, j, 0)
        for c in range(CC):
            last = pe.transpose(at.bank_a[:, c, :], self.c_in[:, j, c * P:(c + 1) * P], self.core.ident[:, :])
        last.then_inc(at.a_made.sem, 1)

    def take(self, act, i, j):
        at = self.at
        act.wait_ge(at.a_made.sem, at.a_made.done(at.use_a(2 * i + j, 0)))
        act.activation(self.cT[:, j], at.bank_a[:, :, :], ACT.Copy).then_inc(at.a_taken.sem, 1)


def masked_context_stage(core, context, mask, mask_cols, w_src, b_src_k, b_src_v, w_tgt, b_tgt, w_out, b_out):
    nc, loads = core.nc, core.loads
    HEADS8, HD = 8, 32
    with ExitStack() as ctx:
        sb = lambda n, s, t=F32: ctx.enter_context(nc.sbuf_tensor(core.named(n), s, t))
        ob = sb("out_bias", [P, D])
        f = Frame(core, ctx, out_bias=ob[:, :], rotated=True)
        ws, wt, wo = sb("w_src", [P, CC, CTX]), sb("w_tgt", [P, DC, D]), sb("w_out", [P, CC, D])
        bk, bt, bv = sb("b_k", [P, DC]), sb("b_t", [P, DC]), sb("b_v", [P, D])
        mrow, mcol = sb("mask_row", [P, B, P]), sb("mask_col", [P, B, 1])
        left_out = sb("left_out", [P, B, P], BF16)
        chunks = [(32 * r, [(cc, 4 * cc + r) for cc in range(2)]) for r in range(4)]
        at = Attention(core, ctx, f, HEADS8, HD, chunks, HD ** -0.5, a_items=1, b_items=3, q_chunks=2,
                       mask=lambda b: left_out[:, b, :])
        feed = ContextFeed(core, ctx, at, context)
        consts, v_raw = core.count("constants_made"), core.count("v_raw")
        plain = ((ws[:, :, :], chunked(w_src)), (wt[:, :, :], chunked(w_tgt)), (wo[:, :, :], chunked(w_out)),
                 (bk[:, :], b_src_k[:, :]), (bt[:, :], b_tgt[:, :]), (bv[:, :], row_everywhere(b_src_v)),
                 (ob[:, :], row_everywhere(b_out)), (mcol[:, :, 0], mask_cols[:, :]),
                 (mrow[:, :, :], mask.rearrange("(o b) t -> o b t", o=1).broadcast_to([P, B, P])))
        weights = loads.base + 16 * len(plain)

        def sync(sp):
            for dst, src in plain:
                sp.dma_start(dst, src).then_inc(loads.sem, 16)
            feed.load(sp)

        def pool_before(pool):
            pool.memset(at.v[:, :, :, :, HD:], 1.0).then_inc(consts.sem, 1)
            pool.wait_ge(loads.sem, weights)

        def dve_before(dve):
            dve.wait_ge(loads.sem, weights)
            dve.tensor_scalar(left_out[:, :, :], mrow[:, :, :], 0.0, MASKED, ALU.is_equal, ALU.mult
                              ).then_inc(v_raw.sem, 1)

        def pe_before(pe):
            pe.wait_ge(loads.sem, weights)
            pe.wait_ge(consts.sem, consts.done(0))
            pe.wait_ge(v_raw.sem, v_raw.done(0))

        def project(pe, i, j):
            xT, cT = f.xT[:, j], feed.cT[:, j]
            feed.turn(pe, i, j)
            at.claim_b(pe, 2 * i + j, 0)
            for m in range(DC):
                for c in range(DC):
                    last = pe.matmul(at.bank_b[:, m, :], wt[:, c, m * P:(m + 1) * P], xT[:, c, :],
                                     start=(c == 0), stop=(c == DC - 1))
            last.then_inc(at.b_made.sem, 1)
            pe.wait_ge(at.a_taken.sem, at.a_taken.done(at.use_a(2 * i + j, 0)))
            at.claim_b(pe, 2 * i + j, 1)
            for m in range(DC):
                for c in range(CC):
                    last = pe.matmul(at.bank_b[:, m, :], ws[:, c, m * P:(m + 1) * P], cT[:, c, :],
                                     start=(c == 0), stop=(c == CC - 1))
            last.then_inc(at.b_made.sem, 1)
            at.claim_b(pe, 2 * i + j, 2)
            v_ps = at.bank_b[:, 0:2, :].rearrange("p a b -> p (a b)")
            for c in range(CC):
                last = pe.matmul(v_ps, cT[:, c, :], ws[:, c, D:CTX], start=(c == 0), stop=(c == CC - 1))
            last.then_inc(at.b_made.sem, 1)

        def take_a(act, i, j):
            feed.take(act, i, j)

        def take_b(dve, i, j):
            b = 2 * i + j
            for use, dst, bias in ((0, at.qT, bt), (1, at.kT, bk)):
                dve.wait_ge(at.b_made.sem, at.b_made.done(at.use_b(2 * i + j, use)))
                for m in range(DC):
                    last = dve.scalar_tensor_tensor(out=dst[:, j, m, :], in0=at.bank_b[:, m, :],
                                                    scalar=bias[:, m:m + 1], in1=mrow[:, b, :],
                                                    op0=ALU.add, op1=ALU.mult)
                last.then_inc(at.b_taken.sem, 1)
            dve.wait_ge(at.b_made.sem, at.b_made.done(at.use_b(2 * i + j, 2)))
            v = at.v[:, j, 0, 0:HEADS8, 0:HD]
            dve.tensor_tensor(v, at.bank_b[:, 0:2, :].rearrange("p a (h d) -> p (a h) d", d=HD),
                              bv[:, :].rearrange("p (h d) -> p h d", d=HD), ALU.add).then_inc(v_raw.sem, 1)
            dve.wait_ge(v_raw.sem, v_raw.done(1 + b))
            dve.tensor_scalar(v, v, mcol[:, b, :], None, ALU.mult).then_inc(at.b_taken.sem, 1)

        def out_products(pe, i, j):
            for c in range(CC):
                lhs = f.xT[:, j, c, :] if c < DC else at.aT[:, j, c - DC, :]
                last = pe.matmul(f.out_ps, lhs, wo[:, c, :], start=(c == 0), stop=(c == CC - 1))
            return last

        with nc.Block() as block:
            at.run(block, project, take_a, take_b, out_products, sync=sync, pool_before=pool_before,
                   pe_before=pe_before, dve_before=dve_before)
        loads.advance(16 * len(plain))
        consts.advance(1)
        v_raw.advance(1 + B)
        feed.end()
        at.end()


def wide_context_stage(core, context, wq, wkv, null_kv, wo, ln_scale, ln_bias):
    nc, loads = core.nc, core.loads
    HEADS64, HD = 16, 64
    INNER = HEADS64 * HD
    IC = INNER // P
    with ExitStack() as ctx:
        sb = lambda n, s, t=F32: ctx.enter_context(nc.sbuf_tensor(core.named(n), s, t))
        ob, ls = sb("ln_bias", [P, D]), sb("ln_scale", [P, D])
        f = Frame(core, ctx, out_bias=ob[:, :], inner_norm=ls[:, :], rotated=True)
        wq_sb, wkv_sb, wo_sb = sb("wq", [P, DC, INNER]), sb("wkv", [P, CC, 2 * INNER]), sb("wo", [P, IC, D])
        null_k, null_v = sb("null_k", [P, 2]), sb("null_v_row", [P, HD])
        chunks = [(64 * r, [(cc, 2 * cc + r) for cc in range(first, first + 4)]) for first in (0, 4) for r in range(2)]
        at = Attention(core, ctx, f, HEADS64, HD, chunks, HD ** -0.5, a_items=5, b_items=3, q_chunks=IC, parts=2,
                       null=null_v[:, :])
        feed = ContextFeed(core, ctx, at, context)
        consts = core.count("constants_made")
        plain = ((wq_sb[:, :, :], chunked(wq)), (wkv_sb[:, :, :], chunked(wkv)), (wo_sb[:, :, :], chunked(wo)),
                 (null_v[:, :], null_kv[1:2, :].broadcast_to([P, HD])),
                 (null_k[0:HD, 0:1], null_kv[0:1, :].rearrange("o d -> d o")),
                 (null_k[HD:P, 1:2], null_kv[0:1, :].rearrange("o d -> d o")),
                 (ob[:, :], row_everywhere(ln_bias)), (ls[:, :], row_everywhere(ln_scale)))
        weights = loads.base + 16 * len(plain)

        def sync(sp):
            sp.wait_ge(consts.sem, consts.done(1))
            with nc.allow_non_contiguous_dma(reason="64 values of the null key, once"):
                for dst, src in plain:
                    sp.dma_start(dst, src).then_inc(loads.sem, 16)
            feed.load(sp)

        def pool_before(pool):
            pool.memset(f.inner_eps[:, :], 1e-6).then_inc(consts.sem, 1)
            pool.memset(null_k[:, :], 0.0).then_inc(consts.sem, 1)
            pool.wait_ge(consts.sem, consts.done(1))
            pool.wait_ge(loads.sem, weights)

        def dve_before(dve):
            dve.wait_ge(loads.sem, weights)

        def pe_before(pe):
            pe.wait_ge(loads.sem, weights)

        def project(pe, i, j):
            xT, cT = f.xT[:, j], feed.cT[:, j]
            feed.turn(pe, i, j)

            def columns_of(bank, w, first, src, chunks_in, made):
                for m in range(4):
                    col = first + m * P
                    for c in range(chunks_in):
                        last = pe.matmul(bank[:, m, :], w[:, c, col:col + P], src[:, c, :],
                                         start=(c == 0), stop=(c == chunks_in - 1))
                last.then_inc(made.sem, 1)

            def values_of(bank, first, made):
                out = bank[:, :, :].rearrange("p a b -> p (a b)")
                for c in range(CC):
                    last = pe.matmul(out, cT[:, c, :], wkv_sb[:, c, INNER + first:INNER + first + 4 * P],
                                     start=(c == 0), stop=(c == CC - 1))
                last.then_inc(made.sem, 1)

            at.claim_b(pe, 2 * i + j, 0)
            columns_of(at.bank_b, wq_sb, INNER // 2, xT, DC, at.b_made)
            at.claim_a(pe, 2 * i + j, j, 1)
            columns_of(at.bank_a, wq_sb, 0, xT, DC, at.a_made)
            at.claim_b(pe, 2 * i + j, 1)
            columns_of(at.bank_b, wkv_sb, INNER // 2, cT, CC, at.b_made)
            at.claim_a(pe, 2 * i + j, j, 2)
            columns_of(at.bank_a, wkv_sb, 0, cT, CC, at.a_made)
            at.claim_b(pe, 2 * i + j, 2)
            values_of(at.bank_b, INNER // 2, at.b_made)
            at.claim_a(pe, 2 * i + j, j, 3)
            values_of(at.bank_a, 0, at.a_made)
            at.claim_a(pe, 2 * i + j, j, 4)
            for cc in range(IC):
                last = pe.matmul(at.bank_a[:, 0, 2 * cc:2 * cc + 2], at.qT[:, j, cc, :], null_k[:, :],
                                 start=True, stop=True)
            last.then_inc(at.a_made.sem, 1)

        def take_a(act, i, j):
            feed.take(act, i, j)
            for use, out in ((1, at.qT[:, j, 0:4, :]), (2, at.kT[:, j, 0:4, :]), (3, at.v[:, j, 0, 0:8, :]),
                             (4, at.snull[:, j, :])):
                act.wait_ge(at.a_made.sem, at.a_made.done(at.use_a(2 * i + j, use)))
                src = at.bank_a[:, :, :]
                if use == 3:
                    src = src.rearrange("p a (h d) -> p (a h) d", d=HD)
                if use == 4:
                    src = at.bank_a[:, 0, 0:HEADS64]
                act.activation(out, src, ACT.Copy).then_inc(at.a_taken.sem, 1)

        def take_b(dve, i, j):
            for use, out in ((0, at.qT[:, j, 4:8, :]), (1, at.kT[:, j, 4:8, :]), (2, at.v[:, j, 0, 8:16, :])):
                dve.wait_ge(at.b_made.sem, at.b_made.done(at.use_b(2 * i + j, use)))
                src = at.bank_b[:, :, :]
                if use == 2:
                    src = src.rearrange("p a (h d) -> p (a h) d", d=HD)
                dve.tensor_copy(out, src).then_inc(at.b_taken.sem, 1)
            dve.wait_ge(at.a_taken.sem, at.a_taken.done(at.use_a(2 * i + j, 4)))

        def out_products(pe, i, j):
            for c in range(IC):
                last = pe.matmul(f.out_ps, at.aT[:, j, c, :], wo_sb[:, c, :], start=(c == 0), stop=(c == IC - 1))
            return last

        with nc.Block() as block:
            at.run(block, project, take_a, take_b, out_products, sync=sync, pool_before=pool_before,
                   pe_before=pe_before, dve_before=dve_before)
        loads.advance(16 * len(plain))
        consts.advance(2)
        feed.end()
        at.end()



def linear_attention_stage(core, wq, wk, wv, wo, bo):
    nc, loads = core.nc, core.loads
    H, HD = 8, 64
    INNER = H * HD
    IC = INNER // P
    with ExitStack() as ctx:
        sb = lambda n, s, t=F32: ctx.enter_context(nc.sbuf_tensor(core.named(n), s, t))
        ps = lambda n: ctx.enter_context(nc.psum_tensor(core.named(n), [P, IC, P], F32))
        ob = sb("out_bias", [P, D])
        f = Frame(core, ctx, out_bias=ob[:, :])
        wq_sb, wk_sb, wv_sb, wo_sb = (sb("wq", [P, DC, INNER]), sb("wk", [P, DC, INNER]), sb("wv", [P, DC, INNER]),
                                      sb("wo", [P, IC, D]))
        q_max, q_sum, q_inv = sb("q_max", [P, 2, H]), sb("q_sum", [P, 2, H]), sb("q_inv", [P, 2, H])
        q_low, q_exp, q = sb("q_low", [P, 2, H, HD]), sb("q_exp", [P, 2, H, HD]), sb("q", [P, 2, H, HD])
        k_max, k_neg, k_sum, k_inv = (sb("k_max", [P, 2, IC]), sb("k_neg", [P, 2, IC]), sb("k_sum", [P, 2, IC]),
                                      sb("k_inv", [P, 2, IC]))
        k_exp = sb("k_exp", [P, 2, IC, P])
        v = sb("v", [P, 2, IC, P])
        qT, k_tok = sb("qT", [P, 2, IC, P]), sb("k_tok", [P, 2, IC, P])
        blocks = sb("blocks", [P, 2, IC, P])
        aT = sb("aT", [P, 2, IC, P])
        q_ps, k_ps, v_ps, qT_ps, kt_ps, c_ps, a_ps = (ps(n) for n in ("q_ps", "k_ps", "v_ps", "qT_ps", "kt_ps",
                                                                     "c_ps", "a_ps"))
        c = core.count
        (q_made, k_made, v_made, q_maxed, q_lowered, q_exped, q_summed, q_inverted, q_ready, q_turned, qT_ready,
         k_maxed, k_negated, k_exped, k_inverted, k_turned, k_ready, v_ready, c_made, blocks_ready, a_made,
         aT_ready) = names = (
            c("q_made"), c("k_made"), c("v_made"), c("q_maxed"), c("q_lowered"), c("q_exped"), c("q_summed"),
            c("q_inverted"), c("q_ready"), c("q_turned"), c("qT_ready"), c("k_maxed"), c("k_negated"),
            c("k_exped"), c("k_inverted"), c("k_turned"), c("k_ready"), c("v_ready"), c("c_made"),
            c("blocks_ready"), c("a_made"), c("aT_ready"))
        consts = core.count("constants_made")
        plain = ((wq_sb[:, :, :], chunked(wq)), (wk_sb[:, :, :], chunked(wk)), (wv_sb[:, :, :], chunked(wv)),
                 (wo_sb[:, :, :], chunked(wo)), (ob[:, :], row_everywhere(bo)))
        weights = loads.base + 16 * len(plain)
        with nc.Block() as block:
            @block.sync
            def _(sp):
                for dst, src in plain:
                    sp.dma_start(dst, src).then_inc(loads.sem, 16)

            @block.gpsimd
            def _(pool):
                pool.memset(blocks[:, :, :, :], 0.0).then_inc(consts.sem, 1)
                pool.wait_ge(loads.sem, weights)
                with pool.Fori(0, B // 2) as i:
                    for j in range(2):
                        f.fetch(pool, 2 * i + j, j)
                    for j in range(2):
                        f.rstd_out(pool, 2 * i + j, j)

            @block.tensor
            def _(pe):
                pe.wait_ge(loads.sem, weights)
                with pe.Fori(0, B // 2) as i:
                    for j in range(2):
                        f.turn(pe, 2 * i + j, j)
                    for j in range(2):
                        b = 2 * i + j
                        xT = f.xT[:, j]
                        pe.wait_ge(f.xT_ready.sem, f.xT_ready.done(b))
                        pe.wait_ge(k_exped.sem, k_exped.freed(b, 1))
                        for m in range(IC):
                            for cc in range(DC):
                                last = pe.matmul(k_ps[:, m, :], wk_sb[:, cc, m * P:(m + 1) * P], xT[:, cc, :],
                                                 start=(cc == 0), stop=(cc == DC - 1))
                        last.then_inc(k_made.sem, 1)
                        pe.wait_ge(q_lowered.sem, q_lowered.freed(b, 1))
                        for cc in range(DC):
                            last = pe.matmul(q_ps[:, :, :].rearrange("p a b -> p (a b)"), xT[:, cc, :], wq_sb[:, cc, :],
                                             start=(cc == 0), stop=(cc == DC - 1))
                        last.then_inc(q_made.sem, 1)
                        pe.wait_ge(v_ready.sem, v_ready.freed(b, 1))
                        for cc in range(DC):
                            last = pe.matmul(v_ps[:, :, :].rearrange("p a b -> p (a b)"), xT[:, cc, :], wv_sb[:, cc, :],
                                             start=(cc == 0), stop=(cc == DC - 1))
                        last.then_inc(v_made.sem, 1)
                    for j in range(2):
                        b = 2 * i + j
                        pe.wait_ge(k_exped.sem, k_exped.done(b))
                        pe.wait_ge(k_ready.sem, k_ready.freed(b, 1))
                        for m in range(IC):
                            last = pe.transpose(kt_ps[:, m, :], k_exp[:, j, m, :], core.ident[:, :])
                        last.then_inc(k_turned.sem, 1)
                        pe.wait_ge(q_ready.sem, q_ready.done(b))
                        pe.wait_ge(qT_ready.sem, qT_ready.freed(b, 1))
                        for m in range(IC):
                            last = pe.transpose(qT_ps[:, m, :],
                                                q[:, j, 2 * m:2 * m + 2, :].rearrange("p h d -> p (h d)"),
                                                core.ident[:, :])
                        last.then_inc(q_turned.sem, 1)
                    for j in range(2):
                        b = 2 * i + j
                        pe.wait_ge(k_ready.sem, k_ready.done(b))
                        pe.wait_ge(v_ready.sem, v_ready.done(b))
                        pe.wait_ge(blocks_ready.sem, blocks_ready.freed(b, 1))
                        for m in range(IC):
                            last = pe.matmul(c_ps[:, m, :], k_tok[:, j, m, :], v[:, j, m, :], start=True, stop=True)
                        last.then_inc(c_made.sem, 1)
                    for j in range(2):
                        b = 2 * i + j
                        pe.wait_ge(blocks_ready.sem, blocks_ready.done(b))
                        pe.wait_ge(qT_ready.sem, qT_ready.done(b))
                        pe.wait_ge(aT_ready.sem, aT_ready.freed(b, 1))
                        for m in range(IC):
                            last = pe.matmul(a_ps[:, m, :], blocks[:, j, m, :], qT[:, j, m, :], start=True, stop=True)
                        last.then_inc(a_made.sem, 1)
                    for j in range(2):
                        b = 2 * i + j
                        pe.wait_ge(aT_ready.sem, aT_ready.done(b))
                        f.claim_bank(pe, b, j)
                        for m in range(IC):
                            last = pe.matmul(f.out_ps, aT[:, j, m, :], wo_sb[:, m, :], start=(m == 0), stop=(m == IC - 1))
                        last.then_inc(f.out_ready.sem, 1)

            @block.scalar
            def _(act):
                with act.Fori(0, B // 2) as i:
                    for j in range(2):
                        f.copy_turned(act, 2 * i + j, j)
                    for j in range(2):
                        b = 2 * i + j
                        act.wait_ge(k_negated.sem, k_negated.done(b))
                        act.wait_ge(k_turned.sem, k_turned.freed(b))
                        for m in range(IC):
                            last = act.activation(k_exp[:, j, m, :], k_ps[:, m, :], ACT.Exp,
                                                  bias=k_neg[:, j, m:m + 1], accum_out=k_sum[:, j, m:m + 1])
                        last.then_inc(k_exped.sem, 1)
                        act.wait_ge(q_lowered.sem, q_lowered.done(b))
                        act.wait_ge(q_ready.sem, q_ready.freed(b))
                        act.activation(q_exp[:, j], q_low[:, j], ACT.Exp).then_inc(q_exped.sem, 1)
                        act.wait_ge(v_made.sem, v_made.done(b))
                        act.wait_ge(c_made.sem, c_made.freed(b))
                        act.activation(v[:, j], v_ps[:, :, :], ACT.Copy).then_inc(v_ready.sem, 1)
                    for j in range(2):
                        b = 2 * i + j
                        act.wait_ge(k_turned.sem, k_turned.done(b))
                        act.wait_ge(c_made.sem, c_made.freed(b))
                        act.activation(k_tok[:, j], kt_ps[:, :, :], ACT.Copy).then_inc(k_ready.sem, 1)
                        act.wait_ge(q_turned.sem, q_turned.done(b))
                        act.wait_ge(a_made.sem, a_made.freed(b))
                        act.activation(qT[:, j], qT_ps[:, :, :], ACT.Copy).then_inc(qT_ready.sem, 1)
                    for j in range(2):
                        b = 2 * i + j
                        act.wait_ge(a_made.sem, a_made.done(b))
                        act.wait_ge(f.out_ready.sem, f.out_ready.freed(b))
                        act.activation(aT[:, j], a_ps[:, :, :], ACT.Copy).then_inc(aT_ready.sem, 1)

            @block.vector
            def _(dve):
                dve.wait_ge(consts.sem, consts.done(0))
                with dve.Fori(0, B // 2) as i:
                    for j in range(2):
                        b = 2 * i + j
                        q_bank = q_ps[:, :, :].rearrange("p a (h d) -> p (a h) d", d=HD)
                        dve.wait_ge(k_made.sem, k_made.done(b))
                        dve.tensor_reduce(k_max[:, j, :], k_ps[:, :, :], AX.X, ALU.max).then_inc(k_maxed.sem, 1)
                        dve.wait_ge(k_maxed.sem, k_maxed.done(b))
                        dve.wait_ge(k_exped.sem, k_exped.freed(b))
                        dve.tensor_scalar(k_neg[:, j, :], k_max[:, j, :], -1.0, None, ALU.mult
                                          ).then_inc(k_negated.sem, 1)
                        dve.wait_ge(q_made.sem, q_made.done(b))
                        dve.tensor_reduce(q_max[:, j, :], q_bank, AX.X, ALU.max).then_inc(q_maxed.sem, 1)
                        dve.wait_ge(q_maxed.sem, q_maxed.done(b))
                        dve.wait_ge(q_exped.sem, q_exped.freed(b))
                        dve.tensor_tensor(q_low[:, j], q_bank, q_max[:, j, :].unsqueeze(2).broadcast_to([P, H, HD]),
                                          ALU.subtract).then_inc(q_lowered.sem, 1)
                    for j in range(2):
                        b = 2 * i + j
                        dve.wait_ge(q_exped.sem, q_exped.done(b))
                        dve.tensor_reduce(q_sum[:, j, :], q_exp[:, j], AX.X, ALU.add).then_inc(q_summed.sem, 1)
                        dve.wait_ge(q_summed.sem, q_summed.done(b))
                        dve.reciprocal(q_inv[:, j, :], q_sum[:, j, :]).then_inc(q_inverted.sem, 1)
                        dve.wait_ge(q_inverted.sem, q_inverted.done(b))
                        dve.wait_ge(q_turned.sem, q_turned.freed(b))
                        dve.tensor_tensor(q[:, j], q_exp[:, j], q_inv[:, j, :].unsqueeze(2).broadcast_to([P, H, HD]),
                                          ALU.mult).then_inc(q_ready.sem, 1)
                        dve.wait_ge(k_exped.sem, k_exped.done(b))
                        dve.reciprocal(k_inv[:, j, :], k_sum[:, j, :]).then_inc(k_inverted.sem, 1)
                    for j in range(2):
                        b = 2 * i + j
                        dve.wait_ge(c_made.sem, c_made.done(b))
                        dve.wait_ge(k_inverted.sem, k_inverted.done(b))
                        dve.wait_ge(a_made.sem, a_made.freed(b))
                        for r in range(2):
                            rows = slice(HD * r, HD * (r + 1))
                            for m in range(IC):
                                last = dve.tensor_scalar(blocks[rows, j, m, rows], c_ps[rows, m, rows],
                                                         k_inv[rows, j, m:m + 1], HD ** -0.5, ALU.mult, ALU.mult)
                        last.then_inc(blocks_ready.sem, 1)
                    for j in range(2):
                        f.finish(dve, 2 * i + j, j)
                    for j in range(2):
                        f.save_normed(dve, 2 * i + j, j)
        for n in names:
            n.advance(B)
        loads.advance(16 * len(plain))
        consts.advance(1)
        f.end()



def gate_stage(core, hT_all, weight_all, gate_w, experts, top, norm_scale=None, norm_shift=None, x_from=None):
    nc, loads = core.nc, core.loads
    pre = norm_scale is not None
    E = experts
    with ExitStack() as ctx:
        sb = lambda n, s, t=F32: ctx.enter_context(nc.sbuf_tensor(core.named(n), s, t))
        f = Frame(core, ctx, pre_norm=pre, feeds_only=True)
        src_x = core.x if x_from is None else x_from
        gw = sb("gate_w", [P, DC, E])
        if pre:
            ns, nh = sb("norm_scale", [P, DC]), sb("norm_shift", [P, DC])
        number = sb("expert_number", [P, E])
        scores, best, which = sb("scores", [P, B, E]), sb("best", [P, B, 8]), sb("which", [P, B, 8], U32)
        which_f, low, ex = sb("which_f", [P, B, 2]), sb("low", [P, B, E]), sb("ex", [P, B, E])
        tot, inv = sb("tot", [P, B, 1]), sb("inv", [P, B, 1])
        first, second, chosen_ex = sb("first", [P, B, E]), sb("second", [P, B, E]), sb("chosen_ex", [P, B, E])
        g_ps = ctx.enter_context(nc.psum_tensor(core.named("g_ps"), [P, B, 512 // B], F32))
        c = core.count
        g_made, kept = c("g_made"), c("hT_kept")
        scored, found, exped, chosen = c("gate_scores_out"), c("best_found"), c("exped"), c("gate_step")
        consts = core.count("constants_made")
        plain = [(gw[:, :, :], chunked(gate_w))]
        if pre:
            plain += [(ns[:, :], norm_scale[:, :]), (nh[:, :], norm_shift[:, :])]
        weights = loads.base + 16 * len(plain)
        with nc.Block() as block:
            @block.sync
            def _(sp):
                for dst, src in plain:
                    sp.dma_start(dst, src).then_inc(loads.sem, 16)

            @block.gpsimd
            def _(pool):
                pool.iota(number[:, :], pattern=[[1, E]], base=0, channel_multiplier=0,
                          allow_small_or_imprecise_dtypes=True).then_inc(consts.sem, 1)
                with pool.Fori(0, B // 2) as i:
                    for j in range(2):
                        f.fetch(pool, 2 * i + j, j, src_x)

            @block.tensor
            def _(pe):
                pe.wait_ge(loads.sem, weights)
                with pe.Fori(0, B // 2) as i:
                    for j in range(2):
                        f.turn(pe, 2 * i + j, j)
                    for j in range(2):
                        b = 2 * i + j
                        pe.wait_ge(f.xT_ready.sem, f.xT_ready.done(b))
                        for cc in range(DC):
                            last = pe.matmul(g_ps[:, b, 0:E], f.xT[:, j, cc, :], gw[:, cc, :],
                                             start=(cc == 0), stop=(cc == DC - 1))
                        last.then_inc(g_made.sem, 1)

            @block.scalar
            def _(act):
                act.wait_ge(loads.sem, weights)
                with act.Fori(0, B // 2) as i:
                    for j in range(2):
                        b = 2 * i + j
                        act.wait_ge(g_made.sem, g_made.freed(b))
                        f.copy_turned(act, b, j, ns if pre else None, nh if pre else None)
                        act.wait_ge(f.xT_ready.sem, f.xT_ready.done(b))
                        act.activation(hT_all[:, :, b, :], f.xT[:, j], ACT.Copy).then_inc(kept.sem, 1)
                act.wait_ge(chosen.sem, chosen.done(0))
                act.activation(ex[:, :, :], low[:, :, :], ACT.Exp).then_inc(exped.sem, 1)

            @block.vector
            def _(dve):
                if pre:
                    with dve.Fori(0, B // 2) as i:
                        for j in range(2):
                            f.normalise_in(dve, 2 * i + j, j)
                dve.wait_ge(g_made.sem, g_made.done(B - 1))
                dve.tensor_copy(scores[:, :, :], g_ps[:, :, 0:E]).then_inc(scored.sem, 1)
                dve.wait_ge(scored.sem, scored.done(0))
                dve.sem_inc(f.passed.sem, 1)
                for b in range(B):
                    last = dve.max(best[:, b, :], scores[:, b, :])
                last.then_inc(found.sem, 1)
                dve.wait_ge(found.sem, found.done(0))
                dve.tensor_tensor(low[:, :, :], scores[:, :, :], best[:, :, 0:1].broadcast_to([P, B, E]), ALU.subtract
                                  ).then_inc(chosen.sem, 1)
                dve.sem_inc(f.passed.sem, 1)
                for b in range(B):
                    last = dve.max_index(which[:, b, :], best[:, b, :], scores[:, b, :])
                last.then_inc(found.sem, 1)
                dve.wait_ge(found.sem, found.done(1))
                dve.tensor_copy(which_f[:, :, :], which[:, :, 0:2]).then_inc(chosen.sem, 1)
                dve.wait_ge(chosen.sem, chosen.done(1))
                dve.wait_ge(consts.sem, consts.done(0))
                for k, pick in enumerate((first, second)):
                    last = dve.tensor_tensor(pick[:, :, :], number[:, :].unsqueeze(1).broadcast_to([P, B, E]),
                                             which_f[:, :, k:k + 1].broadcast_to([P, B, E]), ALU.is_equal)
                last.then_inc(chosen.sem, 1)
                dve.wait_ge(chosen.sem, chosen.done(2))
                if top == 2:
                    dve.tensor_tensor(first[:, :, :], first[:, :, :], second[:, :, :], ALU.add
                                      ).then_inc(chosen.sem, 1)
                else:
                    dve.sem_inc(chosen.sem, 1)
                dve.wait_ge(chosen.sem, chosen.done(3))
                dve.wait_ge(exped.sem, exped.done(0))
                dve.tensor_tensor(chosen_ex[:, :, :], first[:, :, :], ex[:, :, :], ALU.mult).then_inc(chosen.sem, 1)
                dve.wait_ge(chosen.sem, chosen.done(4))
                dve.tensor_reduce(tot[:, :, :], (chosen_ex if top == 2 else ex)[:, :, :], AX.X, ALU.add
                                  ).then_inc(chosen.sem, 1)
                dve.wait_ge(chosen.sem, chosen.done(5))
                dve.reciprocal(inv[:, :, :], tot[:, :, :]).then_inc(chosen.sem, 1)
                dve.wait_ge(chosen.sem, chosen.done(6))
                dve.tensor_tensor(weight_all[:, :, :, 0], chosen_ex[:, :, :].rearrange("p b e -> p e b"),
                                  inv[:, :, 0].unsqueeze(1).broadcast_to([P, E, B]), ALU.mult).then_inc(chosen.sem, 1)
        g_made.advance(B)
        kept.advance(B)
        scored.advance(1)
        found.advance(2)
        exped.advance(1)
        chosen.advance(8)
        loads.advance(16 * len(plain))
        consts.advance(1)
        f.end()


def expert_stage(core, hT_all, weight_all, acc, w_up, w_down, w_gate=None, b_up=None, b_down=None, residual=None):
    nc, loads = core.nc, core.loads
    E, _, HID = w_up.shape
    HC = HID // P
    G, S = 4, B // 4
    units = 2 * G
    gated = w_gate is not None
    with ExitStack() as ctx:
        sb = lambda n, s, t=F32: ctx.enter_context(nc.sbuf_tensor(core.named(n), s, t))
        up_sb, down_sb = sb("w_up", [P, 2, DC, HID]), sb("w_down", [P, 2, HC, D])
        gate_sb = sb("w_gate", [P, 2, DC, HID]) if gated else None
        bias_sb = sb("b_up", [P, 2, HC]) if b_up is not None else None
        if b_down is not None:
            down_bias, with_bias = sb("b_down", [P, 2, D]), sb("with_bias", [P, 2, D])
            biased = core.count("out_biased")
        hid = sb("hid", [P, 2, HC, S * P])
        silu = sb("silu", [P, 2, S * P]) if gated else None
        up_ps = [ctx.enter_context(nc.psum_tensor(core.named(f"up_ps{k}"), [P, S * P], F32)) for k in range(2)]
        gate_ps = [ctx.enter_context(nc.psum_tensor(core.named(f"gate_ps{k}"), [P, S * P], F32)) for k in range(2)] if gated else None
        out_ps = [ctx.enter_context(nc.psum_tensor(core.named(f"e_out_ps{k}"), [P, 2, D], F32)) for k in range(2)]
        c = core.count
        upped, gated_done, silued, hid_ready, downed, added = (
            c("upped"), c("gate_made"), c("silued"), c("hid_ready"), c("downed"), c("added"))
        begun = c("acc_begun")
        landed = [c("expert_landed0"), c("expert_landed1")]
        per_load = 2 + gated + (b_up is not None) + (b_down is not None)
        with nc.Block() as block:
            @block.sync
            def _(sp):
                with sp.Fori(0, E // 2) as i:
                    for k in range(2):
                        e = 2 * i + k
                        sp.wait_ge(downed.sem, downed.done(2 * (units * i + G * k - G) - 1))
                        pairs = [(up_sb[:, k], w_up[e]), (down_sb[:, k], w_down[e])]
                        if gated:
                            pairs.append((gate_sb[:, k], w_gate[e]))
                        for dst, src in pairs:
                            sp.dma_start(dst, chunked(src)).then_inc(landed[k].sem, 16)
                        if b_up is not None:
                            sp.dma_start(bias_sb[:, k], b_up[e]).then_inc(landed[k].sem, 16)
                        if b_down is not None:
                            sp.wait_ge(added.sem, added.done(2 * (units * i + G * k - G) - 1))
                            sp.dma_start(down_bias[:, k, :], b_down[e].broadcast_to([P, D])).then_inc(landed[k].sem, 16)

            @block.gpsimd
            def _(pool):
                if residual is None:
                    pool.tensor_copy(acc[:, :, :], core.x[:, :, :]).then_inc(begun.sem, 1)
                else:
                    pool.tensor_tensor(acc[:, :, :], core.x[:, :, :], residual[:, :, :], ALU.add
                                       ).then_inc(begun.sem, 1)

            @block.tensor
            def _(pe):
                with pe.Fori(0, E // 2) as i:
                    for n in range(units + 1):
                        if n < units:
                            k, g = n // G, n % G
                            if g == 0:
                                pe.wait_ge(landed[k].sem, landed[k].base + 16 * per_load * (i + 1))
                            for m in range(HC):
                                u = HC * (units * i + n) + m
                                for ps, w, used, made in (((gate_ps, gate_sb, silued, gated_done),) if gated else ()) + (
                                        (up_ps, up_sb, hid_ready, upped),):
                                    pe.wait_ge(used.sem, used.freed(u))
                                    for cc in range(DC):
                                        last = pe.matmul(ps[m % 2][:, :], w[:, k, cc, m * P:(m + 1) * P],
                                                         hT_all[:, cc, S * g:S * (g + 1), :].rearrange("p b t -> p (b t)"),
                                                         start=(cc == 0), stop=(cc == DC - 1))
                                    last.then_inc(made.sem, 1)
                        if n >= 1:
                            q = n - 1
                            unit = units * i + q
                            pe.wait_ge(hid_ready.sem, hid_ready.done(HC * unit + HC - 1))
                            for t in range(S):
                                if t % 2 == 0:
                                    half = 2 * unit + t // 2
                                    pe.wait_ge(added.sem, added.freed(half))
                                for m in range(HC):
                                    last = pe.matmul(out_ps[t // 2][:, t % 2, :], hid[:, q % 2, m, t * P:(t + 1) * P],
                                                     down_sb[:, q // G, m, :], start=(m == 0), stop=(m == HC - 1))
                                if t % 2:
                                    last.then_inc(downed.sem, 1)

            @block.scalar
            def _(act):
                with act.Fori(0, E // 2) as i:
                    for n in range(units):
                        k = n // G
                        if b_up is not None and n % G == 0:
                            act.wait_ge(landed[k].sem, landed[k].base + 16 * per_load * (i + 1))
                        for m in range(HC):
                            u = HC * (units * i + n) + m
                            if gated:
                                act.wait_ge(gated_done.sem, gated_done.done(u))
                                act.wait_ge(hid_ready.sem, hid_ready.freed(u))
                                act.activation(silu[:, m % 2, :], gate_ps[m % 2][:, :], ACT.Silu
                                               ).then_inc(silued.sem, 1)
                            else:
                                act.wait_ge(upped.sem, upped.done(u))
                                if m == 0:
                                    act.wait_ge(downed.sem, downed.done(2 * (units * i + n - 2) + 1))
                                act.activation(hid[:, n % 2, m, :], up_ps[m % 2][:, :], ACT.Relu,
                                               bias=bias_sb[:, k, m:m + 1]).then_inc(hid_ready.sem, 1)

            @block.vector
            def _(dve):
                dve.wait_ge(begun.sem, begun.done(0))
                with dve.Fori(0, E // 2) as i:
                    for n in range(units + 1):
                        for m in range(HC if gated and n < units else 0):
                            u = HC * (units * i + n) + m
                            dve.wait_ge(silued.sem, silued.done(u))
                            dve.wait_ge(upped.sem, upped.done(u))
                            if m == 0:
                                dve.wait_ge(downed.sem, downed.done(2 * (units * i + n - 2) + 1))
                            dve.tensor_tensor(hid[:, n % 2, m, :], up_ps[m % 2][:, :], silu[:, m % 2, :], ALU.mult
                                              ).then_inc(hid_ready.sem, 1)
                        if n >= 1:
                            q = n - 1
                            for t in range(S):
                                half = 2 * (units * i + q) + t // 2
                                b = S * (q % G) + t
                                if t % 2 == 0:
                                    dve.wait_ge(downed.sem, downed.done(half))
                                    dve.wait_ge(added.sem, added.done(half - 2 * G))
                                product = out_ps[t // 2][:, t % 2, :]
                                if b_down is not None:
                                    item = S * (units * i + q) + t
                                    if t == 0:
                                        dve.wait_ge(landed[q // G].sem,
                                                    landed[q // G].base + 16 * per_load * (i + 1))
                                    dve.tensor_tensor(with_bias[:, t % 2, :], product, down_bias[:, q // G, :], ALU.add
                                                      ).then_inc(biased.sem, 1)
                                    dve.wait_ge(biased.sem, biased.done(item))
                                    product = with_bias[:, t % 2, :]
                                last = dve.scalar_tensor_tensor(
                                    out=acc[:, b, :], in0=product,
                                    scalar=weight_all[:, 2 * i + q // G, b, :], in1=acc[:, b, :],
                                    op0=ALU.mult, op1=ALU.add)
                                if t % 2:
                                    last.then_inc(added.sem, 1)
        total = E * G
        for n, items in ((upped, HC), (hid_ready, HC), (downed, 2), (added, 2)):
            n.advance(total * items)
        if b_down is not None:
            biased.advance(total * S)
        if gated:
            gated_done.advance(total * HC)
            silued.advance(total * HC)
        begun.advance(1)
        for n in landed:
            n.advance(16 * per_load * E // 2)


def norm_stage(core, acc):
    nc = core.nc
    with ExitStack() as ctx:
        sb = lambda n, s, t=F32: ctx.enter_context(nc.sbuf_tensor(core.named(n), s, t))
        stats, mv = sb("stats_all", [P, B, 6]), sb("mv_all", [P, B, 2])
        var_eps, rstd = sb("var_all", [P, B, 1]), sb("rstd_all", [P, B, 1])
        step, var_done, rstd_done, saved = (core.count("norm_step"), core.count("y_var"), core.count("y_rstd"),
                                            core.count("x_saved"))
        passed = core.count("waits_passed")
        with nc.Block() as block:
            @block.vector
            def _(dve):
                for b in range(B):
                    last = dve.bn_stats(stats[:, b, :], acc[:, b, :])
                last.then_inc(step.sem, 1)
                dve.wait_ge(step.sem, step.done(0))
                dve.sem_inc(passed.sem, 1)
                for b in range(B):
                    last = dve.bn_aggr(mv[:, b, :], stats[:, b, :])
                last.then_inc(step.sem, 1)
                dve.wait_ge(step.sem, step.done(1))
                dve.wait_ge(rstd_done.sem, rstd_done.done(0))
                with dve.Fori(0, B) as b:
                    dve.tensor_scalar(core.x[:, b, :], acc[:, b, :], mv[:, b, 0:1], rstd[:, b, :],
                                      ALU.subtract, ALU.mult).then_inc(saved.sem, 1)

            @block.gpsimd
            def _(pool):
                pool.wait_ge(step.sem, step.done(1))
                pool.tensor_tensor(var_eps[:, :, :], mv[:, :, 1:2], core.ln_eps[:, :].unsqueeze(1).broadcast_to([P, B, 1]),
                                   ALU.add).then_inc(var_done.sem, 1)
                pool.wait_ge(var_done.sem, var_done.done(0))
                pool.tensor_tensor(rstd[:, :, :], var_eps[:, :, :],
                                   core.minus_half[:, :].unsqueeze(1).broadcast_to([P, B, 1]), ALU.pow
                                   ).then_inc(rstd_done.sem, 1)
        step.advance(2)
        var_done.advance(1)
        rstd_done.advance(1)
        saved.advance(B)



def depool_constants():
    logp = np.float32(-0.001)
    dt = np.float32(-np.log(-np.expm1(logp)))
    decay = np.exp(-np.float64(dt))
    gap = np.arange(P)[:, None] - np.arange(P)[None, :]
    table = np.where(gap >= 0, decay ** np.maximum(gap, 0), 0.0).astype(np.float32)
    return table, float(np.float32(1.0) / dt), float(np.float32(dt * np.exp(logp)))


def depool_stage(core, context, patch_lens, decay, upto, w_in, b_in, g_res, g_init):
    nc, loads = core.nc, core.loads
    _, over_dt, times_dt = depool_constants()
    with ExitStack() as ctx:
        sb = lambda n, s, t=F32: ctx.enter_context(nc.sbuf_tensor(core.named(n), s, t))
        ob = sb("out_bias", [P, D])
        f = Frame(core, ctx, out_bias=ob[:, :], own_input=True)
        w_sb, gr, gi, gi2 = sb("w_in", [P, DC, D]), sb("g_res", [P, DC]), sb("g_init", [P, D]), sb("g_init2", [P, D])
        lens_i, lens, ends = sb("lens_i", [P, B, P], I32), sb("lens", [P, B, P]), sb("ends", [P, B, P])
        hit, hits, hit_col = sb("hit", [P, B, P]), sb("hits", [P, 2, B]), sb("hit_col", [P, B])
        decay_sb, upto_sb = sb("decay", [P, P]), sb("upto", [P, P])
        zeros, token, token1, token2 = sb("zeros", [P, P]), sb("token", [P, 1]), sb("token1", [P, 1]), sb("token2", [P, 1])
        plug, spread = sb("plug", [P, B, P]), sb("spread", [P, B, P])
        c_in = sb("c_in", [P, 2, CTX])
        sq, ss, ms, rs = sb("sq", [P, CTX]), sb("ss", [P, 2, 2]), sb("ms", [P, 2, 2]), sb("rs", [P, 2, 2])
        over_n, rms_eps = sb("over_n", [P, 2]), sb("rms_eps", [P, 2])
        half2 = sb("half2", [P, 2])
        u, spread_in = sb("u", [P, 2, D]), sb("spread_in", [P, 2, P])
        wide_ps = ctx.enter_context(nc.psum_tensor(core.named("wide_ps"), [P, 4, 4, P], F32))
        c = core.count
        consts, prep, prep_pe, prep_act = c("constants_made"), c("prep_done"), c("prep_products"), c("prep_copied")
        landed = [c("c_landed0"), c("c_landed1")]
        prep_hits, squared_x = c("prep_hits"), c("squared_x")
        squared, ms1, ms2, rs_ready, u_ready, spread_ready = (c("squared"), c("ms1_done"), c("ms2_done"), c("rs_ready"),
                                                               c("u_ready"), c("spread_ready"))
        plain = ((w_sb[:, :, :], chunked(w_in)), (gr[:, :], g_res[:, :]), (gi[:, :], row_everywhere(g_init[0:D])),
                 (ob[:, :], row_everywhere(b_in)), (decay_sb[:, :], decay[:, :]), (upto_sb[:, :], upto[:, :]),
                 (lens_i[:, :, :], patch_lens.rearrange("(o b) t -> o b t", o=1).broadcast_to([P, B, P])))
        weights = loads.base + 16 * len(plain)
        with nc.Block() as block:
            @block.sync
            def _(sp):
                for dst, src in plain:
                    sp.dma_start(dst, src).then_inc(loads.sem, 16)
                with sp.Fori(0, B // 2) as i:
                    for j in range(2):
                        b = 2 * i + j
                        sp.wait_ge(u_ready.sem, u_ready.freed(b))
                        sp.dma_start(c_in[:, j, :], context[b]).then_inc(landed[j].sem, 16)

            @block.gpsimd
            def _(pool):
                pool.memset(zeros[:, :], 0.0)
                pool.memset(over_n[:, 0:1], 1.0 / D)
                pool.memset(over_n[:, 1:2], 1.0 / CTX)
                pool.memset(rms_eps[:, :], 1e-5)
                pool.memset(half2[:, :], -0.5)
                pool.iota(token[:, :], pattern=[[0, 1]], base=0, channel_multiplier=1,
                          allow_small_or_imprecise_dtypes=True)
                pool.iota(token1[:, :], pattern=[[0, 1]], base=1, channel_multiplier=1,
                          allow_small_or_imprecise_dtypes=True)
                pool.iota(token2[:, :], pattern=[[0, 1]], base=1 - P, channel_multiplier=1,
                          allow_small_or_imprecise_dtypes=True).then_inc(consts.sem, 1)
                pool.wait_ge(consts.sem, consts.done(0))
                pool.wait_ge(loads.sem, weights)
                pool.wait_ge(prep_act.sem, prep_act.done(0))
                with pool.Fori(0, B // 2) as i:
                    for j in range(2):
                        b = 2 * i + j
                        f.fetch(pool, b, j)
                        pool.wait_ge(f.out_ready.sem, f.out_ready.freed(b))
                        pool.tensor_copy(spread_in[:, j, :], spread[:, b, :]).then_inc(spread_ready.sem, 1)
                        pool.wait_ge(squared.sem, squared.done(b))
                        pool.tensor_tensor(ms[:, j, :], ss[:, j, :], over_n[:, :], ALU.mult).then_inc(ms1.sem, 1)
                        pool.wait_ge(ms1.sem, ms1.done(b))
                        pool.tensor_tensor(ms[:, j, :], ms[:, j, :], rms_eps[:, :], ALU.add).then_inc(ms2.sem, 1)
                        pool.wait_ge(ms2.sem, ms2.done(b))
                        pool.tensor_tensor(rs[:, j, :], ms[:, j, :], half2[:, :], ALU.pow).then_inc(rs_ready.sem, 1)
                    for j in range(2):
                        f.rstd_out(pool, 2 * i + j, j)

            @block.scalar
            def _(act):
                act.wait_ge(prep_pe.sem, prep_pe.done(1))
                act.activation(spread[:, :, :].rearrange("p (g s) t -> p g s t", g=4), wide_ps[:, :, :, :], ACT.Copy
                               ).then_inc(prep_act.sem, 1)
                act.wait_ge(loads.sem, weights)
                with act.Fori(0, B // 2) as i:
                    for j in range(2):
                        b = 2 * i + j
                        act.wait_ge(f.x_in_ready.sem, f.x_in_ready.done(b))
                        act.wait_ge(ms1.sem, ms1.freed(b))
                        act.activation(sq[:, 0:D], f.x_in[:, j, :], ACT.Square, accum_out=ss[:, j, 0:1]
                                       ).then_inc(squared_x.sem, 1)
                        act.wait_ge(landed[j].sem, landed[j].base + 16 * (i + 1))
                        act.wait_ge(squared_x.sem, squared_x.done(b))
                        act.activation(sq[:, :], c_in[:, j, :], ACT.Square, accum_out=ss[:, j, 1:2]
                                       ).then_inc(squared.sem, 1)
                    for j in range(2):
                        f.copy_turned(act, 2 * i + j, j, scale=gr)

            @block.tensor
            def _(pe):
                wide = lambda t: t[:, :, :].rearrange("p (g s) t -> p g (s t)", g=4)
                pe.wait_ge(loads.sem, weights)
                pe.wait_ge(prep.sem, prep.done(6))
                for g in range(4):
                    last = pe.matmul(wide_ps[:, g].rearrange("p s t -> p (s t)"), core.ones[:, :], wide(hit)[:, g, :],
                                     start=True, stop=True)
                last.then_inc(prep_pe.sem, 1)
                pe.wait_ge(prep.sem, prep.done(8))
                for g in range(4):
                    last = pe.matmul(wide_ps[:, g].rearrange("p s t -> p (s t)"), decay_sb[:, :], wide(plug)[:, g, :],
                                     start=True, stop=True)
                last.then_inc(prep_pe.sem, 1)
                with pe.Fori(0, B // 2) as i:
                    for j in range(2):
                        f.turn(pe, 2 * i + j, j)
                    for j in range(2):
                        b = 2 * i + j
                        f.claim_bank(pe, b, j)
                        pe.wait_ge(f.xT_ready.sem, f.xT_ready.done(b))
                        pe.wait_ge(u_ready.sem, u_ready.done(b))
                        pe.wait_ge(spread_ready.sem, spread_ready.done(b))
                        for cc in range(DC):
                            pe.matmul(f.out_ps, f.xT[:, j, cc, :], w_sb[:, cc, :], start=(cc == 0), stop=False)
                        pe.matmul(f.out_ps, spread_in[:, j, :], u[:, j, :], start=False, stop=True
                                  ).then_inc(f.out_ready.sem, 1)

            @block.vector
            def _(dve):
                def step(instruction, n):
                    instruction.then_inc(prep.sem, 1)
                    dve.wait_ge(prep.sem, prep.done(n))

                dve.wait_ge(loads.sem, weights)
                dve.wait_ge(consts.sem, consts.done(0))
                step(dve.tensor_copy(lens[:, :, :], lens_i[:, :, :]), 0)
                for b in range(B):
                    last = dve.tensor_tensor_scan(ends[:, b, :], lens[:, b, :], zeros[:, :], 0.0, ALU.add, ALU.add)
                step(last, 1)
                step(dve.tensor_scalar(hit[:, :, :], ends[:, :, :], token1[:, :], None, ALU.is_equal), 2)
                step(dve.tensor_reduce(hits[:, 0, :], hit[:, :, :], AX.X, ALU.max), 3)
                step(dve.tensor_scalar(hit[:, :, :], ends[:, :, :], token2[:, :], None, ALU.is_equal), 4)
                dve.tensor_reduce(hits[:, 1, :], hit[:, :, :], AX.X, ALU.max).then_inc(prep_hits.sem, 1)
                dve.wait_ge(prep_hits.sem, prep_hits.done(0))
                step(dve.tensor_tensor(hit_col[:, :], hits[:, 0, :], hits[:, 1, :], ALU.max), 5)
                step(dve.tensor_tensor(hit[:, :, :], hit_col[:, :].unsqueeze(2).broadcast_to([P, B, P]),
                                       upto_sb[:, :].unsqueeze(1).broadcast_to([P, B, P]), ALU.mult), 6)
                dve.wait_ge(prep_pe.sem, prep_pe.done(0))
                step(dve.tensor_scalar(plug[:, :, :].rearrange("p (g s) t -> p g s t", g=4), wide_ps[:, :, :, :],
                                       -1.0, 0.0, ALU.add, ALU.max), 7)
                step(dve.tensor_scalar(plug[:, :, :], plug[:, :, :], float(P - 1), token[:, :], ALU.min,
                                       ALU.is_equal), 8)
                step(dve.tensor_scalar(gi2[:, :], gi[:, :], over_dt, times_dt, ALU.mult, ALU.mult), 9)
                with dve.Fori(0, B // 2) as i:
                    for j in range(2):
                        b = 2 * i + j
                        dve.wait_ge(rs_ready.sem, rs_ready.done(b))
                        dve.wait_ge(f.xT_turned.sem, f.xT_turned.freed(b))
                        dve.tensor_scalar(f.h_in[:, j, :], f.x_in[:, j, :], rs[:, j, 0:1], None, ALU.mult
                                          ).then_inc(f.pre[4].sem, 1)
                        dve.wait_ge(f.out_ready.sem, f.out_ready.freed(b))
                        dve.scalar_tensor_tensor(out=u[:, j, :], in0=c_in[:, j, 0:D], scalar=rs[:, j, 1:2],
                                                 in1=gi2[:, :], op0=ALU.mult, op1=ALU.mult).then_inc(u_ready.sem, 1)
                    for j in range(2):
                        f.finish(dve, 2 * i + j, j)
                    for j in range(2):
                        f.save_normed(dve, 2 * i + j, j)
        loads.advance(16 * len(plain))
        consts.advance(1)
        prep.advance(10)
        prep_hits.advance(1)
        prep_pe.advance(2)
        prep_act.advance(1)
        for n in (squared, squared_x, ms1, ms2, rs_ready, u_ready, spread_ready):
            n.advance(B)
        for n in landed:
            n.advance(16 * B // 2)
        f.end()



def ternary_stage(core, weight, gamma, beta):
    nc, loads = core.nc, core.loads
    QB, EPS = 128.0, 1e-5
    LIMIT = float(np.float32(QB - EPS))
    ROUND = 1.5 * 2.0 ** 23
    with ExitStack() as ctx:
        sb = lambda n, s, t=F32: ctx.enter_context(nc.sbuf_tensor(core.named(n), s, t))
        gb = sb("out_scale", [P, 1])
        f = Frame(core, ctx, own_input=True, out_scale=gb[:, :])
        w, wq, g_row, b_row = sb("w", [P, DC, D]), sb("w_q", [P, DC, D]), sb("gamma", [P, D]), sb("beta", [P, D])
        w_abs, w_sum, w_tot, mean_w, inv_w = (sb("w_abs", [P, DC, D]), sb("w_sum", [P, 1]), sb("w_tot", [P, 1]),
                                              sb("mean_w", [P, 1]), sb("inv_w", [P, 1]))
        xn = sb("xn", [P, B, D])
        stats, mv, var, rstd = sb("n_stats", [P, 2, 6]), sb("n_mv", [P, 2, 2]), sb("n_var", [P, 2, 1]), sb("n_rstd", [P, 2, 1])
        n_eps, centred, scaled, mag = sb("n_eps", [P, 1]), sb("centred", [P, 2, D]), sb("scaled", [P, 2, D]), sb("mag", [P, 2, D])
        largest, of_part, of_all, inv_g, up = (sb("largest", [P, B, 1]), sb("of_part", [P, 1]), sb("of_all", [P, 1]),
                                               sb("inv_g", [P, 1]), sb("up", [P, 1]))
        xs = sb("xs", [P, 2, D])
        c = core.count
        consts, prep, prep_pool = c("constants_made"), c("prep_done"), c("prep_pool")
        n1 = (stats_done, mv_done, var_done, rstd_done, centred_done, scaled_done, xn_done, mag_done, largest_done) = (
            c("n_stats_done"), c("n_mv_done"), c("n_var_done"), c("n_rstd_done"), c("centred_done"), c("scaled_done"),
            c("xn_done"), c("mag_done"), c("largest_done"))
        xs_done = c("xs_done")
        plain = ((w[:, :, :], chunked(weight)), (g_row[:, :], row_everywhere(gamma)), (b_row[:, :], row_everywhere(beta)))
        weights = loads.base + 16 * len(plain)
        with nc.Block() as block:
            @block.sync
            def _(sp):
                for dst, src in plain:
                    sp.dma_start(dst, src).then_inc(loads.sem, 16)

            @block.gpsimd
            def _(pool):
                pool.memset(n_eps[:, :], 1e-3).then_inc(consts.sem, 1)
                pool.wait_ge(consts.sem, consts.done(0))
                with pool.Fori(0, B // 2) as i:
                    for j in range(2):
                        b = 2 * i + j
                        pool.wait_ge(mv_done.sem, mv_done.done(b))
                        pool.tensor_tensor(var[:, j, :], mv[:, j, 1:2], n_eps[:, :], ALU.add).then_inc(var_done.sem, 1)
                        pool.wait_ge(var_done.sem, var_done.done(b))
                        pool.tensor_tensor(rstd[:, j, :], var[:, j, :], core.minus_half[:, :], ALU.pow
                                           ).then_inc(rstd_done.sem, 1)
                pool.wait_ge(prep.sem, prep.done(1))
                pool.partition_all_reduce(w_tot[:, :], w_sum[:, :], P, bass.bass_isa.ReduceOp.add
                                          ).then_inc(prep_pool.sem, 1)
                pool.wait_ge(prep.sem, prep.done(2))
                pool.partition_all_reduce(of_all[:, :], of_part[:, :], P, bass.bass_isa.ReduceOp.max
                                          ).then_inc(prep_pool.sem, 1)
                with pool.Fori(0, B // 2) as i:
                    for j in range(2):
                        f.fetch(pool, 2 * i + j, j)
                    for j in range(2):
                        f.rstd_out(pool, 2 * i + j, j)

            @block.tensor
            def _(pe):
                pe.wait_ge(prep.sem, prep.done(8))
                with pe.Fori(0, B // 2) as i:
                    for j in range(2):
                        f.turn(pe, 2 * i + j, j)
                    for j in range(2):
                        b = 2 * i + j
                        f.claim_bank(pe, b, j)
                        pe.wait_ge(f.xT_ready.sem, f.xT_ready.done(b))
                        for cc in range(DC):
                            last = pe.matmul(f.out_ps, f.xT[:, j, cc, :], wq[:, cc, :], start=(cc == 0), stop=(cc == DC - 1))
                        last.then_inc(f.out_ready.sem, 1)

            @block.scalar
            def _(act):
                with act.Fori(0, B // 2) as i:
                    for j in range(2):
                        f.copy_turned(act, 2 * i + j, j)

            @block.vector
            def _(dve):
                def step(instruction, n):
                    instruction.then_inc(prep.sem, 1)
                    dve.wait_ge(prep.sem, prep.done(n))

                dve.wait_ge(loads.sem, weights)
                with dve.Fori(0, B // 2) as i:
                    for j in range(2):
                        b = 2 * i + j
                        dve.bn_stats(stats[:, j, :], core.x[:, b, :]).then_inc(stats_done.sem, 1)
                        dve.wait_ge(stats_done.sem, stats_done.done(b))
                        dve.sem_inc(f.passed.sem, 1)
                        dve.bn_aggr(mv[:, j, :], stats[:, j, :]).then_inc(mv_done.sem, 1)
                    for j in range(2):
                        b = 2 * i + j
                        dve.wait_ge(mv_done.sem, mv_done.done(b))
                        dve.wait_ge(rstd_done.sem, rstd_done.done(b))
                        dve.tensor_scalar(centred[:, j, :], core.x[:, b, :], mv[:, j, 0:1], rstd[:, j, :],
                                          ALU.subtract, ALU.mult).then_inc(centred_done.sem, 1)
                        dve.wait_ge(centred_done.sem, centred_done.done(b))
                        dve.tensor_tensor(scaled[:, j, :], centred[:, j, :], g_row[:, :], ALU.mult
                                          ).then_inc(scaled_done.sem, 1)
                        dve.wait_ge(scaled_done.sem, scaled_done.done(b))
                        dve.tensor_tensor(xn[:, b, :], scaled[:, j, :], b_row[:, :], ALU.add).then_inc(xn_done.sem, 1)
                        dve.wait_ge(xn_done.sem, xn_done.done(b))
                        dve.scalar_tensor_tensor(out=mag[:, j, :], in0=xn[:, b, :], scalar=-1.0, in1=xn[:, b, :],
                                                 op0=ALU.mult, op1=ALU.max).then_inc(mag_done.sem, 1)
                        dve.wait_ge(mag_done.sem, mag_done.done(b))
                        dve.tensor_reduce(largest[:, b, :], mag[:, j, :], AX.X, ALU.max).then_inc(largest_done.sem, 1)
                dve.wait_ge(largest_done.sem, largest_done.done(B - 1))
                step(dve.scalar_tensor_tensor(out=w_abs[:, :, :], in0=w[:, :, :], scalar=-1.0, in1=w[:, :, :],
                                              op0=ALU.mult, op1=ALU.max), 0)
                step(dve.tensor_reduce(w_sum[:, :], w_abs[:, :, :], AX.XY, ALU.add), 1)
                step(dve.tensor_reduce(of_part[:, :], largest[:, :, 0], AX.X, ALU.max), 2)
                dve.wait_ge(prep_pool.sem, prep_pool.done(1))
                step(dve.tensor_scalar(mean_w[:, :], w_tot[:, :], 1.0 / (D * D), None, ALU.mult), 3)
                step(dve.tensor_scalar(inv_w[:, :], mean_w[:, :], EPS, None, ALU.add), 4)
                step(dve.reciprocal(inv_w[:, :], inv_w[:, :]), 5)
                step(dve.tensor_scalar(wq[:, :, :], w[:, :, :], inv_w[:, :], ROUND, ALU.mult, ALU.add), 6)
                step(dve.tensor_scalar(wq[:, :, :], wq[:, :, :], -ROUND, 1.0, ALU.add, ALU.min), 7)
                step(dve.tensor_scalar(wq[:, :, :], wq[:, :, :], -1.0, None, ALU.max), 8)
                step(dve.reciprocal(inv_g[:, :], of_all[:, :]), 9)
                step(dve.tensor_scalar(up[:, :], inv_g[:, :], QB, None, ALU.mult), 10)
                step(dve.tensor_scalar(gb[:, :], of_all[:, :], mean_w[:, :], 1.0 / QB, ALU.mult, ALU.mult), 11)
                with dve.Fori(0, B // 2) as i:
                    for j in range(2):
                        b = 2 * i + j
                        dve.tensor_scalar(xs[:, j, :], xn[:, b, :], up[:, :], LIMIT, ALU.mult, ALU.min
                                          ).then_inc(xs_done.sem, 1)
                        dve.wait_ge(xs_done.sem, xs_done.done(b))
                        dve.wait_ge(f.xT_turned.sem, f.xT_turned.freed(b))
                        dve.tensor_scalar(f.h_in[:, j, :], xs[:, j, :], -LIMIT, None, ALU.max
                                          ).then_inc(f.pre[4].sem, 1)
                    for j in range(2):
                        f.finish(dve, 2 * i + j, j)
                    for j in range(2):
                        f.save_normed(dve, 2 * i + j, j)
        loads.advance(16 * len(plain))
        consts.advance(1)
        prep.advance(12)
        prep_pool.advance(2)
        for n in n1 + (xs_done,):
            n.advance(B)
        f.end()



def mamba_stage(core, w_in, conv_w, conv_b, w_x, w_dt, b_dt, a_log, d_skip, w_out):
    nc, loads = core.nc, core.loads
    INNER, N, K, R = 512, 16, 4, 16
    IC = INNER // P
    XD = R + 2 * N
    with ExitStack() as ctx:
        sb = lambda n, s, t=F32: ctx.enter_context(nc.sbuf_tensor(core.named(n), s, t))
        ps = lambda n: ctx.enter_context(nc.psum_tensor(core.named(n), [P, IC, P], F32))
        f = Frame(core, ctx, ahead=True)
        w_in_sb, w_x_sb, w_dt_sb, w_out_sb = (sb("w_in", [P, DC, 2 * INNER]), sb("w_x", [P, IC, XD]),
                                              sb("w_dt", [R, INNER]), sb("w_out", [P, IC, D]))
        taps_w, conv_b_sb, b_dt_sb, d_sb, a_sb = (sb("taps_w", [P, IC, K]), sb("conv_b", [P, IC]), sb("b_dt", [P, IC]),
                                                  sb("d_skip", [P, IC]), sb("a", [P, IC, N]))
        taps, skip = sb("taps", [P, IC, K, P]), sb("skip", [P, IC, P])
        u = sb("u", [P, 1, IC, K - 1 + P])
        uc, sz, xd = sb("uc", [P, 2, IC, P]), sb("sz", [P, 2, IC, P]), sb("xd", [XD, 2, P])
        pre, low = sb("dt_pre", [P, IC, P]), sb("dt_low", [P, IC, P])
        dt, dtu = sb("dt", [P, 2, IC, P]), sb("dtu", [P, 2, IC, P])
        bc = sb("bc", [P, 2, 2 * N, P])
        da, dbu, h, hc = sb("da", [P, 2, N, P]), sb("dbu", [P, 2, N, P]), sb("h", [P, N, P]), sb("hc", [P, 2, N, P])
        yT = sb("yT", [P, 2, IC, P])
        u_ps, z_ps, v_ps, dt_ps, y_ps = ps("u_ps"), ps("z_ps"), ps("v_ps"), ps("dt_ps"), ps("y_ps")
        bc_ps = [ps("bc_ps0"), ps("bc_ps1")]
        c = core.count
        per_b = (u_made, z_made, u_ready, conv_made, uc_ready, sz_ready, xd_made, xd_ready, dt_made, pre_ready,
                 abs_done, dexp_done, low_ready, relu_done, dt_ready, dtu_ready, yT_ready) = (
            c("u_made"), c("z_made"), c("u_ready"), c("conv_made"), c("uc_ready"), c("sz_ready"), c("xd_made"),
            c("xd_ready"), c("dt_made"), c("pre_ready"), c("abs_done"), c("dexp_done"), c("low_ready"),
            c("relu_done"), c("dt_ready"), c("dtu_ready"), c("yT_ready"))
        bc_made, bc_ready = c("bc_made"), c("bc_ready")
        da_ready, dbu_ready, scanned, hc_ready, y_summed = (c("da_ready"), c("dbu_ready"), c("scanned"),
                                                            c("hc_ready"), c("y_summed"))
        consts, prep, prep_a = c("constants_made"), c("prep_done"), c("prep_a")
        plain = ((w_in_sb[:, :, :], chunked(w_in)), (w_x_sb[:, :, :], chunked(w_x)), (w_dt_sb[:, :], w_dt[:, :]),
                 (w_out_sb[:, :, :], chunked(w_out)), (taps_w[:, :, :], conv_w[:, :, :]), (conv_b_sb[:, :], conv_b[:, :]),
                 (b_dt_sb[:, :], b_dt[:, :]), (d_sb[:, :], d_skip[:, :]), (a_sb[:, :, :], a_log[:, :, :]))
        weights = loads.base + 16 * len(plain)
        BCN = 2 * N // IC

        def every_sequence(eng, unit):
            unit(0, 0, True, 2)
            with eng.Fori(0, B // 2 - 2) as i:
                unit(2 * i + 1, 1, False, 2)
                unit(2 * i + 2, 0, False, 2)
            unit(B - 3, 1, False, 2)
            unit(B - 2, 0, False, 1)
            unit(B - 1, 1, False, 0)

        with nc.Block() as block:
            @block.sync
            def _(sp):
                for dst, src in plain:
                    sp.dma_start(dst, src).then_inc(loads.sem, 16)

            @block.gpsimd
            def _(pool):
                pool.memset(u[:, :, :, 0:K - 1], 0.0)
                pool.memset(da[:, :, :, 0:1], 0.0).then_inc(consts.sem, 1)

                def front(b, j):
                    pool.wait_ge(low_ready.sem, low_ready.done(b))
                    pool.wait_ge(scanned.sem, scanned.done(IC * (b - 2) + IC - 1))
                    pool.sem_inc(f.passed.sem, 1)
                    pool.tensor_scalar(dt[:, j], pre[:, :, :], 0.0, None, ALU.max).then_inc(relu_done.sem, 1)
                    pool.wait_ge(relu_done.sem, relu_done.done(b))
                    pool.tensor_tensor(dt[:, j], dt[:, j], low[:, :, :], ALU.add).then_inc(dt_ready.sem, 1)
                    pool.wait_ge(dt_ready.sem, dt_ready.done(b))
                    pool.wait_ge(uc_ready.sem, uc_ready.done(b))
                    pool.wait_ge(dbu_ready.sem, dbu_ready.done(IC * (b - 2) + IC - 1))
                    pool.tensor_tensor(dtu[:, j], dt[:, j], uc[:, j], ALU.mult).then_inc(dtu_ready.sem, 1)

                def unit(b, j, first, left):
                    for m in range(IC):
                        if m == 0:
                            pool.wait_ge(dtu_ready.sem, dtu_ready.done(b))
                            pool.wait_ge(bc_ready.sem, bc_ready.done(BCN * b + BCN - 1))
                        pool.wait_ge(scanned.sem, scanned.freed(IC * b + m))
                        pool.tensor_tensor(dbu[:, m % 2], dtu[:, j, m, :].unsqueeze(1).broadcast_to([P, N, P]),
                                           bc[:, j, 0:N, :], ALU.mult).then_inc(dbu_ready.sem, 1)
                        if m == 2 and not first:
                            f.rstd_out(pool, b - 1, 1 - j)
                        if m == 0 and left == 2:
                            f.fetch(pool, b + 2, j)
                    if left:
                        front(b + 1, 1 - j)
                    else:
                        f.rstd_out(pool, b, j)

                f.fetch(pool, 0, 0)
                f.fetch(pool, 1, 1)
                front(0, 0)
                every_sequence(pool, unit)

            @block.tensor
            def _(pe):
                def turn(b, j):
                    pe.wait_ge(f.x_in_ready.sem, f.x_in_ready.done(b))
                    pe.wait_ge(f.out_used.sem, f.out_used.freed(b, 3))
                    pe.wait_ge(f.xT_ready.sem, f.xT_ready.freed(b, 1))
                    for cc in range(DC):
                        last = pe.transpose(f.xT_ps[:, cc, :], f.x_in[:, j, cc * P:(cc + 1) * P], core.ident[:, :])
                    last.then_inc(f.xT_turned.sem, 1)

                def project(b, j):
                    pe.wait_ge(f.xT_ready.sem, f.xT_ready.done(b))
                    for half, (bank, used, made) in enumerate(((u_ps, u_ready, u_made), (z_ps, sz_ready, z_made))):
                        pe.wait_ge(used.sem, used.freed(b, 1))
                        for m in range(IC):
                            col = half * INNER + m * P
                            for cc in range(DC):
                                last = pe.matmul(bank[:, m, :], w_in_sb[:, cc, col:col + P], f.xT[:, j, cc, :],
                                                 start=(cc == 0), stop=(cc == DC - 1))
                        last.then_inc(made.sem, 1)

                def convolve(b, j):
                    pe.wait_ge(u_ready.sem, u_ready.done(b))
                    pe.wait_ge(xd_ready.sem, xd_ready.freed(b, 1))
                    for m in range(IC):
                        for k in range(K):
                            last = pe.matmul(v_ps[:, m, :], taps[:, m, k, :], u[:, 0, m, k:k + P],
                                             start=(k == 0), stop=(k == K - 1))
                    last.then_inc(conv_made.sem, 1)

                def project_xd(b, j):
                    pe.wait_ge(uc_ready.sem, uc_ready.done(b))
                    for m in range(IC):
                        last = pe.matmul(v_ps[0:XD, 0, :], w_x_sb[:, m, :], uc[:, j, m, :],
                                         start=(m == 0), stop=(m == IC - 1))
                    last.then_inc(xd_made.sem, 1)

                def step_sizes(b, j):
                    pe.wait_ge(xd_ready.sem, xd_ready.done(b))
                    pe.wait_ge(pre_ready.sem, pre_ready.freed(b, 1))
                    for m in range(IC):
                        last = pe.matmul(dt_ps[:, m, :], w_dt_sb[:, m * P:(m + 1) * P], xd[0:R, j, :],
                                         start=True, stop=True)
                    last.then_inc(dt_made.sem, 1)
                    for q in range(BCN):
                        pe.wait_ge(bc_ready.sem, bc_ready.freed(BCN * b + q))
                        for r in range(IC):
                            row = R + IC * q + r
                            last = pe.matmul(bc_ps[q % 2][:, r, :], core.ident[0:XD, row:row + 1].broadcast_to([XD, P]),
                                             xd[:, j, :], start=True, stop=True)
                        last.then_inc(bc_made.sem, 1)

                def sum_states(b, j, m):
                    if m == 0:
                        pe.wait_ge(yT_ready.sem, yT_ready.freed(b, 1))
                    pe.wait_ge(hc_ready.sem, hc_ready.done(IC * b + m))
                    pe.matmul(y_ps[:, m, :], skip[:, m, :], uc[:, j, m, :], start=True, stop=False)
                    for n in range(N):
                        last = pe.matmul(y_ps[:, m, :], core.ident[:, :], hc[:, m % 2, n, :], start=False,
                                         stop=(n == N - 1))
                    last.then_inc(y_summed.sem, 1)

                def out(b, j, turned):
                    pe.wait_ge(yT_ready.sem, yT_ready.done(b))
                    pe.wait_ge(f.xT_ready.sem, f.xT_ready.done(turned))
                    pe.wait_ge(f.out_used.sem, f.out_used.freed(b, 1))
                    for m in range(IC):
                        last = pe.matmul(f.out_ps, yT[:, j, m, :], w_out_sb[:, m, :], start=(m == 0), stop=(m == IC - 1))
                    last.then_inc(f.out_ready.sem, 1)

                def unit(b, j, first, left):
                    if left:
                        project(b + 1, 1 - j)
                        convolve(b + 1, 1 - j)
                    sum_states(b, j, 0)
                    if not first:
                        out(b - 1, 1 - j, b + 1 if left else b)
                    if left:
                        project_xd(b + 1, 1 - j)
                    sum_states(b, j, 1)
                    if left:
                        step_sizes(b + 1, 1 - j)
                    sum_states(b, j, 2)
                    if left == 2:
                        turn(b + 2, j)
                    sum_states(b, j, 3)
                    if not left:
                        out(b, j, b)

                pe.wait_ge(loads.sem, weights)
                pe.wait_ge(prep.sem, prep.done(1))
                turn(0, 0)
                project(0, 0)
                convolve(0, 0)
                project_xd(0, 0)
                step_sizes(0, 0)
                turn(1, 1)
                every_sequence(pe, unit)

            @block.scalar
            def _(act):
                def copy_xT(b, j):
                    act.wait_ge(f.xT_turned.sem, f.xT_turned.done(b))
                    act.wait_ge(z_made.sem, z_made.freed(b))
                    act.activation(f.xT[:, j], f.xT_ps, ACT.Copy).then_inc(f.xT_ready.sem, 1)

                def copy_u(b, j):
                    act.wait_ge(u_made.sem, u_made.done(b))
                    act.wait_ge(conv_made.sem, conv_made.freed(b, 1))
                    act.activation(u[:, 0, :, K - 1:], u_ps[:, :, :], ACT.Copy).then_inc(u_ready.sem, 1)

                def silus(b, j):
                    act.wait_ge(z_made.sem, z_made.done(b))
                    act.wait_ge(yT_ready.sem, yT_ready.freed(b))
                    act.activation(sz[:, j], z_ps[:, :, :], ACT.Silu).then_inc(sz_ready.sem, 1)
                    act.wait_ge(conv_made.sem, conv_made.done(b))
                    act.wait_ge(y_summed.sem, y_summed.done(IC * (b - 2) + IC - 1))
                    for m in range(IC):
                        last = act.activation(uc[:, j, m, :], v_ps[:, m, :], ACT.Silu, bias=conv_b_sb[:, m:m + 1])
                    last.then_inc(uc_ready.sem, 1)

                def step_sizes(b, j):
                    act.wait_ge(dt_made.sem, dt_made.done(b))
                    act.wait_ge(dt_ready.sem, dt_ready.freed(b, 1))
                    for m in range(IC):
                        last = act.activation(pre[:, m, :], dt_ps[:, m, :], ACT.Identity, bias=b_dt_sb[:, m:m + 1])
                    last.then_inc(pre_ready.sem, 1)
                    act.wait_ge(pre_ready.sem, pre_ready.done(b))
                    act.activation(low[:, :, :], pre[:, :, :], ACT.Abs).then_inc(abs_done.sem, 1)
                    act.wait_ge(abs_done.sem, abs_done.done(b))
                    act.activation(low[:, :, :], low[:, :, :], ACT.Exp, scale=-1.0).then_inc(dexp_done.sem, 1)
                    act.wait_ge(dexp_done.sem, dexp_done.done(b))
                    act.activation(low[:, :, :], low[:, :, :], ACT.Ln, bias=1.0).then_inc(low_ready.sem, 1)

                def unit(b, j, first, left):
                    if left:
                        copy_xT(b + 1, 1 - j)
                    act.wait_ge(dt_ready.sem, dt_ready.done(b))
                    for m in range(IC):
                        act.wait_ge(scanned.sem, scanned.freed(IC * b + m))
                        for n in range(N):
                            last = act.activation(da[:, m % 2, n, 1:P], dt[:, j, m, 1:P], ACT.Exp,
                                                  scale=a_sb[:, m, n:n + 1])
                        last.then_inc(da_ready.sem, 1)
                        if m < 3 and left:
                            (copy_u, silus, step_sizes)[m](b + 1, 1 - j)

                act.wait_ge(loads.sem, weights)
                act.wait_ge(consts.sem, consts.done(0))
                act.activation(a_sb[:, :, :], a_sb[:, :, :], ACT.Exp).then_inc(prep_a.sem, 1)
                act.wait_ge(prep.sem, prep.done(2))
                copy_xT(0, 0)
                copy_u(0, 0)
                silus(0, 0)
                step_sizes(0, 0)
                every_sequence(act, unit)

            @block.vector
            def _(dve):
                dve.wait_ge(loads.sem, weights)
                for m in range(IC):
                    for k in range(K):
                        last = dve.tensor_scalar(taps[:, m, k, :], core.ident[:, :], taps_w[:, m, k:k + 1], None, ALU.mult)
                last.then_inc(prep.sem, 1)
                for m in range(IC):
                    last = dve.tensor_scalar(skip[:, m, :], core.ident[:, :], d_sb[:, m:m + 1], None, ALU.mult)
                last.then_inc(prep.sem, 1)
                dve.wait_ge(prep_a.sem, prep_a.done(0))
                dve.tensor_scalar(a_sb[:, :, :], a_sb[:, :, :], -1.0, None, ALU.mult).then_inc(prep.sem, 1)

                def gate(b, j):
                    dve.wait_ge(y_summed.sem, y_summed.done(IC * b + IC - 1))
                    dve.wait_ge(sz_ready.sem, sz_ready.done(b))
                    dve.wait_ge(f.out_ready.sem, f.out_ready.freed(b))
                    dve.tensor_tensor(yT[:, j], y_ps[:, :, :], sz[:, j], ALU.mult).then_inc(yT_ready.sem, 1)

                def copy_xd(b, j):
                    dve.wait_ge(xd_made.sem, xd_made.done(b))
                    dve.wait_ge(bc_made.sem, bc_made.done(BCN * (b - 2) + BCN - 1))
                    dve.tensor_copy(xd[:, j, :], v_ps[0:XD, 0, :]).then_inc(xd_ready.sem, 1)

                def copy_bc(b, j):
                    dve.wait_ge(hc_ready.sem, hc_ready.done(IC * (b - 2) + IC - 1))
                    for q in range(BCN):
                        dve.wait_ge(bc_made.sem, bc_made.done(BCN * b + q))
                        dve.tensor_copy(bc[:, j, IC * q:IC * (q + 1), :], bc_ps[q % 2][:, :, :]
                                        ).then_inc(bc_ready.sem, 1)

                def unit(b, j, first, left):
                    flat = lambda t: t.rearrange("p n t -> p (n t)")
                    for m in range(IC):
                        g = IC * b + m
                        dve.wait_ge(da_ready.sem, da_ready.done(g))
                        dve.wait_ge(dbu_ready.sem, dbu_ready.done(g))
                        dve.wait_ge(hc_ready.sem, hc_ready.freed(g, 1))
                        dve.tensor_tensor_scan(flat(h[:, :, :]), flat(da[:, m % 2]), flat(dbu[:, m % 2]), 0.0,
                                               ALU.mult, ALU.add).then_inc(scanned.sem, 1)
                        if m == 0 and not first:
                            gate(b - 1, 1 - j)
                        dve.wait_ge(scanned.sem, scanned.done(g))
                        dve.wait_ge(y_summed.sem, y_summed.freed(g))
                        dve.tensor_tensor(hc[:, m % 2], h[:, :, :], bc[:, j, N:2 * N, :], ALU.mult
                                          ).then_inc(hc_ready.sem, 1)
                        if m == 1 and left:
                            copy_xd(b + 1, 1 - j)
                        if m == 1 and not first:
                            f.finish(dve, b - 1, 1 - j)
                        if m == 2 and left:
                            copy_bc(b + 1, 1 - j)
                        if m == 2 and not first:
                            f.save_normed(dve, b - 1, 1 - j)
                    if not left:
                        gate(b, j)
                        f.finish(dve, b, j)
                        f.save_normed(dve, b, j)

                copy_xd(0, 0)
                copy_bc(0, 0)
                every_sequence(dve, unit)
        for n in per_b:
            n.advance(B)
        for n in (bc_made, bc_ready):
            n.advance(B * BCN)
        for n in (da_ready, dbu_ready, scanned, hc_ready, y_summed):
            n.advance(B * IC)
        loads.advance(16 * len(plain))
        consts.advance(1)
        prep.advance(3)
        prep_a.advance(1)
        f.end()



COUNTS = (
    "x_in_ready", "xT_turned", "xT_ready", "xres_ready", "out_ready", "out_used", "y_stats", "y_mv", "y_var",
    "y_rstd", "x_saved", "waits_passed", "in_stats_done", "in_mv_done", "in_var_done", "in_rstd_done",
    "z_scaled_done", "y_ready", "pre_stats_done", "pre_mv_done", "pre_var_done", "pre_rstd_done", "h_ready",
    "gate_ready", "up_ready", "silu_done", "hT_ready", "spare_heads_zeroed", "bank_a_made", "bank_a_taken",
    "bank_b_made", "bank_b_taken", "result_turned", "result_copied", "scored", "biased_done", "max_done",
    "negmax_done", "exp_done", "p_turned", "weighed", "pT_even_ready", "pT_odd_ready", "inv_ready", "a_ready",
    "max_all", "null_arg", "tot_ready", "null_v_ready", "o_summed", "c_spread", "c_v_copied", "pads_zeroed",
    "constants_made", "table_made", "c_landed0", "c_landed1", "v_raw", "q_made", "k_made", "v_made", "q_maxed",
    "q_lowered", "q_exped", "q_summed", "q_inverted", "q_ready", "q_turned", "qT_ready", "k_maxed", "k_negated",
    "k_exped", "k_inverted", "k_turned", "k_ready", "v_ready", "c_made", "blocks_ready", "a_made", "aT_ready",
    "g_made", "hT_kept", "gate_scores_out", "best_found", "exped", "gate_step", "out_biased", "upped", "gate_made",
    "silued", "hid_ready", "downed", "added", "acc_begun", "expert_landed0", "expert_landed1", "norm_step",
    "prep_done", "prep_products", "prep_copied", "prep_hits", "squared_x", "squared", "ms1_done", "ms2_done",
    "rs_ready", "u_ready", "spread_ready", "prep_pool", "n_stats_done", "n_mv_done", "n_var_done", "n_rstd_done",
    "centred_done", "scaled_done", "xn_done", "mag_done", "largest_done", "xs_done", "u_made", "z_made",
    "conv_made", "uc_ready", "sz_ready", "xd_made", "xd_ready", "dt_made", "pre_ready", "abs_done", "dexp_done",
    "low_ready", "relu_done", "dt_ready", "dtu_ready", "yT_ready", "bc_made", "bc_ready", "da_ready", "dbu_ready",
    "scanned", "hc_ready", "y_summed", "prep_a",
)


def build(nc, a, out):
    with ExitStack() as ctx:
        core = Core(nc, ctx)
        for name in COUNTS:
            core.count(name)
        setup_stage(core)
        load_stage(core, a["x"])
        mamba_stage(core, a["L0_attn_W_in"], a["L0_attn_conv_w"], a["L0_attn_conv_b"], a["L0_attn_W_x"],
                    a["L0_attn_W_dt"], a["L0_attn_b_dt"], a["L0_attn_A_log"], a["L0_attn_D"], a["L0_attn_W_out"])
        depool_stage(core, a["ctx_2048"], a["mask_BxS2_if0"], a["decay"], a["upto"], a["L0_xattn_W_in"],
                     a["L0_xattn_b_in"], a["L0_xattn_g_res"], a["L0_xattn_g_init"])
        ternary_stage(core, a["L0_ffn_weight"], a["L0_ffn_ln_gamma"], a["L0_ffn_ln_beta"])
        linear_attention_stage(core, a["L1_attn_Wq"], a["L1_attn_Wk"], a["L1_attn_Wv"], a["L1_attn_Wo"],
                               a["L1_attn_bo"])
        self_attention_stage(core, a["L1_xattn_w_qkv"][:, 0:D], a["L1_xattn_w_qkv"][:, D:2 * D],
                             a["L1_xattn_w_qkv"][:, 2 * D:], a["L1_xattn_w_proj"],
                             out_bias=a["L1_xattn_b_proj"], context=a["ctx_2048"])
        with ExitStack() as moe:
            x1 = moe.enter_context(nc.sbuf_tensor(core.named("x1"), [P, B, D], F32))
            self_attention_stage(core, a["L1_ffn_wq"], a["L1_ffn_wk"], a["L1_ffn_wv"], a["L1_ffn_wo"],
                                 out_bias=a["L1_ffn_bo"], causal=True, target=x1, norm=False,
                                 pre_norm=(a["L1_ffn_ln1_scale"], a["L1_ffn_ln1_shift"]))
            hT_all = moe.enter_context(nc.sbuf_tensor(core.named("hT_all"), [P, DC, B, P], F32))
            weight_all = moe.enter_context(nc.sbuf_tensor(core.named("weight_all"), [P, 8, B, 1], F32))
            acc = moe.enter_context(nc.sbuf_tensor(core.named("acc"), [P, B, D], F32))
            gate_stage(core, hT_all, weight_all, a["L1_ffn_gate_w"], 8, 2, a["L1_ffn_ln2_scale"],
                       a["L1_ffn_ln2_shift"], x_from=x1)
            expert_stage(core, hT_all, weight_all, acc, a["L1_ffn_w2"], a["L1_ffn_w3"], w_gate=a["L1_ffn_w1"],
                         residual=x1)
            norm_stage(core, acc)
        w = a["L2_attn_W_qkv"]
        self_attention_stage(core, w[:, 0:D], w[:, D:2 * D], w[:, 2 * D:], a["L2_attn_W_out"],
                             qkv_bias=(a["L2_attn_bq"], a["L2_attn_bk"], a["L2_attn_bv"]), out_bias=a["L2_attn_b_out"],
                             alibi=True)
        wide_context_stage(core, a["ctx_2048"], a["L2_xattn_Wq"], a["L2_xattn_Wkv"], a["L2_xattn_null_kv"],
                           a["L2_xattn_Wout"], a["L2_xattn_ln_scale"], a["L2_xattn_ln_bias"])
        with ExitStack() as moe:
            hT_all = moe.enter_context(nc.sbuf_tensor(core.named("hT_all"), [P, DC, B, P], F32))
            weight_all = moe.enter_context(nc.sbuf_tensor(core.named("weight_all"), [P, 8, B, 1], F32))
            acc = moe.enter_context(nc.sbuf_tensor(core.named("acc"), [P, B, D], F32))
            gate_stage(core, hT_all, weight_all, a["L2_ffn_gate_w"], 8, 1)
            expert_stage(core, hT_all, weight_all, acc, a["L2_ffn_w1"], a["L2_ffn_w2"], b_up=a["L2_ffn_b1"],
                         b_down=a["L2_ffn_b2"])
            norm_stage(core, acc)
        self_attention_stage(core, a["L3_attn_Wq"], a["L3_attn_Wk"], a["L3_attn_Wv"], a["L3_attn_Wo"],
                             qkv_bias=(a["L3_attn_bq"], a["L3_attn_bk"], a["L3_attn_bv"]),
                             out_bias=a["L3_attn_bo"], causal=True)
        masked_context_stage(core, a["ctx_2048"], a["mask_BxS2_fk1"], a["mask_cols"], a["L3_xattn_W_src"],
                             a["L3_xattn_b_src_k"], a["L3_xattn_b_src_v"], a["L3_xattn_W_tgt"],
                             a["L3_xattn_b_tgt"], a["L3_xattn_W_out"], a["L3_xattn_b_out"])
        int_mlp_stage(core, a["L3_ffn_w_gate"], a["L3_ffn_w_up"], a["L3_ffn_w_down"])
        store_stage(core, out)


TURNED = ("L0_attn_W_in", "L0_attn_W_x", "L0_attn_W_dt", "L0_attn_W_out", "L0_xattn_W_in", "L2_ffn_gate_w", "L3_xattn_W_src", "L3_xattn_W_tgt", "L3_xattn_W_out", "L1_xattn_w_qkv", "L1_xattn_w_proj", "L2_attn_W_qkv", "L2_attn_W_out", "L3_ffn_w_gate", "L3_ffn_w_up", "L3_ffn_w_down")


COLUMNS = ("L0_attn_conv_b", "L0_attn_b_dt", "L0_attn_D", "L0_xattn_g_res", "L3_xattn_b_src_k", "L3_xattn_b_tgt", "L1_ffn_ln1_scale", "L1_ffn_ln1_shift", "L1_ffn_ln2_scale", "L1_ffn_ln2_shift")

HEADWISE = ("L3_attn_Wq", "L3_attn_Wk", "L3_attn_Wv")


def columns(v, rows):
    return v.reshape(-1, rows).T


def by_row(v):
    return v.reshape(4, 4, -1).transpose(0, 2, 1).reshape(-1, 4)


def laid_out(inputs):
    a = {name: np.asarray(v) for name, v in inputs.items()}
    for name in TURNED:
        a[name] = a[name].T
    for name in HEADWISE:
        a[name] = a[name].transpose(1, 0, 2).reshape(D, -1)
    qkv = a.pop("L2_attn_b_qkv")
    a["L2_attn_bq"], a["L2_attn_bk"], a["L2_attn_bv"] = by_row(qkv[:D]), by_row(qkv[D:2 * D]), qkv[2 * D:]
    a["L3_attn_bq"], a["L3_attn_bk"] = by_row(a["L3_attn_bq"]), by_row(a["L3_attn_bk"])
    a["L3_attn_bv"] = a["L3_attn_bv"].reshape(-1)
    a["mask_cols"] = a["mask_BxS2_fk1"].T
    src = a.pop("L3_xattn_b_src")
    a["L3_xattn_b_src_k"], a["L3_xattn_b_src_v"] = src[:D], src[D:]
    a["L2_ffn_b2"] = a["L2_ffn_b2"][:, None, :]
    b1 = a["L2_ffn_b1"]
    a["L2_ffn_b1"] = b1.reshape(b1.shape[0], -1, P).transpose(0, 2, 1)
    a["decay"] = depool_constants()[0]
    a["upto"] = np.triu(np.ones((P, P), np.float32))
    for name in ("L0_attn_conv_w", "L0_attn_A_log"):
        a[name] = a[name].reshape(-1, P, a[name].shape[1]).transpose(1, 0, 2)
    for name in COLUMNS:
        a[name] = columns(a[name], P)
    return {name: np.ascontiguousarray(v) for name, v in a.items()}


def kernel(**inputs):
    import concourse.bacc as bacc
    from concourse.bass_utils import run_bass_kernel_spmd

    nc = bacc.Bacc("TRN2", target_bir_lowering=False, num_devices=1)
    arrays, args = {}, {}
    for name, value in laid_out(inputs).items():
        arrays[f"in_{name}"] = value
        args[name] = nc.dram_tensor(f"in_{name}", value.shape, mybir.dt.from_np(value.dtype),
                                    kind="ExternalInput").ap()
    out = nc.dram_tensor("out", (B, P, D), F32, kind="ExternalOutput").ap()
    build(nc, args, out)
    return run_bass_kernel_spmd(nc, [arrays], core_ids=[0]).results[0]["out"]
```
